# Optimizing a Trainium2 kernel written in Bass

```python
import numpy as np
import jax
import jax.numpy as jnp

def _softmax(x, axis=-1):
    return jax.nn.softmax(x, axis=axis)

def _gelu(x):
    return jax.nn.gelu(x, approximate=True)

def _silu(x):
    return jax.nn.silu(x)

def _sigmoid(x):
    return jax.nn.sigmoid(x)

def _layernorm(x, axis=-1, eps=1e-05):
    m = jnp.mean(x, axis=axis, keepdims=True)
    v = jnp.var(x, axis=axis, keepdims=True)
    return (x - m) / jnp.sqrt(v + eps)

def _scatter_add(tgt, idx, src, axis=0):
    return tgt.at[idx].add(src)

def _segment_sum(src, seg, n):
    return jax.ops.segment_sum(src, seg, n)
kernel_name = 'mk_gnn_ffn_d1_gnn_r32_45f451'

def setup_inputs(seed: int=0):
    np.random.seed(seed)
    _w = jnp.asarray

    def _rec_inputs():
        import jax
        import jax.numpy as jnp
        _gk = jax.random.key(seed)
        x = -0.0002117 + 1 * jax.random.normal(jax.random.fold_in(_gk, 1), (3125, 256), jnp.float32)
        src = jax.random.randint(jax.random.fold_in(_gk, 2), (50000,), 0, 3125, jnp.int32)
        dst = jax.random.randint(jax.random.fold_in(_gk, 3), (50000,), 0, 3125, jnp.int32)
        _o = jnp.argsort(dst, stable=True)
        src = src[_o]
        dst = dst[_o]
        edge_weight = jax.random.uniform(jax.random.fold_in(_gk, 12), (50000,), jnp.float32, 0.0, 1)
        return (x, src, dst, edge_weight)
    x, src, dst, edge_weight = _rec_inputs()

    def _L0_gnn_setup():
        import jax, jax.numpy as jnp
        import numpy as np
        N_NODES = 3125
        N_EDGES = 100000
        DIM_IN = 256
        DIM_OUT = 256
        key = jax.random.key(seed)
        ks = jax.random.split(key, 8)
        feat_in = jax.random.normal(ks[0], (N_NODES, DIM_IN), dtype=jnp.float32)
        edge_row = jax.random.randint(ks[1], (N_EDGES,), 0, N_NODES, dtype=jnp.int32)
        edge_col = jax.random.randint(ks[2], (N_EDGES,), 0, N_NODES, dtype=jnp.int32)
        edge_val = jax.random.uniform(ks[3], (N_EDGES,), dtype=jnp.float32)
        s1 = 1.0 / np.sqrt(DIM_IN)
        s2 = 1.0 / np.sqrt(DIM_OUT)
        W1 = jax.random.normal(ks[4], (DIM_IN, DIM_OUT), dtype=jnp.float32) * s1
        b1 = jnp.zeros((DIM_OUT,), dtype=jnp.float32)
        W2 = jax.random.normal(ks[5], (DIM_OUT, DIM_OUT), dtype=jnp.float32) * s2
        b2 = jnp.zeros((DIM_OUT,), dtype=jnp.float32)
        eps = jnp.zeros((1,), dtype=jnp.float32)
        offset = jnp.zeros((DIM_OUT,), dtype=jnp.float32)
        scale = jnp.ones((DIM_OUT,), dtype=jnp.float32)
        return {'feat_in': feat_in, 'edge_row': edge_row, 'edge_col': edge_col, 'edge_val': edge_val, 'W1': W1, 'b1': b1, 'W2': W2, 'b2': b2, 'eps': eps, 'offset': offset, 'scale': scale}
    _L0_gnn_all = _L0_gnn_setup()
    _L0_gnn_in = {k: v for k, v in _L0_gnn_all.items() if k in ('W1', 'b1', 'W2', 'b2', 'eps', 'offset', 'scale')}
    del _L0_gnn_all

    def _L0_ffn_setup():
        import jax, jax.numpy as jnp
        import numpy as np
        TOP_K = 2
        LN_EPS = 1e-05
        key = jax.random.key(seed)
        ks = jax.random.split(key, 8)
        B, S, D, E, H = (16, 1024, 256, 8, 1024)
        x = jax.random.normal(ks[0], (B, S, D), dtype=jnp.float32)
        Wr = jax.random.normal(ks[1], (D, E), dtype=jnp.float32) * 0.1
        br = jnp.zeros((E,), dtype=jnp.float32)
        ln_g = jnp.ones((E, D), dtype=jnp.float32)
        ln_b = jnp.zeros((E, D), dtype=jnp.float32)
        W1 = jax.random.normal(ks[2], (E, D, H), dtype=jnp.float32) * (1.0 / np.sqrt(D))
        b1 = jnp.zeros((E, H), dtype=jnp.float32)
        W2 = jax.random.normal(ks[3], (E, H, D), dtype=jnp.float32) * (1.0 / np.sqrt(H))
        b2 = jnp.zeros((E, D), dtype=jnp.float32)
        return {'x': x, 'Wr': Wr, 'br': br, 'ln_g': ln_g, 'ln_b': ln_b, 'W1': W1, 'b1': b1, 'W2': W2, 'b2': b2}
    _L0_ffn_all = _L0_ffn_setup()
    _L0_ffn_in = {k: v for k, v in _L0_ffn_all.items() if k in ('Wr', 'br', 'ln_g', 'ln_b', 'W1', 'b1', 'W2', 'b2')}
    del _L0_ffn_all
    return {'x': x, 'src': src, 'dst': dst, 'edge_weight': edge_weight, 'L0_gnn_W1': _L0_gnn_in['W1'], 'L0_gnn_b1': _L0_gnn_in['b1'], 'L0_gnn_W2': _L0_gnn_in['W2'], 'L0_gnn_b2': _L0_gnn_in['b2'], 'L0_gnn_eps': _L0_gnn_in['eps'], 'L0_gnn_offset': _L0_gnn_in['offset'], 'L0_gnn_scale': _L0_gnn_in['scale'], 'L0_ffn_Wr': _L0_ffn_in['Wr'], 'L0_ffn_br': _L0_ffn_in['br'], 'L0_ffn_ln_g': _L0_ffn_in['ln_g'], 'L0_ffn_ln_b': _L0_ffn_in['ln_b'], 'L0_ffn_W1': _L0_ffn_in['W1'], 'L0_ffn_b1': _L0_ffn_in['b1'], 'L0_ffn_W2': _L0_ffn_in['W2'], 'L0_ffn_b2': _L0_ffn_in['b2']}

def reference(x, src, dst, edge_weight, L0_gnn_W1, L0_gnn_b1, L0_gnn_W2, L0_gnn_b2, L0_gnn_eps, L0_gnn_offset, L0_gnn_scale, L0_ffn_Wr, L0_ffn_br, L0_ffn_ln_g, L0_ffn_ln_b, L0_ffn_W1, L0_ffn_b1, L0_ffn_W2, L0_ffn_b2):
    import jax
    import jax.numpy as jnp

    def _L0_gnn_ref(feat_in, edge_row, edge_col, edge_val, W1, b1, W2, b2, eps, offset, scale):
        import jax, jax.numpy as jnp
        import numpy as np
        N_NODES = 3125
        N_EDGES = 100000
        DIM_IN = 256
        DIM_OUT = 256
        msg = edge_val[:, None] * feat_in[edge_col]
        aggr = jax.ops.segment_sum(msg, edge_row, num_segments=feat_in.shape[0])
        aggr = aggr + (1.0 + eps) * feat_in
        h = jnp.maximum(aggr @ W1 + b1, 0.0) @ W2 + b2
        h = jnp.maximum(h, 0.0)
        mean = jnp.mean(h, axis=1, keepdims=True)
        var = jnp.var(h, axis=1, keepdims=True) + 1e-10
        return (h - mean) * scale * jax.lax.rsqrt(var) + offset

    def _L0_ffn_ref(x, Wr, br, ln_g, ln_b, W1, b1, W2, b2):
        import jax, jax.numpy as jnp
        import numpy as np
        TOP_K = 2
        LN_EPS = 1e-05
        B, S, D = x.shape
        N = B * S
        xt = x.reshape(N, D)
        logits = xt @ Wr + br
        probs = jax.nn.softmax(logits, axis=-1)
        top_p, top_idx = jax.lax.top_k(probs, TOP_K)
        weights = top_p / top_p.sum(axis=-1, keepdims=True)
        mu = xt.mean(axis=-1, keepdims=True)
        var = ((xt - mu) ** 2).mean(axis=-1, keepdims=True)
        xn = (xt - mu) * jax.lax.rsqrt(var + LN_EPS)
        xe = xn[None, :, :] * ln_g[:, None, :] + ln_b[:, None, :]
        h = jax.nn.gelu(jnp.einsum('end,edh->enh', xe, W1) + b1[:, None, :], approximate=False)
        y = jnp.einsum('enh,ehd->end', h, W2) + b2[:, None, :]
        y_tok = jnp.transpose(y, (1, 0, 2))
        sel = jnp.take_along_axis(y_tok, top_idx[:, :, None], axis=1)
        out = (weights[:, :, None] * sel).sum(axis=1)
        return out.reshape(B, S, D)
    x = x + _L0_gnn_ref(_layernorm(x, axis=-1), src, dst, edge_weight, L0_gnn_W1, L0_gnn_b1, L0_gnn_W2, L0_gnn_b2, L0_gnn_eps, L0_gnn_offset, L0_gnn_scale)
    x = x + _L0_ffn_ref(_layernorm(x, axis=-1)[None], L0_ffn_Wr, L0_ffn_br, L0_ffn_ln_g, L0_ffn_ln_b, L0_ffn_W1, L0_ffn_b1, L0_ffn_W2, L0_ffn_b2)[0]
    return x

_drawn_inputs = setup_inputs


def setup_inputs(seed=0):
    import zlib

    import numpy as np

    out = dict(_drawn_inputs(seed))
    spreads = {'L0_gnn_b1': (0.0, 0.1),
     'L0_gnn_b2': (0.0, 0.1),
     'L0_gnn_offset': (0.0, 0.1),
     'L0_gnn_scale': (1.0, 0.2),
     'L0_ffn_br': (0.0, 0.1),
     'L0_ffn_ln_g': (1.0, 0.2),
     'L0_ffn_ln_b': (0.0, 0.1),
     'L0_ffn_b1': (0.0, 0.1),
     'L0_ffn_b2': (0.0, 0.1)}
    factors = {}
    for name, (base, spread) in spreads.items():
        noise = np.random.default_rng([zlib.crc32(name.encode()), seed]).standard_normal(out[name].shape)
        drawn = base * np.exp(spread * noise) if base else spread * noise
        out[name] = jnp.asarray(drawn.astype(out[name].dtype))
    for name, factor in factors.items():
        out[name] = (out[name] * factor).astype(out[name].dtype)
    return out
```

```python
from contextlib import ExitStack

import numpy as np

import concourse.bass as bass
from concourse import mybir

ALU = mybir.AluOpType
ACT = mybir.ActivationFunctionType
AX_X = mybir.AxisListType.X
F32 = mybir.dt.float32
F16 = mybir.dt.float16
BF16 = mybir.dt.bfloat16
I32 = mybir.dt.int32
U32 = mybir.dt.uint32

P = 128


def moe_gnn_program(nc, x, src, dst, edge_weight, gW1, gb1, gW2, gb2, geps, goffset, gscale,
                    Wr, br, ln_g, ln_b, W1, b1, W2, b2, out):
    N, D = x.shape
    E = src.shape[0]
    NE, _, H = W1.shape
    KC, HC = D // P, H // P
    NT = (N + P - 1) // P
    LAST = N - (NT - 1) * P
    NB = NT
    U = 8
    HALF = U // 2

    EC_FULL = (E + P - 1) // P
    EC = (EC_FULL + U - 1) // U * U
    extra = NB - 1
    C0 = (EC - extra) // 2 // U * U
    S0 = (C0 + extra + U - 1) // U * U
    C1 = EC - C0
    S1 = (C1 + extra + U - 1) // U * U
    assert C1 == S0 and S1 <= 256
    COLS, SLOTS, CSTART = (C0, C1), (S0, S1), (0, C0)
    CMAX, SMAX = max(COLS), max(SLOTS)

    KTOP = 2
    RC = KTOP * NT
    FT = (N * KTOP + NE * (P - 1)) // P
    FT += FT % 2
    WSCALE = 32.0
    WE = 2 * KC * H
    assert WE == 2 * HC * D
    PREP2 = NE // 2

    xl_d = nc.dram_tensor("xl_d", (N, D), F32, kind="Internal").ap()
    xs_d = nc.dram_tensor("xs_d", (FT * P, D), F32, kind="Internal").ap()
    ys_d = nc.dram_tensor("ys_d", (FT * P, D), F32, kind="Internal").ap()

    with ExitStack() as ctx:
        def sb(name, shape, dt):
            return ctx.enter_context(nc.sbuf_tensor(name, shape, dt))

        def sem(name):
            return ctx.enter_context(nc.semaphore(name))

        bank = [ctx.enter_context(nc.psum_tensor(f"bank{i}", [P, 512], F32)) for i in range(8)]

        Wall = sb("Wall", [P, 2 * NE * WE], F16)
        RA = sb("RA", [P, NT * D], F32)
        RB = sb("RB", [P, NT * D], F32)
        gbuf = sb("gbuf", [P, U, D], F32)
        stage = sb("stage", [P, KC * H], F32)
        W2BASE = NE * WE

        def f32view(t, at, n):
            return t[:, 2 * at:2 * (at + n)].bitcast(F32)

        w2f = W2BASE // 2
        x_in = f32view(Wall, w2f, NT * D).rearrange("p (t d) -> p t d", d=D)
        xl = f32view(Wall, w2f + NT * D, NT * D).rearrange("p (t d) -> p t d", d=D)
        late = w2f + PREP2 * WE // 2
        h1T = f32view(Wall, late, NT * D).rearrange("p (c n) -> p c n", c=KC)
        xl2 = f32view(Wall, late, NT * D).rearrange("p (t d) -> p t d", d=D)
        acc = RA[:, :].rearrange("p (t d) -> p t d", d=D)
        h2, xn = acc, acc
        aggT = RB[:, :].rearrange("p (c n) -> p c n", c=KC)
        x1 = RB[:, :].rearrange("p (t d) -> p t d", d=D)
        NBC = NB * CMAX
        e_oh = Wall[:, 0:NBC]
        e_cum = Wall[:, NBC:2 * NBC]
        e_pos = Wall[:, 2 * NBC:4 * NBC].bitcast(F32)
        PAY = 7
        epay = RB[:, 0:EC * PAY].rearrange("p (c k) -> p c k", k=PAY)
        at = EC * PAY
        SR = 4
        lo16 = RB[:, at:at + SR * P].bitcast(F16).rearrange("p (s k n) -> p s k n", s=SR, k=2)
        at += SR * P
        lobf = RB[:, at:at + SR * P * 3 // 2].bitcast(BF16).rearrange("p (s k n) -> p s k n", s=SR, k=3)
        at += SR * P * 3 // 2
        hi16 = RB[:, at:at + SR * SMAX // 2].bitcast(F16).rearrange("p (s n) -> p s n", s=SR)
        at += SR * SMAX // 2
        rec_i, rec_f = [], []
        for c in range(2):
            rec_i.append(RB[:, at:at + SLOTS[c]].bitcast(I32))
            at += SLOTS[c]
            rec_f.append(RB[:, at:at + 2 * SLOTS[c]].rearrange("p (c k) -> p c k", k=2))
            at += 2 * SLOTS[c]
        assert at <= NT * D
        xs = [RA[:, q * D:(q + 1) * D] for q in range(2)]
        at = 2 * D
        xhi, xlo, hhi, hlo, h32, ysb = [], [], [], [], [], []
        for q in range(2):
            for lst, n in ((xhi, D // 2), (xlo, D // 2), (hhi, H // 2), (hlo, H // 2)):
                lst.append(RA[:, at:at + n].bitcast(F16))
                at += n
            h32.append(RA[:, at:at + H])
            at += H
            ysb.append(RA[:, at:at + D])
            at += D
        assert at <= NT * D
        gw1 = gbuf[:, 0:2, :]
        gw2 = gbuf[:, 2:4, :]
        gb2_bc, gsc_bc, gof_bc = gbuf[:, 4, :], gbuf[:, 5, :], gbuf[:, 6, :]
        xT = [stage[:, q * D:(q + 1) * D] for q in range(2)]

        ident = sb("ident", [P, P], F32)
        ones = sb("ones", [P, P], F32)
        above = sb("above", [P, P], F32)
        upto = sb("upto", [P, P], F32)
        iota_i = RA[:, 0:256].bitcast(I32)
        iota_f = sb("iota_f", [P, 256], F32)
        iota_h = sb("iota_h", [P, 256], F16)
        tile_at = sb("tile_at", [P, 256], F32)
        part_i = sb("part_i", [P, 1], F32)
        zero_h = sb("zero_h", [P, 256], F16)
        one_h = sb("one_h", [P, 1], F16)
        one_b = sb("one_b", [3, P], BF16)
        Sw = sb("Sw", [P, 4, P], F32)
        pay_slot = sb("pay_slot", [P, 2, HALF, PAY], F32)
        idx_slot = sb("idx_slot", [P, 2, HALF], I32)
        rec_slot = sb("rec_slot", [P, 2, HALF, 2], F32)
        blk_tab = [sb(f"blk_tab{c}", [1, SLOTS[c]], I32) for c in range(2)]
        exp_tab = sb("exp_tab", [1, FT], I32)
        biasT = sb("biasT", [P, P], F32)
        b1T = sb("b1T", [P, NE * HC], F32)
        b2raw = gbuf[0:3, :, :].rearrange("p a d -> p (a d)")
        b2rows = stage[0:3, 0:NE * D // 2].bitcast(BF16)
        eps1 = sb("eps1", [P, 1], F32)
        Wr_sb = sb("Wr_sb", [P, KC, NE], F32)
        br_bc = sb("br_bc", [P, NE], F32)
        stats = sb("stats", [P, NT, 6], F32)
        lnt = sb("lnt", [P, 4, NT], F32)
        rstd = sb("rstd", [P, NT], F32)
        nmr = sb("nmr", [P, NT], F32)
        cnt = sb("cnt", [P, 32], F32)
        cprev = sb("cprev", [P, 32], F32)
        room_i = sb("room_i", [P, 64], I32)
        room_f = sb("room_f", [P, 64], F32)
        first = sb("first", [P, 32], F32)
        ends = sb("ends", [P, 1], F32)
        past = sb("past", [32, 256], F16)
        pos_u = sb("pos_u", [P, RC], I32)
        gate = sb("gate", [P, 2, NT], F32)
        rows_in = stage[:, 0:P]

        ei = [stage[:, (k + 1) * 400:(k + 1) * 400 + EC].bitcast(I32) for k in range(3)]
        e_src, e_dst, e_tmp = ei
        ew = gbuf[:, 0:2, :].rearrange("p a d -> p (a d)")[:, 0:EC]
        blk_h = gbuf[:, 2:4, :].rearrange("p a d -> p (a d)")[:, 0:EC // 2].bitcast(F16)
        wpart = gbuf[:, 4:6, :].rearrange("p a d -> p (a d)")[:, 0:EC // 2].bitcast(BF16)
        pos_i = gbuf[:, 6:8, :].rearrange("p a d -> p (a d)")[:, 0:CMAX].bitcast(I32)
        pos_j = gbuf[:, 6:8, :].rearrange("p a d -> p (a d)")[:, CMAX:2 * CMAX].bitcast(I32)
        rt = gbuf[:, :, :].rearrange("p a d -> p (a d)")
        def rslice(k, n):
            return rt[:, 200 * k:200 * k + n]
        lg = rslice(0, NT * NE).rearrange("p (t e) -> p t e", e=NE)
        eq = rslice(1, NT * NE).rearrange("p (t e) -> p t e", e=NE)
        cand = rslice(2, NT * NE).rearrange("p (t e) -> p t e", e=NE)
        topv = rslice(3, 2 * NT).rearrange("p (k t) -> p k t", k=2)
        topi = rslice(4, 2 * NT).rearrange("p (k t) -> p k t", k=2)
        r_ok = rslice(5, NT)
        r_e = rslice(6, NT)
        r_oh = rt[:, 1400:1400 + NE * RC // 2].bitcast(F16)
        r_cum = rt[:, 1600:1600 + NE * RC // 2].bitcast(F16)
        r_tmp = rt[:, 800 + 50:800 + 50 + NT]
        r_pos = stage[:, 512:512 + NE * RC]
        pos_f = stage[:, 1024:1024 + RC]
        bwork = stage[0:3, NE * D // 2:NE * D]

        edges_in = sem("edges_in")
        x_loaded = sem("x_loaded")
        stats_done = sem("stats_done")
        var_ready = sem("var_ready")
        root_done = sem("root_done")
        scaled = sem("scaled")
        x1_done = sem("x1_done")
        hhi_done = sem("hhi_done")
        g_scaled = sem("g_scaled")
        small_in = sem("small_in")
        const_done = sem("const_done")
        dve_step = sem("dve_step")
        act_step = sem("act_step")
        pool_step = sem("pool_step")
        xl_scaled = sem("xl_scaled")
        xl_done = sem("xl_done")
        acc_set = sem("acc_set")
        xl_stored = sem("xl_stored")
        xs_zeroed = sem("xs_zeroed")
        counts_ready = sem("counts_ready")
        counts_mm = sem("counts_mm")
        ends_mm = sem("ends_mm")
        room_ready = sem("room_ready")
        past_ready = sem("past_ready")
        table_mm = sem("table_mm")
        bias_mm = sem("bias_mm")
        payload_set = sem("payload_set")
        acc_cleared = sem("acc_cleared")
        pay_ready = sem("pay_ready")
        sort_built = sem("sort_built")
        sort_mm = sem("sort_mm")
        recs_taken = sem("recs_taken")
        rec_ready = sem("rec_ready")
        gathered = [sem(f"gathered{j}") for j in range(U)]
        slot_claimed = sem("slot_claimed")
        sw_built = sem("sw_built")
        agg_mm = sem("agg_mm")
        agg_added = sem("agg_added")
        staged = sem("staged")
        w_hi = sem("w_hi")
        w_done = sem("w_done")
        b1_mm = sem("b1_mm")
        b1_free = sem("b1_free")
        mlp_in = sem("mlp_in")
        t_mm = sem("t_mm")
        t_out = sem("t_out")
        h1_mm = sem("h1_mm")
        h1_out = sem("h1_out")
        h2_mm = sem("h2_mm")
        h2_out = sem("h2_out")
        h2_relu = sem("h2_relu")
        x_again = sem("x_again")
        x_shift = sem("x_shift")
        ln_coef = sem("ln_coef")
        norm_out = sem("norm_out")
        r_mm = sem("r_mm")
        r_out = sem("r_out")
        lg_mm = sem("lg_mm")
        top_ready = sem("top_ready")
        exp_done = sem("exp_done")
        pos_ready = sem("pos_ready")
        router_done = sem("router_done")
        b2_in = sem("b2_in")
        b2_ready = sem("b2_ready")
        scattered = sem("scattered")
        xs_in = [sem(f"xs_in{q}") for q in range(2)]
        ft_mm = sem("ft_mm")
        fx_hi = sem("fx_hi")
        fx_split = sem("fx_split")
        up_mm = sem("up_mm")
        gelu_done = sem("gelu_done")
        h_split = sem("h_split")
        down_mm = sem("down_mm")
        y_out = sem("y_out")
        y_stored = [sem(f"y_stored{q}") for q in range(2)]
        combined_in = [sem(f"combined_in{j}") for j in range(U)]
        combined = sem("combined")
        out_done = sem("out_done")

        block = ctx.enter_context(nc.Block())
        FULL = (NT - 1) * P

        @block.sync
        def _(sp):
            pcols = EC_FULL
            rows = E // pcols
            rest = E - rows * pcols
            sp.wait_ge(const_done, 1)
            for a, t in ((src, e_src), (dst, e_dst), (edge_weight, ew)):
                sp.dma_start(t[0:rows, 0:pcols], a[0:rows * pcols].rearrange("(p c) -> p c", c=pcols)
                             ).then_inc(edges_in, 16)
                sp.dma_start(t[rows:rows + 1, 0:rest], a[rows * pcols:E].rearrange("(p c) -> p c", p=1)
                             ).then_inc(edges_in, 16)
            sp.wait_ge(const_done, 2)
            sp.dma_start(x_in[:, 0:NT - 1, :], x[0:FULL, :].rearrange("(t p) d -> p t d", p=P)).then_inc(x_loaded, 16)
            sp.dma_start(x_in[0:LAST, NT - 1, :], x[FULL:N, :]).then_inc(x_loaded, 16)
            sp.wait_ge(const_done, 3)
            sp.dma_start(rows_in[0:64, :], b1.rearrange("e (c p) -> (e c) p", p=P)).then_inc(small_in, 16)
            sp.dma_start(rows_in[64:80, :], ln_g.rearrange("e (c p) -> (e c) p", p=P)).then_inc(small_in, 16)
            sp.dma_start(rows_in[80:96, :], ln_b.rearrange("e (c p) -> (e c) p", p=P)).then_inc(small_in, 16)
            sp.dma_start(rows_in[96:98, :], gb1.rearrange("(c p) -> c p", p=P)).then_inc(small_in, 16)
            sp.dma_start(eps1[:, :], geps.partition_broadcast(P)).then_inc(small_in, 16)
            sp.dma_start(Wr_sb[:, :, :], Wr.rearrange("(c p) e -> p c e", p=P)).then_inc(small_in, 16)
            sp.dma_start(br_bc[:, :], br.partition_broadcast(P)).then_inc(small_in, 16)
            sp.wait_ge(xl_done, NT)
            sp.dma_start(xl_d[0:FULL, :].rearrange("(t p) d -> p t d", p=P), xl[:, 0:NT - 1, :]).then_inc(xl_stored, 16)
            sp.dma_start(xl_d[FULL:N, :], xl[0:LAST, NT - 1, :]).then_inc(xl_stored, 16)
            zrow = zero_h[:, :].bitcast(F32)
            for h in range(2):
                sp.dma_start(xs_d[:, h * P:(h + 1) * P].rearrange("(t p) d -> p t d", p=P),
                             zrow.rearrange("p (a d) -> p a d", a=1).to_broadcast([P, FT, P])).then_inc(xs_zeroed, 16)
            sp.wait_ge(recs_taken, 1)
            sp.wait_ge(bias_mm, 2)
            w1_v = W1.rearrange("e (c p) h -> p e c h", p=P)
            w2_v = W2.rearrange("e (c p) d -> p e c d", p=P)
            with sp.Fori(0, NE) as e:
                sp.wait_ge(w_done, 2 * e)
                sp.wait_ge(b1_mm, e)
                sp.dma_start(stage[:, :].rearrange("p (a c h) -> p a c h", a=1, c=KC),
                             w1_v[:, bass.ds(e, 1), :, :]).then_inc(staged, 16)
            sp.wait_ge(b1_mm, NE)
            with sp.Fori(0, PREP2) as e:
                sp.wait_ge(w_done, 2 * NE + 2 * e)
                sp.dma_start(stage[:, :].rearrange("p (a c d) -> p a c d", a=1, c=HC),
                             w2_v[:, bass.ds(e, 1), :, :]).then_inc(staged, 16)
            sp.wait_ge(agg_mm, U + S0 + S1)
            sp.dma_start(gw1, gW1.rearrange("(c p) n -> p c n", p=P)).then_inc(mlp_in, 16)
            sp.dma_start(gw2, gW2.rearrange("(c p) n -> p c n", p=P)).then_inc(mlp_in, 16)
            sp.dma_start(gb2_bc, gb2.partition_broadcast(P)).then_inc(mlp_in, 16)
            sp.dma_start(gsc_bc, gscale.partition_broadcast(P)).then_inc(mlp_in, 16)
            sp.dma_start(gof_bc, goffset.partition_broadcast(P)).then_inc(mlp_in, 16)
            sp.wait_ge(h1_out, 8 * KC)
            sp.dma_start(x1[:, 0:NT - 1, :], x[0:FULL, :].rearrange("(t p) d -> p t d", p=P)).then_inc(x_again, 16)
            sp.dma_start(x1[0:LAST, NT - 1, :], x[FULL:N, :]).then_inc(x_again, 16)
            sp.wait_ge(router_done, 1)
            sp.dma_start(b2raw, b2.rearrange("e d -> (e d)").partition_broadcast(3)).then_inc(b2_in, 16)
            with sp.Fori(0, NE - PREP2) as e:
                sp.wait_ge(w_done, 2 * NE + 2 * PREP2 + 2 * e)
                sp.dma_start(stage[:, :].rearrange("p (a c d) -> p a c d", a=1, c=HC),
                             w2_v[:, bass.ds(e + PREP2, 1), :, :]).then_inc(staged, 16)
            xs_v = xs_d.rearrange("(t p) d -> t p d", p=P)
            ys_v = ys_d.rearrange("(t p) d -> t p d", p=P)
            sp.wait_ge(scattered, 16 * RC)
            for q in range(2):
                sp.dma_start(xs[q], xs_v[q]).then_inc(xs_in[q], 16)

            def store(t, q):
                sp.wait_ge(y_out, 2 + t + 1)
                sp.dma_start(ys_v[bass.ds(t, 1), :, :].rearrange("a p d -> p (a d)"), ysb[q]).then_inc(y_stored[q], 16)

            with sp.Fori(0, FT // 2 - 1) as i:
                for q in range(2):
                    sp.wait_ge(ft_mm, 2 + 2 * i + q + 1)
                    sp.dma_start(xs[q], xs_v[bass.ds(2 * i + q + 2, 1), :, :].rearrange("a p d -> p (a d)")
                                 ).then_inc(xs_in[q], 16)
                    store(2 * i + q, q)
            for q in range(2):
                sp.wait_ge(y_out, 2 + FT - 2 + q + 1)
                sp.dma_start(ys_v[FT - 2 + q], ysb[q]).then_inc(y_stored[q], 16)
            for t in range(NT):
                n = P if t < NT - 1 else LAST
                sp.wait_ge(combined, 2 * (t + 1))
                sp.dma_start(out[t * P:t * P + n, :], x1[0:n, t, :]).then_inc(out_done, 16)
            sp.wait_ge(out_done, 16 * NT)

        @block.gpsimd
        def _(pool):
            steps = [0]

            def link(ins):
                steps[0] += 1
                ins.then_inc(pool_step, 1)
                pool.wait_ge(pool_step, steps[0])

            pool.memset(e_src, NB * P)
            pool.memset(e_dst, 0)
            link(pool.memset(ew, 0.0))
            pool.nop().then_inc(const_done, 1)
            link(pool.memset(x_in[:, NT - 1, :], 0.0))
            pool.nop().then_inc(const_done, 1)
            link(pool.iota(iota_i[:, 0:1], [[1, 1]], base=0, channel_multiplier=1))
            link(pool.tensor_copy(part_i[:, :], iota_i[:, 0:1]))
            link(pool.iota(iota_i[:, :], [[1, 256]], base=0, channel_multiplier=0))
            link(pool.tensor_copy(iota_f[:, :], iota_i[:, :]))
            pool.tensor_copy(iota_h[:, :], iota_f[:, :])
            pool.tensor_scalar(tile_at[:, :], iota_f[:, :], float(P), None, ALU.mult)
            pool.memset(zero_h[:, :], 0.0)
            pool.memset(one_h[:, :], 1.0)
            pool.memset(one_b[:, :], 1.0)
            pool.memset(ones[:, :], 1.0)
            pool.memset(above[:, :], 1.0)
            pool.memset(upto[:, :], 1.0)
            pool.memset(rows_in, 0.0)
            link(pool.memset(ident[:, :], 0.0))
            pool.affine_select(out=ident[:, :], in_=ident[:, :], compare_op=ALU.not_equal, fill=1.0, base=0,
                               pattern=[[-1, P]], channel_multiplier=1)
            pool.affine_select(out=above[:, :], in_=above[:, :], compare_op=ALU.is_ge, fill=0.0, base=-1,
                               pattern=[[1, P]], channel_multiplier=-1)
            link(pool.affine_select(out=upto[:, :], in_=upto[:, :], compare_op=ALU.is_ge, fill=0.0, base=0,
                                    pattern=[[1, P]], channel_multiplier=-1))
            pool.nop().then_inc(const_done, 1)

            pool.wait_ge(xl_stored, 32)

            def gathers(tiles, before):
                with pool.Fori(0, tiles // U) as i:
                    for j in range(U):
                        if j % HALF == 0:
                            pool.wait_ge(rec_ready, (before // HALF + 2 * i + j // HALF + 1) * 2)
                        pool.wait_ge(agg_mm, before + U * i + j + 1)
                        pool.sem_inc(slot_claimed, 1)
                        pool.indirect_dma_start(
                            out=gbuf[:, j, :], out_offset=None, in_=xl_d,
                            in_offset=bass.IndirectOffsetOnAxis(ap=idx_slot[:, j // HALF, j % HALF:j % HALF + 1].bitcast(U32), axis=0),
                        ).then_inc(gathered[j], 16)

            gathers(S0, 0)
            gathers(S1, S0)

            pool.wait_ge(x_again, 32)
            pool.wait_ge(mlp_in, 80)
            pool.tensor_tensor(x1, x1, gof_bc.rearrange("p (a d) -> p a d", a=1).to_broadcast([P, NT, D]),
                               ALU.add).then_inc(x_shift, 1)
            pool.wait_ge(pos_ready, 1)
            pool.wait_ge(norm_out, 3 * NT)
            pool.wait_ge(xs_zeroed, 32)
            for k in range(KTOP):
                for t in range(NT):
                    n = P if t < NT - 1 else LAST
                    pool.indirect_dma_start(
                        out=xs_d, out_offset=bass.IndirectOffsetOnAxis(
                            ap=pos_u[0:n, k * NT + t:k * NT + t + 1].bitcast(U32), axis=0),
                        in_=xn[0:n, t, :], in_offset=None).then_inc(scattered, 16)
            pool.wait_ge(y_stored[0], 16 * (FT // 2))
            pool.wait_ge(y_stored[1], 16 * (FT // 2))
            for t in range(NT):
                n = P if t < NT - 1 else LAST
                for k in range(KTOP):
                    g = KTOP * t + k
                    if g >= U:
                        pool.wait_ge(combined, g - U + 1)
                    pool.indirect_dma_start(
                        out=gbuf[0:n, g % U, :], out_offset=None, in_=ys_d,
                        in_offset=bass.IndirectOffsetOnAxis(
                            ap=pos_u[0:n, k * NT + t:k * NT + t + 1].bitcast(U32), axis=0),
                    ).then_inc(combined_in[g % U], 16)

        @block.tensor
        def _(pe):
            mm = nc.tensor.matmul
            pe.nop().then_inc(sort_mm, SR)
            pe.nop().then_inc(agg_mm, U)
            pe.nop().then_inc(ft_mm, 2)
            pe.nop().then_inc(up_mm, 4)
            pe.nop().then_inc(down_mm, 2)
            pe.wait_ge(const_done, 3)
            misc = bank[7]

            def prefixes(nth, B, S):
                pe.wait_ge(counts_ready, nth)
                mm(misc[:, 0:B], above[:, :], cnt[:, 0:B], start=True, stop=True)
                mm(misc[:, 32:32 + B], ones[:, :], cnt[:, 0:B], start=True, stop=True)
                mm(misc[0:B, 64:65], cnt[:, 0:B], ones[:, 0:1], start=True, stop=True).then_inc(counts_mm, 1)
                pe.wait_ge(room_ready, nth)
                mm(misc[0:B, 96:97], upto[0:B, 0:B], room_f[0:B, 32:33], start=True, stop=True).then_inc(ends_mm, 1)
                pe.wait_ge(past_ready, nth)
                mm(misc[0:1, 128:128 + S], one_h32[0:B, :], past[0:B, 0:S], start=True, stop=True).then_inc(table_mm, 1)

            one_h32 = one_h[0:32, :]

            prefixes(1, NB, S0)
            prefixes(2, NB, S1)
            pe.wait_ge(payload_set, 2)
            pe.wait_ge(small_in, 112)
            nc.tensor.transpose(misc[:, 0:P], rows_in, ident[:, :]).then_inc(bias_mm, 1)

            def clear(S):
                for k in range(5):
                    mm(bank[k][:, 0:S], zero_h[:, 0:P], zero_h[:, 0:S], start=True, stop=False, skip_group_check=True)

            def sort_step(c, S, s):
                pe.wait_ge(sort_built, c + 1)
                for k in range(5):
                    left = lo16[:, s, k, :] if k < 2 else lobf[:, s, k - 2, :]
                    m = mm(bank[k][:, 0:S], left, hi16[:, s, 0:S], start=False, stop=False, skip_group_check=True)
                m.then_inc(sort_mm, 1)

            def agg_step(g, gi, j):
                pe.wait_ge(sw_built, g + 1)
                pe.wait_ge(agg_added, g + 1)
                pe.wait_ge(gathered[j], gi)
                mm(bank[5 + j % 2][:, 0:D], Sw[:, j % 4, :], gbuf[:, j, :], start=True, stop=True).then_inc(agg_mm, 1)

            clear(S0)
            with pe.Fori(0, C0 // U) as i:
                for j in range(U):
                    sort_step(U * i + j, S0, j % SR)
            pe.wait_ge(recs_taken, 1)
            clear(S1)
            with pe.Fori(0, C1 // U) as i:
                for j in range(U):
                    sort_step(C0 + U * i + j, S1, j % SR)
                    agg_step(U * i + j, 16 * (i + 1), j)

            def agg_loop(it0, n, w1):
                with pe.Fori(it0, it0 + n) as i:
                    for j in range(U):
                        agg_step(S0 + U * i + j, 16 * (S0 // U + i + 1), j)
                    if w1:
                        pe.wait_ge(staged, 16 * (i + 1))
                        pe.wait_ge(b1_free, i + 1)
                        for hc in range(HC):
                            for kc in range(KC):
                                m = mm(misc[:, hc:hc + 1], stage[:, kc * H + hc * P:kc * H + hc * P + P],
                                       biasT[:, bass.ds(80 + KC * i + kc, 1)], start=kc == 0, stop=kc == KC - 1)
                        m.then_inc(b1_mm, 1)

            agg_loop(0, NE, True)
            agg_loop(NE, S1 // U - NE, False)

            pe.wait_ge(agg_added, 2 + S0 + S1)
            for t in range(NT):
                if t >= 4:
                    pe.wait_ge(t_out, t - 3)
                for kc in range(KC):
                    m = nc.tensor.transpose(bank[t % 4][:, kc * P:kc * P + P], acc[:, t, kc * P:kc * P + P], ident[:, :])
                m.then_inc(t_mm, 1)
            pe.wait_ge(mlp_in, 80)
            NBK = NT * P // 8
            for nb in range(8):
                pe.wait_ge(t_out, min(NT, -(-(nb + 1) * NBK // P)))
                for oc in range(KC):
                    b = bank[4 + (nb * KC + oc) % 4]
                    if nb * KC + oc >= 4:
                        pe.wait_ge(h1_out, nb * KC + oc - 3)
                    for kc in range(KC):
                        m = mm(b[:, 0:NBK], gw1[:, kc, oc * P:oc * P + P], aggT[:, kc, nb * NBK:(nb + 1) * NBK],
                               start=kc == 0, stop=kc == KC - 1)
                    m.then_inc(h1_mm, 1)
            for t in range(NT):
                pe.wait_ge(h1_out, min(8, -(-(t + 1) * P // NBK)) * KC)
                if t >= 4:
                    pe.wait_ge(h2_out, t - 3)
                for kc in range(KC):
                    m = mm(bank[t % 4][:, 0:D], h1T[:, kc, t * P:t * P + P], gw2[:, kc, :],
                           start=kc == 0, stop=kc == KC - 1)
                m.then_inc(h2_mm, 1)
            for t in range(NT):
                pe.wait_ge(norm_out, NT + t + 1)
                if t >= 2:
                    pe.wait_ge(r_out, t - 1)
                for kc in range(KC):
                    m = nc.tensor.transpose(bank[4 + t % 2][:, kc * P:kc * P + P], xl2[:, t, kc * P:kc * P + P], ident[:, :])
                m.then_inc(r_mm, 1)
                pe.wait_ge(r_out, t + 1)
                for kc in range(KC):
                    m = mm(bank[6][:, t * NE:(t + 1) * NE], xT[t % 2][:, kc * P:kc * P + P], Wr_sb[:, kc, :],
                           start=kc == 0, stop=kc == KC - 1)
                m.then_inc(lg_mm, 1)
            prefixes(3, NE, FT)

            def turn(t, q, n):
                pe.wait_ge(xs_in[q], 16 * n)
                pe.wait_ge(fx_split, t + 1)
                for kc in range(KC):
                    m = nc.tensor.transpose(bank[6 + q][:, kc * P:kc * P + P], xs[q][:, kc * P:kc * P + P], ident[:, :])
                m.then_inc(ft_mm, 1)

            def up(t, q):
                e = pe.snap(pe.value_load(exp_tab[0:1, bass.ds(t, 1)], min_val=0, max_val=NE - 1) * WE)
                pe.wait_ge(fx_split, 2 + t + 1)
                for hb in range(2):
                    pe.wait_ge(gelu_done, 2 * t + hb + 1)
                    for hc in range(HC // 2 * hb, HC // 2 * (hb + 1)):
                        o = bank[2 * q + hb][:, (hc % 4) * P:(hc % 4) * P + P]
                        for kc in range(KC):
                            w = [Wall[:, bass.ds(e + (part * KC + kc) * H + hc * P, P)] for part in range(2)]
                            xh, xo = xhi[q][:, kc * P:kc * P + P], xlo[q][:, kc * P:kc * P + P]
                            mm(o, w[0], xh, start=kc == 0, stop=False)
                            mm(o, w[0], xo, start=False, stop=False)
                            m = mm(o, w[1], xh, start=False, stop=kc == KC - 1)
                    m.then_inc(up_mm, 1)

            def down(t, q):
                e = pe.value_load(exp_tab[0:1, bass.ds(t, 1)], min_val=0, max_val=NE - 1)
                ew2 = pe.snap(e * WE + W2BASE)
                eb = pe.snap(e * D)
                pe.wait_ge(y_out, t + 1)
                mm(bank[4 + q][:, 0:D], one_b[:, :], b2rows[:, bass.ds(eb, D)], start=True, stop=False)
                pe.wait_ge(h_split, 2 + t + 1)
                for hc in range(HC):
                    w = [Wall[:, bass.ds(ew2 + part * HC * D + hc * D, D)] for part in range(2)]
                    hh, hl = hhi[q][:, hc * P:hc * P + P], hlo[q][:, hc * P:hc * P + P]
                    mm(bank[4 + q][:, 0:D], hh, w[0], start=False, stop=False)
                    mm(bank[4 + q][:, 0:D], hh, w[1], start=False, stop=False)
                    m = mm(bank[4 + q][:, 0:D], hl, w[0], start=False, stop=hc == HC - 1)
                m.then_inc(down_mm, 1)

            pe.wait_ge(w_done, 4 * NE)
            pe.wait_ge(b2_ready, 1)
            turn(0, 0, 1)
            turn(1, 1, 1)
            up(0, 0)
            with pe.Fori(0, FT // 2 - 1) as i:
                for q in range(2):
                    turn(2 * i + q + 2, q, i + 2)
                    up(2 * i + q + 1, 1 - q)
                    down(2 * i + q, q)
            up(FT - 1, 1)
            down(FT - 2, 0)
            down(FT - 1, 1)

        @block.scalar
        def _(act):
            steps = [0]

            def link(ins):
                steps[0] += 1
                ins.then_inc(act_step, 1)
                act.wait_ge(act_step, steps[0])

            act.nop().then_inc(gelu_done, 4)
            def root(nth):
                act.wait_ge(var_ready, nth)
                act.activation(rstd[:, :], lnt[:, 2, :], ACT.Sqrt).then_inc(root_done, 1)

            root(1)
            act.wait_ge(xl_scaled, 1)
            act.wait_ge(small_in, 112)
            link(act.activation(eps1[:, :], eps1[:, :], ACT.Copy, bias=1.0))
            with act.Fori(0, NT) as t:
                act.activation(xl[:, bass.ds(t, 1), :], x_in[:, bass.ds(t, 1), :], ACT.Identity,
                               bias=nmr[:, bass.ds(t, 1)], scale=rstd[:, bass.ds(t, 1)]).then_inc(xl_done, 1)
                act.wait_ge(xl_done, t + 1)
                act.activation(acc[:, bass.ds(t, 1), :], xl[:, bass.ds(t, 1), :], ACT.Copy,
                               scale=eps1[:, 0:1]).then_inc(acc_set, 1)
            act.wait_ge(bias_mm, 1)
            act.activation(biasT[:, :], bank[7][:, 0:P], ACT.Copy).then_inc(bias_mm, 1)

            def pay(col, h):
                act.activation(pay_slot[:, h, :, :].rearrange("p c k -> p (c k)"),
                               epay.rearrange("p c k -> p (c k)")[:, bass.ds(col * PAY, HALF * PAY)], ACT.Copy).then_inc(pay_ready, 1)

            def rec(c, col, h):
                act.activation(idx_slot[:, h, :], rec_i[c][:, bass.ds(col, HALF)], ACT.Copy).then_inc(rec_ready, 1)
                act.activation(rec_slot[:, h, :, :].rearrange("p c k -> p (c k)"),
                               rec_f[c].rearrange("p c k -> p (c k)")[:, bass.ds(col * 2, HALF * 2)], ACT.Copy).then_inc(rec_ready, 1)

            def pay_next(col, h):
                act.wait_ge(sort_built, col + HALF)
                pay(col + U, h)

            def rec_next(c, tile, col, gi, h):
                for j in range(HALF * h, HALF * (h + 1)):
                    act.wait_ge(gathered[j], gi)
                act.wait_ge(sw_built, tile + HALF)
                rec(c, col + U, h)

            act.wait_ge(payload_set, 1)
            pay(0, 0)
            pay(HALF, 1)
            with act.Fori(0, C0 // U - 1) as i:
                for h in range(2):
                    pay_next(U * i + HALF * h, h)
            act.wait_ge(payload_set, 2)
            for h in range(2):
                act.wait_ge(sort_built, C0 - U + HALF * (h + 1))
                pay(C0 + HALF * h, h)
            act.wait_ge(recs_taken, 1)
            rec(0, 0, 0)
            rec(0, HALF, 1)
            with act.Fori(0, C1 // U - 1) as i:
                for h in range(2):
                    pay_next(C0 + U * i + HALF * h, h)
                    rec_next(0, U * i + HALF * h, U * i + HALF * h, 16 * (i + 1), h)
            act.wait_ge(recs_taken, 2)
            for h in range(2):
                for j in range(HALF * h, HALF * (h + 1)):
                    act.wait_ge(gathered[j], 16 * (S0 // U))
                act.wait_ge(sw_built, S0 - U + HALF * (h + 1))
                rec(1, HALF * h, h)

            def w1_high(e):
                act.wait_ge(staged, 16 * (e + 1))
                for kc in range(KC):
                    act.activation(Wall[:, bass.ds(e * WE + kc * H, H)], stage[:, kc * H:(kc + 1) * H], ACT.Copy,
                                   scale=biasT[:, bass.ds(64 + KC * e + kc, 1)]).then_inc(w_hi, 1)

            def w2_high(e):
                act.wait_ge(staged, 16 * (NE + e + 1))
                for part in range(2):
                    act.activation(Wall[:, bass.ds(W2BASE + e * WE + part * H, H)], stage[:, part * H:(part + 1) * H],
                                   ACT.Copy, scale=WSCALE).then_inc(w_hi, 1)

            def rec_loop(it0, n, work, shift):
                with act.Fori(it0, it0 + n) as i:
                    for h in range(2):
                        rec_next(1, S0 + U * i + HALF * h, U * i + HALF * h, 16 * (S0 // U + i + 1), h)
                    if work:
                        work(i - shift)

            act.wait_ge(g_scaled, 1)
            rec_loop(0, NE, w1_high, 0)
            rec_loop(NE, PREP2, w2_high, NE)
            rec_loop(NE + PREP2, S1 // U - 1 - NE - PREP2, None, 0)

            for t in range(NT):
                act.wait_ge(t_mm, t + 1)
                act.activation(aggT[:, :, t * P:(t + 1) * P],
                               bank[t % 4][:, 0:D].rearrange("p (c n) -> p c n", c=KC), ACT.Copy).then_inc(t_out, 1)
            NBK = NT * P // 8
            for nb in range(8):
                for oc in range(KC):
                    n = nb * KC + oc
                    act.wait_ge(h1_mm, n + 1)
                    act.activation(h1T[:, oc, nb * NBK:(nb + 1) * NBK], bank[4 + n % 4][:, 0:NBK], ACT.Relu,
                                   bias=biasT[:, 96 + oc:97 + oc]).then_inc(h1_out, 1)
            with act.Fori(0, NT) as t:
                act.wait_ge(h2_out, t + 1)
                act.activation(h2[:, bass.ds(t, 1), :], h2[:, bass.ds(t, 1), :], ACT.Relu).then_inc(h2_relu, 1)

            def normalise(nth, to, of):
                root(1 + nth)
                act.wait_ge(ln_coef, nth)
                with act.Fori(0, NT) as t:
                    act.activation(to[:, bass.ds(t, 1), :], of[:, bass.ds(t, 1), :], ACT.Identity,
                                   bias=nmr[:, bass.ds(t, 1)], scale=rstd[:, bass.ds(t, 1)]).then_inc(norm_out, 1)

            normalise(1, h2, h2)
            normalise(2, xl2, x1)
            for t in range(NT):
                act.wait_ge(r_mm, t + 1)
                if t >= 2:
                    act.wait_ge(lg_mm, t - 1)
                act.activation(xT[t % 2], bank[4 + t % 2][:, 0:D], ACT.Copy).then_inc(r_out, 1)
            normalise(3, xn, xl2)
            act.wait_ge(top_ready, 1)
            act.activation(gate[:, 1, :], r_e, ACT.Exp).then_inc(exp_done, 1)
            act.wait_ge(norm_out, 3 * NT)
            with act.Fori(PREP2, NE) as e:
                w2_high(e)

            def x_high(t, q):
                act.wait_ge(ft_mm, 2 + t + 1)
                act.wait_ge(up_mm, 2 * t + 2)
                act.activation(xhi[q], bank[6 + q][:, 0:D], ACT.Copy).then_inc(fx_hi, 1)

            def gelu(t, q):
                e = act.snap(act.value_load(exp_tab[0:1, bass.ds(t, 1)], min_val=0, max_val=NE - 1) * HC)
                act.wait_ge(h_split, t + 1)
                for hb in range(2):
                    act.wait_ge(up_mm, 4 + 2 * t + hb + 1)
                    for hc in range(HC // 2 * hb, HC // 2 * (hb + 1)):
                        m = act.activation(h32[q][:, hc * P:hc * P + P], bank[2 * q + hb][:, (hc % 4) * P:(hc % 4) * P + P],
                                           ACT.Gelu, bias=b1T[:, bass.ds(e + hc, 1)], scale=1.0 / WSCALE)
                    m.then_inc(gelu_done, 1)

            x_high(0, 0)
            x_high(1, 1)
            gelu(0, 0)
            with act.Fori(0, FT // 2 - 1) as i:
                for q in range(2):
                    x_high(2 * i + q + 2, q)
                    gelu(2 * i + q + 1, 1 - q)
            gelu(FT - 1, 1)

        @block.vector
        def _(dve):
            steps = [0]

            def link(ins):
                steps[0] += 1
                ins.then_inc(dve_step, 1)
                dve.wait_ge(dve_step, steps[0])

            dve.nop().then_inc(agg_added, 2)
            dve.nop().then_inc(b1_free, 1)
            dve.nop().then_inc(fx_split, 2)
            dve.nop().then_inc(h_split, 2)
            dve.nop().then_inc(y_out, 2)
            dve.wait_ge(const_done, 3)

            dve.wait_ge(edges_in, 96)

            def epk(k):
                return epay[:, :, k]

            link(dve.tensor_scalar(e_tmp, e_src, 7, None, ALU.arith_shift_right))
            link(dve.tensor_copy(blk_h, e_tmp))
            link(dve.tensor_scalar(e_src, e_src, P - 1, None, ALU.bitwise_and))
            link(dve.tensor_scalar(e_tmp, e_dst, 1, None, ALU.arith_shift_right))
            link(dve.tensor_copy(epk(2), e_tmp))
            link(dve.tensor_scalar(e_dst, e_dst, 1, 7, ALU.bitwise_and, ALU.arith_shift_left))
            link(dve.tensor_tensor(e_dst, e_dst, e_src, ALU.bitwise_or))
            link(dve.tensor_copy(epk(3), e_dst))
            link(dve.tensor_copy(wpart, ew))
            link(dve.tensor_tensor(epk(5), ew, wpart, ALU.subtract))
            dve.tensor_copy(epk(4), ew)
            link(dve.tensor_copy(wpart, epk(5)))
            link(dve.tensor_tensor(epk(6), epk(5), wpart, ALU.subtract))

            def place(nth, B, T, oh, cum, work, S, pos, table, misc=bank[7]):
                flat = oh.rearrange("p b t -> p (b t)")
                cflat = cum.rearrange("p b t -> p (b t)")
                link(dve.tensor_tensor_scan(cflat, one_h[:, 0:1].to_broadcast([P, B * T]), flat, 0.0, ALU.mult, ALU.add))
                link(dve.tensor_copy(cprev[:, 1:B], cum[:, 0:B - 1, T - 1]))
                link(dve.memset(cprev[:, 0:1], 0.0))
                link(dve.tensor_tensor(cnt[:, 0:B], cum[:, :, T - 1], cprev[:, 0:B], ALU.subtract))
                dve.nop().then_inc(counts_ready, 1)
                dve.wait_ge(counts_mm, nth)
                link(dve.tensor_scalar(room_i[:, 0:B], misc[:, 32:32 + B], float(P - 1), None, ALU.add))
                link(dve.tensor_scalar(room_i[0:B, 32:33], misc[0:B, 64:65], float(P - 1), None, ALU.add))
                link(dve.tensor_scalar(room_i[:, 0:B], room_i[:, 0:B], -P, None, ALU.bitwise_and))
                link(dve.tensor_scalar(room_i[0:B, 32:33], room_i[0:B, 32:33], -P, None, ALU.bitwise_and))
                link(dve.tensor_copy(room_f[:, 0:B], room_i[:, 0:B]))
                link(dve.tensor_copy(room_f[0:B, 32:33], room_i[0:B, 32:33]))
                link(dve.tensor_tensor_scan(first[:, 0:B], ones[:, 0:B], room_f[:, 0:B], 0.0, ALU.mult, ALU.add))
                link(dve.tensor_tensor(first[:, 0:B], first[:, 0:B], room_f[:, 0:B], ALU.subtract))
                link(dve.tensor_tensor(first[:, 0:B], first[:, 0:B], misc[:, 0:B], ALU.add))
                dve.nop().then_inc(room_ready, 1)
                link(dve.scalar_tensor_tensor(out=first[:, 0:B], in0=first[:, 0:B], scalar=-1.0, in1=cprev[:, 0:B],
                                              op0=ALU.add, op1=ALU.subtract))
                link(dve.tensor_tensor(work, cum, first[:, 0:B].rearrange("p (b a) -> p b a", a=1).to_broadcast([P, B, T]), ALU.add))
                link(dve.tensor_tensor(work, work, oh, ALU.mult))
                link(dve.tensor_reduce(pos, work.rearrange("p b t -> p t b"), AX_X, ALU.add))
                dve.wait_ge(ends_mm, nth)
                link(dve.tensor_copy(ends[0:B, :], misc[0:B, 96:97]))
                link(dve.tensor_scalar(past[0:B, 0:S], tile_at[0:B, 0:S], ends[0:B, 0:1], None, ALU.is_ge))
                dve.nop().then_inc(past_ready, 1)
                dve.wait_ge(table_mm, nth)
                link(dve.tensor_scalar(table, misc[0:1, 128:128 + S], float(B - 1), None, ALU.min))

            def edge_places(c):
                T, c0 = COLS[c], CSTART[c]
                oh = e_oh[:, 0:NB * T].rearrange("p (b t) -> p b t", b=NB)
                cum = e_cum[:, 0:NB * T].rearrange("p (b t) -> p b t", b=NB)
                work = e_pos[:, 0:NB * T].rearrange("p (b t) -> p b t", b=NB)
                link(dve.tensor_tensor(oh, blk_h[:, c0:c0 + T].rearrange("p (a t) -> p a t", a=1).to_broadcast([P, NB, T]),
                                       iota_h[:, 0:NB].rearrange("p (b a) -> p b a", a=1).to_broadcast([P, NB, T]), ALU.is_equal))
                place(c + 1, NB, T, oh, cum, work, SLOTS[c], pos_j[:, 0:T].bitcast(F32), blk_tab[c][:, :])
                link(dve.tensor_copy(pos_i[:, 0:T], pos_j[:, 0:T].bitcast(F32)))
                link(dve.tensor_scalar(pos_j[:, 0:T], pos_i[:, 0:T], P - 1, None, ALU.bitwise_and))
                link(dve.tensor_copy(epay[:, c0:c0 + T, 0], pos_j[:, 0:T]))
                link(dve.tensor_scalar(pos_j[:, 0:T], pos_i[:, 0:T], 7, None, ALU.arith_shift_right))
                link(dve.tensor_copy(epay[:, c0:c0 + T, 1], pos_j[:, 0:T]))
                dve.nop().then_inc(payload_set, 1)

            lns = [0]

            def coefficients(eps):
                m0, v0, m1, v1 = (stats[:, :, k] for k in (1, 2, 4, 5))
                mean, dev, var = lnt[:, 0, :], lnt[:, 1, :], lnt[:, 2, :]
                link(dve.tensor_tensor(mean, m0, m1, ALU.add))
                link(dve.tensor_tensor(dev, m0, m1, ALU.subtract))
                link(dve.tensor_tensor(var, v0, v1, ALU.add))
                link(dve.scalar_tensor_tensor(out=dev, in0=dev, scalar=0.25, in1=dev, op0=ALU.mult, op1=ALU.mult))
                link(dve.scalar_tensor_tensor(out=var, in0=var, scalar=1.0 / D, in1=dev, op0=ALU.mult, op1=ALU.add))
                link(dve.tensor_scalar(var, var, eps, None, ALU.add))
                dve.nop().then_inc(var_ready, 1)
                lns[0] += 1
                dve.wait_ge(root_done, lns[0])
                link(dve.reciprocal(rstd[:, :], rstd[:, :]))
                link(dve.tensor_tensor(dev, rstd[:, :], rstd[:, :], ALU.mult))
                link(dve.scalar_tensor_tensor(out=dev, in0=dev, scalar=-0.5, in1=var, op0=ALU.mult, op1=ALU.mult))
                link(dve.scalar_tensor_tensor(out=rstd[:, :], in0=dev, scalar=1.5, in1=rstd[:, :], op0=ALU.add, op1=ALU.mult))
                link(dve.scalar_tensor_tensor(out=nmr[:, :], in0=mean, scalar=-0.5, in1=rstd[:, :], op0=ALU.mult, op1=ALU.mult))

            edge_places(0)
            dve.wait_ge(x_loaded, 32)
            with dve.Fori(0, NT) as t:
                dve.bn_stats(stats[:, bass.ds(t, 1), :].rearrange("p a s -> p (a s)"),
                             x_in[:, bass.ds(t, 1), :].rearrange("p a d -> p (a d)")).then_inc(stats_done, 1)
            dve.wait_ge(stats_done, NT)
            coefficients(1e-5)
            dve.nop().then_inc(xl_scaled, 1)
            edge_places(1)

            def sort_build(c, h, jj, s, S):
                dve.wait_ge(sort_mm, c + 1)
                p_ = [pay_slot[:, h, jj, k:k + 1] for k in range(PAY)]
                for k in range(2):
                    dve.tensor_scalar(lo16[:, s, k, :], iota_h[:, 0:P], p_[0], p_[2 + k], ALU.is_equal, ALU.mult)
                for k in range(3):
                    dve.tensor_scalar(lobf[:, s, k, :], iota_h[:, 0:P], p_[0], p_[4 + k], ALU.is_equal, ALU.mult)
                dve.tensor_scalar(hi16[:, s, 0:S], iota_h[:, 0:S], p_[1], None, ALU.is_equal).then_inc(sort_built, 1)

            def records(c):
                S = SLOTS[c]
                dve.wait_ge(sort_mm, SR + sum(COLS[:c + 1]))
                odd = e_pos[:, 0:S]
                link(dve.tensor_scalar(odd, bank[1][:, 0:S], float(P), None, ALU.is_ge))
                link(dve.scalar_tensor_tensor(out=rec_i[c], in0=bank[0][:, 0:S], scalar=2.0, in1=odd, op0=ALU.mult, op1=ALU.add))
                link(dve.scalar_tensor_tensor(out=rec_f[c][:, :, 0], in0=odd, scalar=-float(P), in1=bank[1][:, 0:S],
                                              op0=ALU.mult, op1=ALU.add))
                link(dve.tensor_copy(odd, bank[4][:, 0:S]))
                link(dve.tensor_tensor(odd, odd, bank[3][:, 0:S], ALU.add))
                link(dve.tensor_tensor(rec_f[c][:, :, 1], odd, bank[2][:, 0:S], ALU.add))
                dve.nop().then_inc(recs_taken, 1)

            with dve.Fori(0, C0 // U) as i:
                for j in range(U):
                    if j % HALF == 0:
                        dve.wait_ge(pay_ready, 2 * i + j // HALF + 1)
                    sort_build(U * i + j, j // HALF, j % HALF, j % SR, S0)
            records(0)
            dve.wait_ge(acc_set, NT)

            def sw_build(g, j):
                dve.wait_ge(agg_mm, g + 5)
                r = rec_slot[:, j // HALF, j % HALF, :]
                dve.tensor_scalar(Sw[:, j % 4, :], iota_f[:, 0:P], r[:, 0:1], r[:, 1:2], ALU.is_equal, ALU.mult).then_inc(sw_built, 1)

            def agg_add(g, c, col, j):
                b = dve.value_load(blk_tab[c][0:1, bass.ds(col, 1)], min_val=0, max_val=NB - 1)
                dve.wait_ge(agg_mm, U + g + 1)
                dve.wait_ge(agg_added, 2 + g)
                a = RA[:, bass.ds(b * D, D)]
                dve.tensor_tensor(a, a, bank[5 + j % 2][:, 0:D], ALU.add).then_inc(agg_added, 1)

            with dve.Fori(0, C1 // U) as i:
                for h in range(2):
                    dve.wait_ge(rec_ready, 2 * (2 * i + h + 1))
                    for j in range(HALF * h, HALF * (h + 1)):
                        sw_build(U * i + j, j)
                    dve.wait_ge(pay_ready, C0 // HALF + 2 * i + h + 1)
                    for j in range(HALF * h, HALF * (h + 1)):
                        sort_build(C0 + U * i + j, h, j % HALF, j % SR, S1)
                        agg_add(U * i + j, 0, U * i + j, j)
            records(1)

            def w1_low(e):
                for kc in range(KC):
                    dve.wait_ge(w_hi, 2 * e + kc + 1)
                    dve.scalar_tensor_tensor(out=Wall[:, bass.ds(e * WE + (KC + kc) * H, H)],
                                             in0=stage[:, kc * H:(kc + 1) * H], scalar=biasT[:, bass.ds(64 + KC * e + kc, 1)],
                                             in1=Wall[:, bass.ds(e * WE + kc * H, H)],
                                             op0=ALU.mult, op1=ALU.subtract).then_inc(w_done, 1)
                dve.wait_ge(b1_mm, e + 1)
                dve.tensor_tensor(b1T[:, bass.ds(e * HC, HC)], biasT[:, bass.ds(e * HC, HC)], bank[7][:, 0:HC],
                                  ALU.add).then_inc(b1_free, 1)

            def w2_low(e):
                for part in range(2):
                    dve.wait_ge(w_hi, 2 * NE + 2 * e + part + 1)
                    dve.scalar_tensor_tensor(out=Wall[:, bass.ds(W2BASE + e * WE + (2 + part) * H, H)],
                                             in0=stage[:, part * H:(part + 1) * H], scalar=WSCALE,
                                             in1=Wall[:, bass.ds(W2BASE + e * WE + part * H, H)],
                                             op0=ALU.mult, op1=ALU.subtract).then_inc(w_done, 1)

            dve.wait_ge(bias_mm, 2)
            link(dve.tensor_scalar(biasT[:, 64:80], biasT[:, 64:80], WSCALE, None, ALU.mult))
            dve.nop().then_inc(g_scaled, 1)

            def agg_loop(it0, n, work, shift):
                with dve.Fori(it0, it0 + n) as i:
                    for h in range(2):
                        dve.wait_ge(rec_ready, 2 * (S0 // HALF + 2 * i + h + 1))
                        for j in range(HALF * h, HALF * (h + 1)):
                            sw_build(S0 + U * i + j, j)
                        for j in range(HALF * h, HALF * (h + 1)):
                            agg_add(S0 + U * i + j, 1, U * i + j, j)
                    if work:
                        work(i - shift)

            agg_loop(0, NE, w1_low, 0)
            agg_loop(NE, PREP2, w2_low, NE)
            agg_loop(NE + PREP2, S1 // U - NE - PREP2, None, 0)

            dve.wait_ge(mlp_in, 80)
            for t in range(NT):
                dve.wait_ge(h2_mm, t + 1)
                dve.tensor_tensor(h2[:, t, :], bank[t % 4][:, 0:D], gb2_bc, ALU.add).then_inc(h2_out, 1)

            nstat = [NT]

            def statistics(rows, ready, base):
                with dve.Fori(0, NT) as t:
                    dve.wait_ge(ready, base + t + 1)
                    dve.bn_stats(stats[:, bass.ds(t, 1), :].rearrange("p a s -> p (a s)"),
                                 rows[:, bass.ds(t, 1), :].rearrange("p a d -> p (a d)")).then_inc(stats_done, 1)
                nstat[0] += NT
                dve.wait_ge(stats_done, nstat[0])

            statistics(h2, h2_relu, 0)
            coefficients(1e-10)
            dve.nop().then_inc(ln_coef, 1)
            dve.wait_ge(x_shift, 1)
            with dve.Fori(0, NT) as t:
                dve.wait_ge(norm_out, t + 1)
                a = h2[:, bass.ds(t, 1), :].rearrange("p a d -> p (a d)")
                b = x1[:, bass.ds(t, 1), :].rearrange("p a d -> p (a d)")
                dve.tensor_tensor(a, a, gsc_bc, ALU.mult).then_inc(scaled, 1)
                dve.wait_ge(scaled, t + 1)
                dve.tensor_tensor(b, b, a, ALU.add).then_inc(x1_done, 1)
            statistics(x1, x1_done, 0)
            coefficients(1e-5)
            dve.nop().then_inc(ln_coef, 1)
            statistics(xl2, norm_out, NT)
            coefficients(1e-5)
            dve.nop().then_inc(ln_coef, 1)

            dve.wait_ge(lg_mm, NT)
            bc_e = lambda a: a.rearrange("p (t a) -> p t a", a=1).to_broadcast([P, NT, NE])
            e_row = iota_f[:, 0:NE].rearrange("p (a e) -> p a e", a=1).to_broadcast([P, NT, NE])
            oh = r_oh.rearrange("p (b t) -> p b t", b=NE)
            link(dve.tensor_tensor(lg, bank[6][:, 0:NT * NE].rearrange("p (t e) -> p t e", e=NE),
                                   br_bc[:, :].rearrange("p (a e) -> p a e", a=1).to_broadcast([P, NT, NE]), ALU.add))
            link(dve.tensor_scalar(r_ok, tile_at[:, 0:NT], part_i[:, 0:1], float(N), ALU.add, ALU.is_lt))
            for k in range(KTOP):
                link(dve.tensor_reduce(topv[:, k, :], lg, AX_X, ALU.max))
                link(dve.tensor_tensor(eq, lg, bc_e(topv[:, k, :]), ALU.is_lt))
                link(dve.scalar_tensor_tensor(out=cand, in0=eq, scalar=float(NE), in1=e_row, op0=ALU.mult, op1=ALU.add))
                link(dve.tensor_reduce(topi[:, k, :], cand, AX_X, ALU.min))
                link(dve.tensor_tensor(eq, e_row, bc_e(topi[:, k, :]), ALU.is_equal))
                if k == 0:
                    link(dve.scalar_tensor_tensor(out=lg, in0=eq, scalar=-3.0e38, in1=lg, op0=ALU.mult, op1=ALU.add))
                link(dve.tensor_tensor(oh[:, :, k * NT:(k + 1) * NT].rearrange("p b t -> p t b"), eq, bc_e(r_ok), ALU.mult))
            link(dve.tensor_tensor(r_e, topv[:, 1, :], topv[:, 0, :], ALU.subtract))
            dve.nop().then_inc(top_ready, 1)
            place(3, NE, RC, oh, r_cum.rearrange("p (b t) -> p b t", b=NE), r_pos.rearrange("p (b t) -> p b t", b=NE),
                  FT, pos_f, exp_tab[:, :])
            link(dve.tensor_copy(pos_u[:, :], pos_f))
            dve.nop().then_inc(pos_ready, 1)
            dve.wait_ge(exp_done, 1)
            link(dve.tensor_scalar(gate[:, 0, :], gate[:, 1, :], 1.0, None, ALU.add))
            link(dve.reciprocal(gate[:, 0, :], gate[:, 0, :]))
            link(dve.tensor_tensor(gate[:, 1, :], gate[:, 1, :], gate[:, 0, :], ALU.mult))
            dve.nop().then_inc(router_done, 1)
            with dve.Fori(PREP2, NE) as e:
                w2_low(e)
            dve.wait_ge(b2_in, 16)
            dve.wait_ge(w_done, 4 * NE)
            half = NE * D // 2
            for a in range(2):
                raw, parts = b2raw[:, a * half:(a + 1) * half], b2rows[:, a * half:(a + 1) * half]
                link(dve.tensor_scalar(raw, raw, WSCALE, None, ALU.mult))
                link(dve.tensor_copy(parts, raw))
                link(dve.tensor_tensor(bwork, raw, parts, ALU.subtract))
                link(dve.tensor_scalar(raw, raw, ident[0:3, 0:1], None, ALU.mult))
                link(dve.scalar_tensor_tensor(out=raw, in0=bwork, scalar=ident[0:3, 1:2], in1=raw,
                                              op0=ALU.mult, op1=ALU.add))
                link(dve.tensor_copy(parts, bwork))
                link(dve.tensor_tensor(bwork, bwork, parts, ALU.subtract))
                link(dve.scalar_tensor_tensor(out=raw, in0=bwork, scalar=ident[0:3, 2:3], in1=raw,
                                              op0=ALU.mult, op1=ALU.add))
                link(dve.tensor_copy(parts, raw))
            dve.nop().then_inc(b2_ready, 1)

            dve.wait_ge(scattered, 16 * RC)

            def x_low(t, q):
                dve.wait_ge(fx_hi, t + 1)
                dve.wait_ge(up_mm, 2 * t + 2)
                dve.tensor_tensor(xlo[q], bank[6 + q][:, 0:D], xhi[q], ALU.subtract).then_inc(fx_split, 1)

            def h_parts(t, q):
                dve.wait_ge(gelu_done, 4 + 2 * t + 2)
                dve.wait_ge(down_mm, t + 1)
                dve.tensor_copy(hhi[q], h32[q]).then_inc(hhi_done, 1)
                dve.wait_ge(hhi_done, t + 1)
                dve.tensor_tensor(hlo[q], h32[q], hhi[q], ALU.subtract).then_inc(h_split, 1)

            def y_rows(t, q, n):
                dve.wait_ge(down_mm, 2 + t + 1)
                dve.wait_ge(y_stored[q], 16 * n)
                dve.tensor_scalar(ysb[q], bank[4 + q][:, 0:D], 1.0 / WSCALE, None, ALU.mult).then_inc(y_out, 1)

            x_low(0, 0)
            x_low(1, 1)
            h_parts(0, 0)
            with dve.Fori(0, FT // 2 - 1) as i:
                for q in range(2):
                    x_low(2 * i + q + 2, q)
                    h_parts(2 * i + q + 1, 1 - q)
                    y_rows(2 * i + q, q, i)
            h_parts(FT - 1, 1)
            y_rows(FT - 2, 0, FT // 2 - 1)
            y_rows(FT - 1, 1, FT // 2 - 1)

            for t in range(NT):
                n = P if t < NT - 1 else LAST
                for k in range(KTOP):
                    g = KTOP * t + k
                    dve.wait_ge(combined_in[g % U], 16 * (g // U + 1))
                    if k:
                        dve.wait_ge(combined, g)
                    dve.scalar_tensor_tensor(out=x1[0:n, t, :], in0=gbuf[0:n, g % U, :], scalar=gate[0:n, k, t:t + 1],
                                             in1=x1[0:n, t, :], op0=ALU.mult, op1=ALU.add).then_inc(combined, 1)


_OUT = ((3125, 256), "float32")


def kernel(**inputs):
    import concourse.bacc as _bacc
    from concourse.bass_utils import run_bass_kernel_spmd as _run

    nc = _bacc.Bacc("TRN2", target_bir_lowering=False, num_devices=1)
    arrays, args = {}, []
    for name, a in inputs.items():
        a = np.ascontiguousarray(a)
        arrays[f"in_{name}"] = a
        args.append(nc.dram_tensor(f"in_{name}", a.shape, mybir.dt.from_np(a.dtype), kind="ExternalInput").ap())
    out = nc.dram_tensor("out_dram", _OUT[0], F32, kind="ExternalOutput").ap()
    moe_gnn_program(nc, *args, out)
    r = _run(nc, [arrays], core_ids=[0])
    return r.results[0]["out_dram"]
```

```python
from contextlib import ExitStack

import numpy as np

import concourse.bass as bass
from concourse import mybir

ALU = mybir.AluOpType
ACT = mybir.ActivationFunctionType
AX_X = mybir.AxisListType.X
F32 = mybir.dt.float32
F16 = mybir.dt.float16
BF16 = mybir.dt.bfloat16
I32 = mybir.dt.int32
U32 = mybir.dt.uint32

P = 128


def moe_gnn_program(nc, x, src, dst, edge_weight, gW1, gb1, gW2, gb2, geps, goffset, gscale,
                    Wr, br, ln_g, ln_b, W1, b1, W2, b2, out):
    N, D = x.shape
    E = src.shape[0]
    NE, _, H = W1.shape
    KC, HC = D // P, H // P
    NT = (N + P - 1) // P
    LAST = N - (NT - 1) * P
    NB = NT
    U = 8
    HALF = U // 2

    EC_FULL = (E + P - 1) // P
    EC = (EC_FULL + U - 1) // U * U
    extra = NB - 1
    C0 = (EC - extra) // 2 // U * U
    S0 = (C0 + extra + U - 1) // U * U
    C1 = EC - C0
    S1 = (C1 + extra + U - 1) // U * U
    assert C1 == S0 and S1 <= 256
    COLS, SLOTS, CSTART = (C0, C1), (S0, S1), (0, C0)
    CMAX, SMAX = max(COLS), max(SLOTS)

    KTOP = 2
    LN_EPS, GNN_EPS = 1e-5, 1e-10
    RC = KTOP * NT
    FT = (N * KTOP + NE * (P - 1)) // P
    FT += -FT % 4
    WSCALE = 32.0
    WE = 2 * KC * H
    assert WE == 2 * HC * D
    PREP2 = (S1 // U - 1 - 2 * NE) // 2
    G = 5
    assert NT % G == 0 and 0 < PREP2 < NE

    xl_d = nc.dram_tensor("xl_d", (N, D), F32, kind="Internal").ap()
    xn_d = nc.dram_tensor("xn_d", (N + P, D), F32, kind="Internal").ap()
    sum_d = nc.dram_tensor("sum_d", (N + P, D), F32, kind="Internal").ap()
    biasrow_d = nc.dram_tensor("biasrow_d", (3, (NE + 1) * D), BF16, kind="Internal").ap()

    with ExitStack() as ctx:
        def sb(name, shape, dt):
            return ctx.enter_context(nc.sbuf_tensor(name, shape, dt))

        def sem(name):
            return ctx.enter_context(nc.semaphore(name))

        bank = [ctx.enter_context(nc.psum_tensor(f"bank{i}", [P, 512], F32)) for i in range(8)]

        Wall = sb("Wall", [P, 2 * NE * WE], F16)
        RA = sb("RA", [P, NT * D], F32)
        RB = sb("RB", [P, NT * D], F32)
        gbuf = sb("gbuf", [P, U, D], F32)
        stage = sb("stage", [P, KC * H], F32)
        W2BASE = NE * WE

        def f32view(t, at, n):
            return t[:, 2 * at:2 * (at + n)].bitcast(F32)

        w2f = W2BASE // 2
        x_in = f32view(Wall, w2f, NT * D).rearrange("p (t d) -> p t d", d=D)
        xl = f32view(Wall, w2f + NT * D, NT * D).rearrange("p (t d) -> p t d", d=D)
        acc = RA[:, :].rearrange("p (t d) -> p t d", d=D)
        h2, xn = acc, acc
        x1 = RB[:, :].rearrange("p (t d) -> p t d", d=D)
        NBC = NB * CMAX
        e_oh = Wall[:, 0:NBC]
        e_cum = Wall[:, NBC:2 * NBC]
        e_pos = Wall[:, 2 * NBC:4 * NBC].bitcast(F32)
        PAY = 5
        epay = RB[:, 0:EC * PAY].rearrange("p (c k) -> p c k", k=PAY)
        e16 = RB[:, 0:EC * PAY].bitcast(F16).rearrange("p (c k two) -> p c k two", k=PAY, two=2)
        eb16 = RB[:, 0:EC * PAY].bitcast(BF16).rearrange("p (c k two) -> p c k two", k=PAY, two=2)
        nwords, wwords = e16[:, :, 2, :], eb16[:, :, 3, :]
        at = EC * PAY
        SR = U
        lo_hot = RB[:, at:at + SR * P // 2].bitcast(F16).rearrange("p (s n) -> p s n", s=SR)
        at += SR * P // 2
        lo_node = RB[:, at:at + SR * P].rearrange("p (s n) -> p s n", s=SR)
        at += SR * P
        lo_wt = RB[:, at:at + SR * P].rearrange("p (s n) -> p s n", s=SR)
        at += SR * P
        lo_rest = RB[:, at:at + SR * P // 2].bitcast(BF16).rearrange("p (s n) -> p s n", s=SR)
        at += SR * P // 2
        hi16 = RB[:, at:at + SR * SMAX // 2].bitcast(F16).rearrange("p (s n) -> p s n", s=SR)
        at += SR * SMAX // 2
        assert at <= NT * D
        rec_i, rec_f = [], []
        at = w2f + 2 * NT * D
        for c in range(2):
            rec_i.append(f32view(Wall, at, SLOTS[c]).bitcast(I32))
            at += SLOTS[c]
            rec_f.append(f32view(Wall, at, 2 * SLOTS[c]).rearrange("p (c k) -> p c k", k=2))
            at += 2 * SLOTS[c]
        assert w2f + PREP2 * WE // 2 <= w2f + 2 * NT * D
        gw1 = f32view(Wall, at, KC * D).rearrange("p (c n) -> p c n", c=KC)
        gw2 = f32view(Wall, at + KC * D, KC * D).rearrange("p (c n) -> p c n", c=KC)
        at += 2 * KC * D
        gb2_rows = f32view(Wall, at, D // 2).bitcast(BF16)[0:3, :]
        gsc_bc, gof_bc = (f32view(Wall, at + k * D, D) for k in range(1, 3))
        assert at + 3 * D <= NE * WE
        XR = 4
        xs = [RA[:, q * D:(q + 1) * D] for q in range(XR)]
        at = XR * D
        xhi, xlo, hhi, hlo, h32, ysb = [], [], [], [], [], []
        for q in range(2):
            for lst, n in ((xhi, D // 2), (xlo, D // 2), (hhi, H // 2), (hlo, H // 2)):
                lst.append(RA[:, at:at + n].bitcast(F16))
                at += n
            h32.append(RA[:, at:at + H])
            at += H
            ysb.append(RA[:, at:at + D])
            at += D
        assert at <= NT * D
        aggT, h1T, xT = ([stage[:, (2 * k + q) * D:(2 * k + q + 1) * D] for q in range(2)] for k in range(3))

        ident = sb("ident", [P, P], F32)
        ones = sb("ones", [P, P], F32)
        above = sb("above", [P, P], F32)
        upto = sb("upto", [32, 32], F32)
        iota_i = RA[:, 0:256].bitcast(I32)
        iota_f = sb("iota_f", [P, P], F32)
        iota_h = sb("iota_h", [P, 256], F16)
        tile_at = sb("tile_at", [P, NT], F32)
        part_i = sb("part_i", [P, 1], F32)
        zero_h = sb("zero_h", [P, 256], F16)
        one_h = sb("one_h", [P, 1], F16)
        one_b = sb("one_b", [3, P], BF16)
        Sw = sb("Sw", [P, 4, P], F32)
        pay_slot = sb("pay_slot", [P, 2, HALF, PAY], F32)
        idx_slot = sb("idx_slot", [P, U], I32)
        rec_slot = sb("rec_slot", [P, 2, HALF, 2], F32)
        blk_tab = [sb(f"blk_tab{c}", [1, SLOTS[c] // HALF], I32) for c in range(2)]
        exp_tab = sb("exp_tab", [1, FT], I32)
        biasT = sb("biasT", [P, P], F32)
        b1T = sb("b1T", [P, NE * HC], F32)
        BC = (NE + 1) * D // P
        b2raw = sb("b2raw", [P, BC], F32)
        b2parts = sb("b2parts", [P, 3, BC], BF16)
        b2rows = stage[0:3, 0:NE * D // 2].bitcast(BF16)
        spare = sb("spare", [P, 1], F32)
        slot_tok = sb("slot_tok", [P, FT], I32)
        slot_gate = sb("slot_gate", [P, FT], F32)
        eps1 = sb("eps1", [P, 1], F32)
        Wr_sb = sb("Wr_sb", [P, KC, NE], F32)
        br_bc = sb("br_bc", [P, NE], F32)
        lnt = sb("lnt", [P, 4, NT], F32)
        rstd = sb("rstd", [P, NT], F32)
        nmr = sb("nmr", [P, NT], F32)
        mean1 = sb("mean1", [P, NT], F32)
        ends = sb("ends", [P, 1], F32)
        small = Sw[:, :, :].rearrange("p s n -> p (s n)")
        stats = small[:, 0:NT * 6].rearrange("p (t s) -> p t s", s=6)
        at = NT * 6
        cnt, cprev, first = (small[:, at + 32 * k:at + 32 * (k + 1)] for k in range(3))
        at += 96
        room_i, room_f = small[:, at:at + 33].bitcast(I32), small[:, at + 34:at + 67]
        at += 68
        past = small[0:32, at:at + P].bitcast(F16)
        blk_row = stage[0:1, 1600:1600 + SMAX]
        assert at + P <= 4 * P
        gate = sb("gate", [P, 2, NT], F32)
        rows_in = stage[:, 0:P]

        ei = [stage[:, (k + 1) * 400:(k + 1) * 400 + EC].bitcast(I32) for k in range(3)]
        e_src, e_dst, e_tmp = ei
        ew = gbuf[:, 0:2, :].rearrange("p a d -> p (a d)")[:, 0:EC]
        blk_h = gbuf[:, 2:4, :].rearrange("p a d -> p (a d)")[:, 0:EC // 2].bitcast(F16)
        pos_i = gbuf[:, 6:8, :].rearrange("p a d -> p (a d)")[:, 0:CMAX].bitcast(I32)
        pos_j = gbuf[:, 6:8, :].rearrange("p a d -> p (a d)")[:, CMAX:2 * CMAX].bitcast(I32)
        rt = gbuf[:, :, :].rearrange("p a d -> p (a d)")
        def rslice(k, n):
            return rt[:, 200 * k:200 * k + n]
        lg = rslice(0, NT * NE).rearrange("p (t e) -> p t e", e=NE)
        eq = rslice(1, NT * NE).rearrange("p (t e) -> p t e", e=NE)
        cand = rslice(2, NT * NE).rearrange("p (t e) -> p t e", e=NE)
        topv = rslice(3, 2 * NT).rearrange("p (k t) -> p k t", k=2)
        topi = rslice(4, 2 * NT).rearrange("p (k t) -> p k t", k=2)
        r_ok = rslice(5, NT)
        r_e = rslice(6, NT)
        r_oh = rt[:, 1400:1400 + NE * RC // 2].bitcast(F16)
        r_cum = rt[:, 1600:1600 + NE * RC // 2].bitcast(F16)
        r_tmp = rt[:, 800 + 50:800 + 50 + NT]
        r_pos = rt[:, 0:NE * RC]
        pos_f = rslice(2, RC)
        pos_hi, pos_lo, node_no = (rt[:, 450 + 50 * k:450 + 50 * k + RC] for k in range(3))
        pos_n = rslice(3, RC).bitcast(I32)
        slot_lo = RB[:, :].rearrange("p (c n) -> p c n", n=P)
        slot_hi = RA[:, 0:RC * 2 * FT].rearrange("p (c k n) -> p c k n", k=2, n=FT)
        SCH = RC // 5

        edges_in = sem("edges_in")
        x_loaded = sem("x_loaded")
        stats_done = sem("stats_done")
        var_ready = sem("var_ready")
        root_done = sem("root_done")
        x1_done = sem("x1_done")
        hhi_done = sem("hhi_done")
        g_scaled = sem("g_scaled")
        small_in = sem("small_in")
        const_done = sem("const_done")
        dve_step = sem("dve_step")
        act_step = sem("act_step")
        pool_step = sem("pool_step")
        xl_scaled = sem("xl_scaled")
        xl_done = sem("xl_done")
        acc_set = sem("acc_set")
        xl_stored = sem("xl_stored")
        spare_zeroed = sem("spare_zeroed")
        counts_ready = sem("counts_ready")
        counts_mm = sem("counts_mm")
        ends_mm = sem("ends_mm")
        room_ready = sem("room_ready")
        past_ready = sem("past_ready")
        table_mm = sem("table_mm")
        bias_mm = sem("bias_mm")
        payload_set = sem("payload_set")
        acc_cleared = sem("acc_cleared")
        pay_ready = sem("pay_ready")
        hot_built = sem("hot_built")
        words_built = sem("words_built")
        sort_built = sem("sort_built")
        sort_mm = sem("sort_mm")
        recs_taken = sem("recs_taken")
        idx_ready = sem("idx_ready")
        rec_ready = sem("rec_ready")
        gathered = [sem(f"gathered{j}") for j in range(U)]
        slot_claimed = sem("slot_claimed")
        sw_built = sem("sw_built")
        agg_mm = sem("agg_mm")
        agg_added = sem("agg_added")
        staged = sem("staged")
        w_hi = sem("w_hi")
        w_done = sem("w_done")
        b1_mm = sem("b1_mm")
        b1_free = sem("b1_free")
        mlp_in = sem("mlp_in")
        t_mm = sem("t_mm")
        t_out = sem("t_out")
        h1_mm = sem("h1_mm")
        h1_out = sem("h1_out")
        h2_mm = sem("h2_mm")
        h2_relu = sem("h2_relu")
        x_again = sem("x_again")
        x_shift = sem("x_shift")
        centred = sem("centred")
        xn_coef = sem("xn_coef")
        norm_out = sem("norm_out")
        r_mm = sem("r_mm")
        r_out = sem("r_out")
        lg_mm = sem("lg_mm")
        top_ready = sem("top_ready")
        exp_done = sem("exp_done")
        pos_ready = sem("pos_ready")
        rows_stored = sem("rows_stored")
        slot_lo_built = sem("slot_lo_built")
        slot_hi_built = sem("slot_hi_built")
        slots_mm = sem("slots_mm")
        slots_ready = sem("slots_ready")
        b2_in = sem("b2_in")
        b2_ready = sem("b2_ready")
        xs_in = [sem(f"xs_in{q}") for q in range(XR)]
        ft_mm = sem("ft_mm")
        fx_hi = sem("fx_hi")
        fx_split = sem("fx_split")
        up_mm = sem("up_mm")
        gelu_done = sem("gelu_done")
        h_split = sem("h_split")
        down_mm = sem("down_mm")
        y_out = sem("y_out")
        y_free = sem("y_free")
        y_added = [sem(f"y_added{q}") for q in range(2)]
        out_done = sem("out_done")

        block = ctx.enter_context(nc.Block())
        FULL = (NT - 1) * P
        STORES = 16 * 2 * (NT // G + 1)

        @block.sync
        def _(sp):
            pcols = EC_FULL
            rows = E // pcols
            rest = E - rows * pcols
            sp.wait_ge(const_done, 1)
            for a, t in ((src, e_src), (dst, e_dst), (edge_weight, ew)):
                sp.dma_start(t[0:rows, 0:pcols], a[0:rows * pcols].rearrange("(p c) -> p c", c=pcols)
                             ).then_inc(edges_in, 16)
                sp.dma_start(t[rows:rows + 1, 0:rest], a[rows * pcols:E].rearrange("(p c) -> p c", p=1)
                             ).then_inc(edges_in, 16)
            sp.wait_ge(const_done, 2)
            sp.dma_start(x_in[:, 0:NT - 1, :], x[0:FULL, :].rearrange("(t p) d -> p t d", p=P)).then_inc(x_loaded, 16)
            sp.dma_start(x_in[0:LAST, NT - 1, :], x[FULL:N, :]).then_inc(x_loaded, 16)
            sp.wait_ge(const_done, 3)
            sp.dma_start(rows_in[0:64, :], b1.rearrange("e (c p) -> (e c) p", p=P)).then_inc(small_in, 16)
            sp.dma_start(rows_in[64:80, :], ln_g.rearrange("e (c p) -> (e c) p", p=P)).then_inc(small_in, 16)
            sp.dma_start(rows_in[80:96, :], ln_b.rearrange("e (c p) -> (e c) p", p=P)).then_inc(small_in, 16)
            sp.dma_start(rows_in[96:98, :], gb1.rearrange("(c p) -> c p", p=P)).then_inc(small_in, 16)
            sp.dma_start(eps1[:, :], geps.partition_broadcast(P)).then_inc(small_in, 16)
            sp.dma_start(Wr_sb[:, :, :], Wr.rearrange("(c p) e -> p c e", p=P)).then_inc(small_in, 16)
            sp.dma_start(br_bc[:, :], br.partition_broadcast(P)).then_inc(small_in, 16)
            sp.dma_start(gw1, gW1.rearrange("(c p) n -> p c n", p=P)).then_inc(mlp_in, 16)
            sp.dma_start(gw2, gW2.rearrange("(c p) n -> p c n", p=P)).then_inc(mlp_in, 16)
            sp.dma_start(b2raw[:, 0:BC - KC], b2.rearrange("e d -> (e d)").rearrange("(p c) -> p c", p=P)).then_inc(b2_in, 16)
            sp.dma_start(b2raw[:, BC - KC:BC], gb2.rearrange("(p c) -> p c", p=P)).then_inc(b2_in, 16)
            sp.dma_start(gsc_bc, gscale.partition_broadcast(P)).then_inc(mlp_in, 16)
            sp.dma_start(gof_bc, goffset.partition_broadcast(P)).then_inc(mlp_in, 16)
            sp.wait_ge(xl_done, NT)
            sp.dma_start(xl_d[0:FULL, :].rearrange("(t p) d -> p t d", p=P), xl[:, 0:NT - 1, :]).then_inc(xl_stored, 16)
            sp.dma_start(xl_d[FULL:N, :], xl[0:LAST, NT - 1, :]).then_inc(xl_stored, 16)
            zrow = zero_h[:, :].bitcast(F32)
            for rows in (xn_d, sum_d):
                for h in range(KC):
                    sp.dma_start(rows[N:N + P, h * P:(h + 1) * P], zrow).then_inc(spare_zeroed, 16)
            sp.wait_ge(b2_ready, 1)
            sp.dma_start(biasrow_d[:, 0:NE * D].rearrange("k (p c) -> p k c", p=P), b2parts[:, :, 0:BC - KC]).then_inc(b2_in, 16)
            sp.dma_start(biasrow_d[:, NE * D:].rearrange("k (p c) -> p k c", p=P), b2parts[:, :, BC - KC:BC]).then_inc(b2_in, 16)
            sp.wait_ge(b2_in, 64)
            sp.dma_start(gb2_rows, biasrow_d[:, NE * D:]).then_inc(mlp_in, 16)
            sp.wait_ge(recs_taken, 1)
            sp.wait_ge(bias_mm, 2)
            w1_v = W1.rearrange("e (c p) h -> p e c h", p=P)
            w2_v = W2.rearrange("e (c p) d -> p e c d", p=P)
            with sp.Fori(0, NE) as e:
                sp.wait_ge(b1_mm, 2 * e + 2)
                sp.wait_ge(w_done, 2 * e + 2)
                sp.dma_start(stage[:, :].rearrange("p (a c h) -> p a c h", a=1, c=KC),
                             w1_v[:, bass.ds(e, 1), :, :]).then_inc(staged, 16)
            sp.wait_ge(b1_mm, 2 * NE + 2)
            with sp.Fori(0, PREP2) as e:
                sp.wait_ge(w_done, 2 + 2 * NE + 2 * e)
                sp.dma_start(stage[:, :].rearrange("p (a c d) -> p a c d", a=1, c=HC),
                             w2_v[:, bass.ds(e, 1), :, :]).then_inc(staged, 16)
            sp.wait_ge(recs_taken, 2)
            sp.dma_start(x1[:, 0:NT - 1, :], x[0:FULL, :].rearrange("(t p) d -> p t d", p=P)).then_inc(x_again, 16)
            sp.dma_start(x1[0:LAST, NT - 1, :], x[FULL:N, :]).then_inc(x_again, 16)
            for g in range(NT // G):
                for rows, dst_d, ready in ((x1, sum_d, x1_done), (xn, xn_d, norm_out)):
                    sp.wait_ge(ready, G * (g + 1))
                    last = g == NT // G - 1
                    full = G - 1 if last else G
                    at = g * G * P
                    sp.dma_start(dst_d[at:at + full * P, :].rearrange("(t p) d -> p t d", p=P),
                                 rows[:, G * g:G * g + full, :]).then_inc(rows_stored, 16)
                    if last:
                        sp.dma_start(dst_d[FULL:N, :], rows[0:LAST, NT - 1, :]).then_inc(rows_stored, 16)
            sp.wait_ge(lg_mm, NT)
            with sp.Fori(0, NE - PREP2) as e:
                sp.wait_ge(w_done, 2 + 2 * NE + 2 * PREP2 + 2 * e)
                sp.dma_start(stage[:, :].rearrange("p (a c d) -> p a c d", a=1, c=HC),
                             w2_v[:, bass.ds(e + PREP2, 1), :, :]).then_inc(staged, 16)
            sp.wait_ge(w_done, 2 + 4 * NE)
            sp.dma_start(b2rows, biasrow_d[:, 0:NE * D]).then_inc(b2_in, 16)
            for q in range(2):
                sp.wait_ge(y_added[q], 16 * (FT // 2))
            sp.dma_start(out, sum_d[0:N, :]).then_inc(out_done, 16)
            sp.wait_ge(out_done, 16)

        @block.gpsimd
        def _(pool):
            steps = [0]

            def link(ins):
                steps[0] += 1
                ins.then_inc(pool_step, 1)
                pool.wait_ge(pool_step, steps[0])

            pool.memset(e_src, NB * P)
            pool.memset(e_dst, -2)
            link(pool.memset(ew, 0.0))
            pool.nop().then_inc(const_done, 1)
            link(pool.memset(x_in[:, NT - 1, :], 0.0))
            pool.nop().then_inc(const_done, 1)
            link(pool.iota(iota_i[:, 0:1], [[1, 1]], base=0, channel_multiplier=1))
            link(pool.tensor_copy(part_i[:, :], iota_i[:, 0:1]))
            link(pool.iota(iota_i[:, :], [[1, 256]], base=0, channel_multiplier=0))
            pool.tensor_copy(iota_f[:, :], iota_i[:, 0:P])
            pool.tensor_copy(iota_h[:, :], iota_i[:, :])
            pool.tensor_scalar(tile_at[:, :], iota_i[:, 0:NT], float(P), None, ALU.mult)
            pool.tensor_scalar(spare[:, :], part_i[:, :], float(N + 1), None, ALU.add)
            pool.memset(zero_h[:, :], 0.0)
            pool.memset(one_h[:, :], 1.0)
            pool.memset(one_b[:, :], 1.0)
            pool.memset(ones[:, :], 1.0)
            pool.memset(above[:, :], 1.0)
            pool.memset(upto[:, :], 1.0)
            pool.memset(rows_in, 0.0)
            link(pool.memset(ident[:, :], 0.0))
            pool.affine_select(out=ident[:, :], in_=ident[:, :], compare_op=ALU.not_equal, fill=1.0, base=0,
                               pattern=[[-1, P]], channel_multiplier=1)
            pool.affine_select(out=above[:, :], in_=above[:, :], compare_op=ALU.is_ge, fill=0.0, base=-1,
                               pattern=[[1, P]], channel_multiplier=-1)
            link(pool.affine_select(out=upto[:, :], in_=upto[:, :], compare_op=ALU.is_ge, fill=0.0, base=0,
                                    pattern=[[1, 32]], channel_multiplier=-1))
            pool.nop().then_inc(const_done, 1)

            pool.wait_ge(xl_stored, 32)

            def gathers(tiles, before):
                with pool.Fori(0, tiles // U) as i:
                    for j in range(U):
                        if j % 2 == 0:
                            pool.wait_ge(idx_ready, before // 2 + 4 * i + j // 2 + 1)
                        pool.wait_ge(agg_mm, before + U * i + j + 1)
                        pool.sem_inc(slot_claimed, 1)
                        pool.indirect_dma_start(
                            out=gbuf[:, j, :], out_offset=None, in_=xl_d,
                            in_offset=bass.IndirectOffsetOnAxis(ap=idx_slot[:, j:j + 1].bitcast(U32), axis=0),
                        ).then_inc(gathered[j], 16)

            gathers(S0, 0)
            gathers(S1, S0)

            pool.wait_ge(x_again, 32)
            pool.wait_ge(mlp_in, 80)
            for g in range(NT // G):
                rows = x1[:, G * g:G * (g + 1), :]
                pool.tensor_tensor(rows, rows, gof_bc.rearrange("p (a d) -> p a d", a=1).to_broadcast([P, G, D]),
                                   ALU.add).then_inc(x_shift, 1)
            for t in range(NT):
                pool.wait_ge(xn_coef, t // G + 1)
                pool.tensor_scalar(xn[:, t, :], x1[:, t, :], rstd[:, t:t + 1], nmr[:, t:t + 1],
                                   ALU.mult, ALU.add).then_inc(norm_out, 1)
            pool.wait_ge(pos_ready, 1)
            pool.wait_ge(rows_stored, STORES)
            for c in range(RC):
                pool.tensor_scalar(slot_lo[:, c, :], iota_f[:, :], pos_lo[:, c:c + 1], None, ALU.is_equal
                                   ).then_inc(slot_lo_built, 1)
            pool.wait_ge(slots_ready, 1)
            pool.wait_ge(spare_zeroed, 64)

            def node_rows(t):
                return bass.IndirectOffsetOnAxis(ap=slot_tok[:, t:t + 1].bitcast(U32), axis=0)

            def gather(t):
                pool.indirect_dma_start(out=xs[t % XR], out_offset=None, in_=xn_d, in_offset=node_rows(t)
                                        ).then_inc(xs_in[t % XR], 16)

            for t in range(XR):
                gather(t)
            for t in range(FT):
                if t + XR < FT:
                    pool.wait_ge(ft_mm, 2 + t + 1)
                    gather(t + XR)
                pool.wait_ge(y_out, 2 + t + 1)
                if t:
                    pool.wait_ge(y_added[(t - 1) % 2], 16 * ((t - 1) // 2 + 1))
                    pool.sem_inc(y_free, 1)
                pool.indirect_dma_start(out=sum_d, out_offset=node_rows(t), in_=ysb[t % 2], in_offset=None,
                                        compute_op=ALU.add).then_inc(y_added[t % 2], 16)

        @block.tensor
        def _(pe):
            mm = nc.tensor.matmul
            pe.nop().then_inc(sort_mm, SR)
            pe.nop().then_inc(b1_mm, 2)
            pe.nop().then_inc(agg_mm, U)
            pe.nop().then_inc(ft_mm, 2)
            pe.nop().then_inc(up_mm, 4)
            pe.nop().then_inc(down_mm, 2)
            pe.wait_ge(const_done, 3)
            misc = bank[7]

            def prefixes(nth, B, S):
                pe.wait_ge(counts_ready, nth)
                mm(misc[:, 0:B], above[:, :], cnt[:, 0:B], start=True, stop=True)
                mm(misc[:, 32:32 + B], ones[:, :], cnt[:, 0:B], start=True, stop=True)
                mm(misc[0:B, 64:65], cnt[:, 0:B], ones[:, 0:1], start=True, stop=True).then_inc(counts_mm, 1)
                pe.wait_ge(room_ready, nth)
                mm(misc[0:B, 96:97], upto[0:B, 0:B], room_f[0:B, 32:33], start=True, stop=True).then_inc(ends_mm, 1)
                pe.wait_ge(past_ready, nth)
                mm(misc[0:1, 128:128 + S], one_h32[0:B, :], past[0:B, 0:S], start=True, stop=True).then_inc(table_mm, 1)

            one_h32 = one_h[0:32, :]

            prefixes(1, NB, S0)
            prefixes(2, NB, S1)
            pe.wait_ge(payload_set, 2)
            pe.wait_ge(small_in, 112)
            nc.tensor.transpose(misc[:, 0:P], rows_in, ident[:, :]).then_inc(bias_mm, 1)

            def clear(S):
                for k in range(5):
                    mm(bank[k][:, 0:S], zero_h[:, 0:P], zero_h[:, 0:S], start=True, stop=False, skip_group_check=True)

            def sort_step(c, S, s):
                pe.wait_ge(sort_built, c + 1)
                pe.wait_ge(words_built, c + 1)
                node = lo_node[:, s, :].bitcast(F16).rearrange("p (n two) -> p n two", two=2)
                wt = lo_wt[:, s, :].bitcast(BF16).rearrange("p (n two) -> p n two", two=2)
                for k, left in enumerate((node[:, :, 1], node[:, :, 0], wt[:, :, 1], wt[:, :, 0], lo_rest[:, s, :])):
                    m = mm(bank[k][:, 0:S], left, hi16[:, s, 0:S], start=False, stop=False, skip_group_check=True)
                m.then_inc(sort_mm, 1)

            def agg_step(g, gi, j):
                pe.wait_ge(sw_built, g + 1)
                pe.wait_ge(agg_added, g + 1)
                pe.wait_ge(gathered[j], gi)
                mm(bank[5 + j % 2][:, 0:D], Sw[:, j % 4, :], gbuf[:, j, :], start=True, stop=True).then_inc(agg_mm, 1)

            clear(S0)
            with pe.Fori(0, C0 // U) as i:
                for j in range(U):
                    sort_step(U * i + j, S0, j % SR)
            pe.wait_ge(recs_taken, 1)
            clear(S1)
            with pe.Fori(0, C1 // U) as i:
                for j in range(U):
                    agg_step(U * i + j, 16 * (i + 1), j)
                    sort_step(C0 + U * i + j, S1, j % SR)

            with pe.Fori(0, NE) as e:
                for a in range(2):
                    for j in range(U):
                        agg_step(S0 + U * (2 * e + a) + j, 16 * (S0 // U + 2 * e + a + 1), j)
                    pe.wait_ge(staged, 16 * (e + 1))
                    pe.wait_ge(b1_free, 2 * e + a + 1)
                    for hc in range(HC // 2):
                        for kc in range(KC):
                            w = kc * H + (HC // 2 * a + hc) * P
                            m = mm(misc[:, hc:hc + 1], stage[:, w:w + P],
                                   biasT[:, bass.ds(80 + KC * e + kc, 1)], start=kc == 0, stop=kc == KC - 1)
                    m.then_inc(b1_mm, 1)
            with pe.Fori(2 * NE, S1 // U) as i:
                for j in range(U):
                    agg_step(S0 + U * i + j, 16 * (S0 // U + i + 1), j)

            pe.wait_ge(agg_added, 2 + S0 + S1)
            pe.wait_ge(mlp_in, 80)
            for n in range(-2, NT + 2 * G + 2):
                t = n + 2
                if 0 <= t < NT:
                    if t >= 2:
                        pe.wait_ge(t_out, t - 1)
                    for kc in range(KC):
                        m = nc.tensor.transpose(bank[t % 2][:, kc * P:kc * P + P], acc[:, t, kc * P:kc * P + P], ident[:, :])
                    m.then_inc(t_mm, 1)
                t = n - 2 * G - 1
                if 0 <= t < NT:
                    pe.wait_ge(norm_out, t + 1)
                    if t >= 2:
                        pe.wait_ge(r_out, t - 1)
                    for kc in range(KC):
                        m = nc.tensor.transpose(bank[5 + t % 2][:, kc * P:kc * P + P], xn[:, t, kc * P:kc * P + P], ident[:, :])
                    m.then_inc(r_mm, 1)
                t = n + 1
                if 0 <= t < NT:
                    pe.wait_ge(t_out, t + 1)
                    if t >= 2:
                        pe.wait_ge(h1_out, KC * (t - 1))
                    for oc in range(KC):
                        for kc in range(KC):
                            m = mm(bank[2 + t % 2][:, oc * P:oc * P + P], gw1[:, kc, oc * P:oc * P + P],
                                   aggT[t % 2][:, kc * P:kc * P + P], start=kc == 0, stop=kc == KC - 1)
                    m.then_inc(h1_mm, 1)
                t = n
                if 0 <= t < NT:
                    pe.wait_ge(h1_out, KC * (t + 1))
                    if t >= 1:
                        pe.wait_ge(h2_relu, t)
                    mm(bank[4][:, 0:D], one_b[:, :], gb2_rows, start=True, stop=False)
                    for kc in range(KC):
                        m = mm(bank[4][:, 0:D], h1T[t % 2][:, kc * P:kc * P + P], gw2[:, kc, :],
                               start=False, stop=kc == KC - 1)
                    m.then_inc(h2_mm, 1)
                t = n - 2 * G - 2
                if 0 <= t < NT:
                    pe.wait_ge(r_out, t + 1)
                    for kc in range(KC):
                        m = mm(misc[:, t * NE:(t + 1) * NE], xT[t % 2][:, kc * P:kc * P + P], Wr_sb[:, kc, :],
                               start=kc == 0, stop=kc == KC - 1)
                    m.then_inc(lg_mm, 1)
            prefixes(3, NE, FT)
            for c in range(RC):
                pe.wait_ge(slot_lo_built, c + 1)
                if c % SCH == 0:
                    pe.wait_ge(slot_hi_built, c // SCH + 1)
                m = mm(bank[0][:, 0:2 * FT], slot_lo[:, c, :], slot_hi[:, c, :, :].rearrange("p k n -> p (k n)"),
                       start=c == 0, stop=c == RC - 1)
            m.then_inc(slots_mm, 1)

            def turn(t, q, n):
                pe.wait_ge(xs_in[q], 16 * n)
                pe.wait_ge(fx_split, t + 1)
                for kc in range(KC):
                    m = nc.tensor.transpose(bank[6 + q % 2][:, kc * P:kc * P + P], xs[q][:, kc * P:kc * P + P], ident[:, :])
                m.then_inc(ft_mm, 1)

            def expert(t):
                return pe.value_load(exp_tab[0:1, bass.ds(t, 1)], min_val=0, max_val=NE - 1)

            def up(t, q, ex):
                e = pe.snap(ex * WE)
                pe.wait_ge(fx_split, 2 + t + 1)
                for hb in range(2):
                    pe.wait_ge(gelu_done, 2 * t + hb + 1)
                    for hc in range(HC // 2 * hb, HC // 2 * (hb + 1)):
                        o = bank[2 * q + hb][:, (hc % 4) * P:(hc % 4) * P + P]
                        for kc in range(KC):
                            w = [Wall[:, bass.ds(e + (part * KC + kc) * H + hc * P, P)] for part in range(2)]
                            xh, xo = xhi[q][:, kc * P:kc * P + P], xlo[q][:, kc * P:kc * P + P]
                            mm(o, w[0], xh, start=kc == 0, stop=False)
                            mm(o, w[0], xo, start=False, stop=False)
                            m = mm(o, w[1], xh, start=False, stop=kc == KC - 1)
                    m.then_inc(up_mm, 1)

            def down(t, q, ex):
                ew2 = pe.snap(ex * WE + W2BASE)
                eb = pe.snap(ex * D)
                pe.wait_ge(y_out, t + 1)
                mm(bank[4 + q][:, 0:D], one_b[:, :], b2rows[:, bass.ds(eb, D)], start=True, stop=False)
                pe.wait_ge(h_split, 2 + t + 1)
                for hc in range(HC):
                    w = [Wall[:, bass.ds(ew2 + part * HC * D + hc * D, D)] for part in range(2)]
                    hh, hl = hhi[q][:, hc * P:hc * P + P], hlo[q][:, hc * P:hc * P + P]
                    mm(bank[4 + q][:, 0:D], hh, w[0], start=False, stop=False)
                    mm(bank[4 + q][:, 0:D], hh, w[1], start=False, stop=False)
                    m = mm(bank[4 + q][:, 0:D], hl, w[0], start=False, stop=hc == HC - 1)
                m.then_inc(down_mm, 1)

            pe.wait_ge(w_done, 2 + 4 * NE)
            pe.wait_ge(b2_in, 80)
            turn(0, 0, 1)
            turn(1, 1, 1)
            up(0, 0, expert(0))
            with pe.Fori(0, FT // XR - 1) as i:
                ex = [expert(XR * i + q) for q in range(XR + 1)]
                for q in range(XR):
                    turn(XR * i + q + 2, (q + 2) % XR, i + 1 + (q + 2) // XR)
                    up(XR * i + q + 1, (q + 1) % 2, ex[q + 1])
                    down(XR * i + q, q % 2, ex[q])
            ex = [expert(t) for t in range(FT - XR, FT)]
            for q in range(XR):
                t = FT - XR + q
                if t + 2 < FT:
                    turn(t + 2, (t + 2) % XR, (t + 2) // XR + 1)
                if t + 1 < FT:
                    up(t + 1, (t + 1) % 2, ex[q + 1])
                down(t, q % 2, ex[q])

        @block.scalar
        def _(act):
            steps = [0]

            def link(ins):
                steps[0] += 1
                ins.then_inc(act_step, 1)
                act.wait_ge(act_step, steps[0])

            act.nop().then_inc(gelu_done, 4)
            def root(nth, lo, hi):
                act.wait_ge(var_ready, nth)
                act.activation(rstd[:, lo:hi], lnt[:, 2, lo:hi], ACT.Sqrt).then_inc(root_done, 1)

            root(1, 0, NT)
            act.wait_ge(xl_scaled, 1)
            act.wait_ge(small_in, 112)
            link(act.activation(eps1[:, :], eps1[:, :], ACT.Copy, bias=1.0))
            with act.Fori(0, NT) as t:
                act.activation(xl[:, bass.ds(t, 1), :], x_in[:, bass.ds(t, 1), :], ACT.Identity,
                               bias=nmr[:, bass.ds(t, 1)], scale=rstd[:, bass.ds(t, 1)]).then_inc(xl_done, 1)
                act.wait_ge(xl_done, t + 1)
                act.activation(acc[:, bass.ds(t, 1), :], xl[:, bass.ds(t, 1), :], ACT.Copy,
                               scale=eps1[:, 0:1]).then_inc(acc_set, 1)
            act.wait_ge(bias_mm, 1)
            act.activation(biasT[:, :], bank[7][:, 0:P], ACT.Copy).then_inc(bias_mm, 1)

            def pay(col, h):
                act.activation(pay_slot[:, h, :, :].rearrange("p c k -> p (c k)"),
                               epay.rearrange("p c k -> p (c k)")[:, bass.ds(col * PAY, HALF * PAY)], ACT.Copy).then_inc(pay_ready, 1)

            def idx(c, col, j):
                act.activation(idx_slot[:, j:j + 2], rec_i[c][:, bass.ds(col, 2)], ACT.Copy).then_inc(idx_ready, 1)

            def rec(c, col, h):
                act.activation(rec_slot[:, h, :, :].rearrange("p c k -> p (c k)"),
                               rec_f[c].rearrange("p c k -> p (c k)")[:, bass.ds(col * 2, HALF * 2)], ACT.Copy).then_inc(rec_ready, 1)

            def pay_next(col, h):
                act.wait_ge(sort_built, col + HALF)
                act.wait_ge(words_built, col + HALF)
                pay(col + U, h)

            def idx_next(c, col, gi, j):
                act.wait_ge(gathered[j], gi)
                act.wait_ge(gathered[j + 1], gi)
                idx(c, col + j + U, j)

            def rec_next(c, tile, col, h):
                act.wait_ge(sw_built, tile + HALF)
                rec(c, col + U, h)

            def words(col, s, rest):
                h, jj = s // HALF, s % HALF
                act.wait_ge(hot_built, col + 1)
                act.activation(lo_node[:, s, :], lo_hot[:, s, :], ACT.Copy, scale=pay_slot[:, h, jj, 2:3])
                if rest:
                    act.activation(lo_rest[:, s, :], lo_hot[:, s, :], ACT.Copy, scale=pay_slot[:, h, jj, 4:5])
                act.activation(lo_wt[:, s, :], lo_hot[:, s, :], ACT.Copy, scale=pay_slot[:, h, jj, 3:4]).then_inc(words_built, 1)

            act.wait_ge(payload_set, 1)
            pay(0, 0)
            pay(HALF, 1)
            with act.Fori(0, C0 // U - 1) as i:
                for h in range(2):
                    act.wait_ge(pay_ready, 2 * i + h + 1)
                    for j in range(HALF * h, HALF * (h + 1)):
                        words(U * i + j, j, False)
                    pay_next(U * i + HALF * h, h)
            act.wait_ge(payload_set, 2)
            for h in range(2):
                act.wait_ge(pay_ready, C0 // HALF - 2 + h + 1)
                for j in range(HALF * h, HALF * (h + 1)):
                    words(C0 - U + j, j, False)
                act.wait_ge(sort_built, C0 - U + HALF * (h + 1))
                act.wait_ge(words_built, C0 - U + HALF * (h + 1))
                pay(C0 + HALF * h, h)
            act.wait_ge(recs_taken, 1)
            for j in range(0, U, 2):
                idx(0, j, j)
            rec(0, 0, 0)
            rec(0, HALF, 1)
            with act.Fori(0, C1 // U - 1) as i:
                for h in range(2):
                    act.wait_ge(pay_ready, C0 // HALF + 2 * i + h + 1)
                    for j in range(HALF * h, HALF * (h + 1), 2):
                        words(C0 + U * i + j, j, True)
                        words(C0 + U * i + j + 1, j + 1, True)
                        idx_next(0, U * i, 16 * (i + 1), j)
                    pay_next(C0 + U * i + HALF * h, h)
                    rec_next(0, U * i + HALF * h, U * i + HALF * h, h)
            for h in range(2):
                act.wait_ge(pay_ready, EC // HALF - 2 + h + 1)
                for j in range(HALF * h, HALF * (h + 1)):
                    words(EC - U + j, j, True)
            act.wait_ge(recs_taken, 2)
            for j in range(0, U, 2):
                act.wait_ge(gathered[j], 16 * (S0 // U))
                act.wait_ge(gathered[j + 1], 16 * (S0 // U))
                idx(1, j, j)
            for h in range(2):
                act.wait_ge(sw_built, S0 - U + HALF * (h + 1))
                rec(1, HALF * h, h)

            def w1_high(m):
                act.wait_ge(staged, 16 * (m // 2 + 1))
                act.activation(Wall[:, bass.ds((m // 2) * WE + (m % 2) * H, H)], stage[:, bass.ds((m % 2) * H, H)], ACT.Copy,
                               scale=biasT[:, bass.ds(64 + m, 1)]).then_inc(w_hi, 1)

            def w2_high(m):
                act.wait_ge(staged, 16 * (NE + m // 2 + 1))
                act.activation(Wall[:, bass.ds(W2BASE + (m // 2) * WE + (m % 2) * H, H)], stage[:, bass.ds((m % 2) * H, H)],
                               ACT.Copy, scale=WSCALE).then_inc(w_hi, 1)

            def rec_loop(it0, n, work, shift):
                with act.Fori(it0, it0 + n) as i:
                    for h in range(2):
                        for j in range(HALF * h, HALF * (h + 1), 2):
                            idx_next(1, U * i, 16 * (S0 // U + i + 1), j)
                        rec_next(1, S0 + U * i + HALF * h, U * i + HALF * h, h)
                    if work:
                        work(i - shift)

            act.wait_ge(g_scaled, 1)
            rec_loop(0, 2 * NE, w1_high, 0)
            rec_loop(2 * NE, 2 * PREP2, w2_high, 2 * NE)
            if S1 // U - 1 > 2 * (NE + PREP2):
                rec_loop(2 * (NE + PREP2), S1 // U - 1 - 2 * (NE + PREP2), None, 0)

            act.wait_ge(w_done, 2 + 2 * (NE + PREP2))
            for n in range(-2, NT + 2 * G + 2):
                t = n + 2
                if 0 <= t < NT:
                    act.wait_ge(t_mm, t + 1)
                    if t >= 2:
                        act.wait_ge(h1_mm, t - 1)
                    act.activation(aggT[t % 2], bank[t % 2][:, 0:D], ACT.Copy).then_inc(t_out, 1)
                t = n - 2 * G - 2
                if 0 <= t < NT:
                    act.wait_ge(r_mm, t + 1)
                    if t >= 2:
                        act.wait_ge(lg_mm, t - 1)
                    act.activation(xT[t % 2], bank[5 + t % 2][:, 0:D], ACT.Copy).then_inc(r_out, 1)
                t = n + 1
                if 0 <= t < NT:
                    act.wait_ge(h1_mm, t + 1)
                    if t >= 2:
                        act.wait_ge(h2_mm, t - 1)
                    for oc in range(KC):
                        act.activation(h1T[t % 2][:, oc * P:oc * P + P], bank[2 + t % 2][:, oc * P:oc * P + P], ACT.Relu,
                                       bias=biasT[:, 96 + oc:97 + oc]).then_inc(h1_out, 1)
                t = n
                if t > 0 and t % G == 0 and t <= NT + G:
                    g = t // G - 1
                    root(2 + g, G * max(g - 1, 0), min(G * (g + 1), NT))
                if 0 <= t < NT:
                    act.wait_ge(h2_mm, t + 1)
                    act.activation(h2[:, t, :], bank[4][:, 0:D], ACT.Relu).then_inc(h2_relu, 1)
            act.wait_ge(var_ready, 3 + NT // G)
            act.activation(lnt[:, 1, :], lnt[:, 3, :], ACT.Sqrt).then_inc(root_done, 1)
            act.wait_ge(top_ready, 1)
            act.activation(gate[:, 1, :], r_e, ACT.Exp).then_inc(exp_done, 1)
            act.wait_ge(x1_done, NT)
            with act.Fori(2 * PREP2, 2 * NE) as m:
                w2_high(m)

            def x_high(t, q):
                act.wait_ge(ft_mm, 2 + t + 1)
                act.wait_ge(up_mm, 2 * t + 2)
                act.activation(xhi[q], bank[6 + q][:, 0:D], ACT.Copy).then_inc(fx_hi, 1)

            def gelu(t, q):
                e = act.snap(act.value_load(exp_tab[0:1, bass.ds(t, 1)], min_val=0, max_val=NE - 1) * HC)
                act.wait_ge(h_split, t + 1)
                for hb in range(2):
                    act.wait_ge(up_mm, 4 + 2 * t + hb + 1)
                    for hc in range(HC // 2 * hb, HC // 2 * (hb + 1)):
                        m = act.activation(h32[q][:, hc * P:hc * P + P], bank[2 * q + hb][:, (hc % 4) * P:(hc % 4) * P + P],
                                           ACT.Gelu, bias=b1T[:, bass.ds(e + hc, 1)], scale=1.0 / WSCALE)
                    m.then_inc(gelu_done, 1)

            x_high(0, 0)
            x_high(1, 1)
            gelu(0, 0)
            with act.Fori(0, FT // 2 - 1) as i:
                for q in range(2):
                    x_high(2 * i + q + 2, q)
                    gelu(2 * i + q + 1, 1 - q)
            gelu(FT - 1, 1)

        @block.vector
        def _(dve):
            steps = [0]

            def link(ins):
                steps[0] += 1
                ins.then_inc(dve_step, 1)
                dve.wait_ge(dve_step, steps[0])

            dve.nop().then_inc(agg_added, 2)
            dve.nop().then_inc(b1_free, 1)
            dve.nop().then_inc(fx_split, 2)
            dve.nop().then_inc(h_split, 2)
            dve.nop().then_inc(y_out, 2)
            dve.nop().then_inc(y_free, 2)
            dve.nop().then_inc(w_done, 2)
            dve.wait_ge(const_done, 3)

            dve.wait_ge(edges_in, 96)

            link(dve.tensor_scalar(e_tmp, e_src, 7, None, ALU.arith_shift_right))
            link(dve.tensor_copy(blk_h, e_tmp))
            link(dve.tensor_scalar(e_src, e_src, P - 1, None, ALU.bitwise_and))
            link(dve.tensor_scalar(e_tmp, e_dst, 1, None, ALU.arith_shift_right))
            link(dve.tensor_scalar(nwords[:, :, 1], e_tmp, 1.0, None, ALU.add))
            link(dve.tensor_scalar(e_dst, e_dst, 1, 7, ALU.bitwise_and, ALU.arith_shift_left))
            link(dve.tensor_tensor(e_dst, e_dst, e_src, ALU.bitwise_or))
            link(dve.tensor_copy(nwords[:, :, 0], e_dst))
            link(dve.tensor_copy(wwords[:, :, 1], ew))
            link(dve.tensor_tensor(ew, ew, wwords[:, :, 1], ALU.subtract))
            link(dve.tensor_copy(wwords[:, :, 0], ew))
            link(dve.tensor_tensor(epay[:, :, 4], ew, wwords[:, :, 0], ALU.subtract))

            def place(nth, B, T, oh, cum, work, S, pos, table, misc=bank[7]):
                flat = oh.rearrange("p b t -> p (b t)")
                cflat = cum.rearrange("p b t -> p (b t)")
                link(dve.tensor_tensor_scan(cflat, one_h[:, 0:1].to_broadcast([P, B * T]), flat, 0.0, ALU.mult, ALU.add))
                link(dve.tensor_copy(cprev[:, 1:B], cum[:, 0:B - 1, T - 1]))
                link(dve.memset(cprev[:, 0:1], 0.0))
                link(dve.tensor_tensor(cnt[:, 0:B], cum[:, :, T - 1], cprev[:, 0:B], ALU.subtract))
                dve.nop().then_inc(counts_ready, 1)
                dve.wait_ge(counts_mm, nth)
                link(dve.tensor_scalar(room_i[:, 0:B], misc[:, 32:32 + B], float(P - 1), None, ALU.add))
                link(dve.tensor_scalar(room_i[0:B, 32:33], misc[0:B, 64:65], float(P - 1), None, ALU.add))
                link(dve.tensor_scalar(room_i[:, 0:B], room_i[:, 0:B], -P, None, ALU.bitwise_and))
                link(dve.tensor_scalar(room_i[0:B, 32:33], room_i[0:B, 32:33], -P, None, ALU.bitwise_and))
                link(dve.tensor_copy(room_f[:, 0:B], room_i[:, 0:B]))
                link(dve.tensor_copy(room_f[0:B, 32:33], room_i[0:B, 32:33]))
                link(dve.tensor_tensor_scan(first[:, 0:B], ones[:, 0:B], room_f[:, 0:B], 0.0, ALU.mult, ALU.add))
                link(dve.tensor_tensor(first[:, 0:B], first[:, 0:B], room_f[:, 0:B], ALU.subtract))
                link(dve.tensor_tensor(first[:, 0:B], first[:, 0:B], misc[:, 0:B], ALU.add))
                dve.nop().then_inc(room_ready, 1)
                link(dve.scalar_tensor_tensor(out=first[:, 0:B], in0=first[:, 0:B], scalar=-1.0, in1=cprev[:, 0:B],
                                              op0=ALU.add, op1=ALU.subtract))
                link(dve.tensor_tensor(work, cum, first[:, 0:B].rearrange("p (b a) -> p b a", a=1).to_broadcast([P, B, T]), ALU.add))
                link(dve.tensor_tensor(work, work, oh, ALU.mult))
                link(dve.tensor_reduce(pos, work.rearrange("p b t -> p t b"), AX_X, ALU.add))
                dve.wait_ge(ends_mm, nth)
                link(dve.tensor_scalar(ends[0:B, :], misc[0:B, 96:97], 1.0 / P, None, ALU.mult))
                link(dve.tensor_scalar(past[0:B, 0:S], iota_h[0:B, 0:S], ends[0:B, 0:1], None, ALU.is_ge))
                dve.nop().then_inc(past_ready, 1)
                dve.wait_ge(table_mm, nth)
                link(dve.tensor_scalar(table, misc[0:1, 128:128 + S], float(B - 1), None, ALU.min))
                return table

            def edge_places(c):
                T, c0 = COLS[c], CSTART[c]
                oh = e_oh[:, 0:NB * T].rearrange("p (b t) -> p b t", b=NB)
                cum = e_cum[:, 0:NB * T].rearrange("p (b t) -> p b t", b=NB)
                work = e_pos[:, 0:NB * T].rearrange("p (b t) -> p b t", b=NB)
                link(dve.tensor_tensor(oh, blk_h[:, c0:c0 + T].rearrange("p (a t) -> p a t", a=1).to_broadcast([P, NB, T]),
                                       iota_h[:, 0:NB].rearrange("p (b a) -> p b a", a=1).to_broadcast([P, NB, T]), ALU.is_equal))
                place(c + 1, NB, T, oh, cum, work, SLOTS[c], pos_j[:, 0:T].bitcast(F32), blk_row[:, 0:SLOTS[c]])
                four = blk_row[:, 0:SLOTS[c]].rearrange("p (g k) -> p g k", k=HALF)
                for k in range(HALF - 2, 0, -1):
                    link(dve.scalar_tensor_tensor(out=four[:, :, k], in0=four[:, :, k + 1], scalar=float(NB),
                                                  in1=four[:, :, k], op0=ALU.mult, op1=ALU.add))
                link(dve.scalar_tensor_tensor(out=blk_tab[c][:, :], in0=four[:, :, 1], scalar=float(NB),
                                              in1=four[:, :, 0], op0=ALU.mult, op1=ALU.add))
                link(dve.tensor_copy(pos_i[:, 0:T], pos_j[:, 0:T].bitcast(F32)))
                link(dve.tensor_scalar(pos_j[:, 0:T], pos_i[:, 0:T], P - 1, None, ALU.bitwise_and))
                link(dve.tensor_copy(epay[:, c0:c0 + T, 0], pos_j[:, 0:T]))
                link(dve.tensor_scalar(pos_j[:, 0:T], pos_i[:, 0:T], 7, None, ALU.arith_shift_right))
                link(dve.tensor_copy(epay[:, c0:c0 + T, 1], pos_j[:, 0:T]))
                dve.nop().then_inc(payload_set, 1)

            def moments(lo, hi):
                m0, v0, m1, v1 = (stats[:, lo:hi, k] for k in (1, 2, 4, 5))
                mean, dev, var = (lnt[:, k, lo:hi] for k in range(3))
                link(dve.tensor_tensor(mean, m0, m1, ALU.add))
                link(dve.tensor_tensor(dev, m0, m1, ALU.subtract))
                link(dve.tensor_tensor(var, v0, v1, ALU.add))
                link(dve.scalar_tensor_tensor(out=dev, in0=dev, scalar=0.25, in1=dev, op0=ALU.mult, op1=ALU.mult))
                link(dve.scalar_tensor_tensor(out=var, in0=var, scalar=1.0 / D, in1=dev, op0=ALU.mult, op1=ALU.add))

            def refine(r_, v_, tmp):
                link(dve.reciprocal(r_, r_))
                link(dve.tensor_tensor(tmp, r_, r_, ALU.mult))
                link(dve.scalar_tensor_tensor(out=tmp, in0=tmp, scalar=-0.5, in1=v_, op0=ALU.mult, op1=ALU.mult))
                link(dve.scalar_tensor_tensor(out=r_, in0=tmp, scalar=1.5, in1=r_, op0=ALU.add, op1=ALU.mult))

            def coefficients(nth, lo, hi):
                dve.wait_ge(root_done, nth)
                refine(rstd[:, lo:hi], lnt[:, 2, lo:hi], lnt[:, 1, lo:hi])
                link(dve.scalar_tensor_tensor(out=nmr[:, lo:hi], in0=lnt[:, 0, lo:hi], scalar=-0.5, in1=rstd[:, lo:hi],
                                              op0=ALU.mult, op1=ALU.mult))

            edge_places(0)
            dve.wait_ge(x_loaded, 32)
            with dve.Fori(0, NT) as t:
                dve.bn_stats(stats[:, bass.ds(t, 1), :].rearrange("p a s -> p (a s)"),
                             x_in[:, bass.ds(t, 1), :].rearrange("p a d -> p (a d)")).then_inc(stats_done, 1)
            dve.wait_ge(stats_done, NT)
            moments(0, NT)
            link(dve.tensor_scalar(lnt[:, 2, :], lnt[:, 2, :], LN_EPS, None, ALU.add))
            dve.nop().then_inc(var_ready, 1)
            coefficients(1, 0, NT)
            dve.nop().then_inc(xl_scaled, 1)
            edge_places(1)
            dve.wait_ge(b2_in, 32)
            link(dve.tensor_scalar(b2raw[:, 0:BC - KC], b2raw[:, 0:BC - KC], WSCALE, None, ALU.mult))
            for k in range(3):
                link(dve.tensor_copy(b2parts[:, k, :], b2raw[:, :]))
                if k < 2:
                    link(dve.tensor_tensor(b2raw[:, :], b2raw[:, :], b2parts[:, k, :], ALU.subtract))
            dve.nop().then_inc(b2_ready, 1)

            def sort_build(c, h, jj, s, S, rest):
                dve.wait_ge(sort_mm, c + 1)
                p_ = [pay_slot[:, h, jj, k:k + 1] for k in range(PAY)]
                dve.tensor_scalar(lo_hot[:, s, :], iota_h[:, 0:P], p_[0], None, ALU.is_equal).then_inc(hot_built, 1)
                if rest:
                    dve.tensor_scalar(lo_rest[:, s, :], iota_h[:, 0:P], p_[0], p_[4], ALU.is_equal, ALU.mult)
                dve.tensor_scalar(hi16[:, s, 0:S], iota_h[:, 0:S], p_[1], None, ALU.is_equal).then_inc(sort_built, 1)

            def records(c):
                S = SLOTS[c]
                dve.wait_ge(sort_mm, SR + sum(COLS[:c + 1]))
                odd = e_pos[:, 0:S]
                twice = e_pos[:, 256:256 + S]
                link(dve.tensor_scalar(odd, bank[1][:, 0:S], float(P), None, ALU.is_ge))
                link(dve.scalar_tensor_tensor(out=twice, in0=bank[0][:, 0:S], scalar=2.0, in1=odd, op0=ALU.mult, op1=ALU.add))
                link(dve.tensor_scalar(rec_i[c], twice, -2.0, 0.0, ALU.add, ALU.max))
                link(dve.scalar_tensor_tensor(out=rec_f[c][:, :, 0], in0=odd, scalar=-float(P), in1=bank[1][:, 0:S],
                                              op0=ALU.mult, op1=ALU.add))
                link(dve.tensor_copy(odd, bank[4][:, 0:S]))
                link(dve.tensor_tensor(odd, odd, bank[3][:, 0:S], ALU.add))
                link(dve.tensor_tensor(rec_f[c][:, :, 1], odd, bank[2][:, 0:S], ALU.add))
                if c:
                    link(dve.memset(x1[:, NT - 1, :], 0.0))
                dve.nop().then_inc(recs_taken, 1)

            with dve.Fori(0, C0 // U) as i:
                for j in range(U):
                    if j % HALF == 0:
                        dve.wait_ge(pay_ready, 2 * i + j // HALF + 1)
                    sort_build(U * i + j, j // HALF, j % HALF, j % SR, S0, True)
            dve.wait_ge(pay_ready, C0 // HALF + 1)
            for j in range(HALF):
                sort_build(C0 + j, 0, j, j, S1, False)
            records(0)
            dve.wait_ge(acc_set, NT)

            def sw_build(g, j):
                dve.wait_ge(agg_mm, g + 5)
                r = rec_slot[:, j // HALF, j % HALF, :]
                dve.tensor_scalar(Sw[:, j % 4, :], iota_f[:, 0:P], r[:, 0:1], r[:, 1:2], ALU.is_equal, ALU.mult).then_inc(sw_built, 1)

            def blocks_of(c, group):
                word = dve.value_load(blk_tab[c][0:1, bass.ds(group, 1)], min_val=0, max_val=NB ** HALF - 1)
                return [(word // NB ** k) % NB for k in range(HALF)]

            def agg_add(g, b, j):
                dve.wait_ge(agg_mm, U + g + 1)
                dve.wait_ge(agg_added, 2 + g)
                a = RA[:, bass.ds(b * D, D)]
                dve.tensor_tensor(a, a, bank[5 + j % 2][:, 0:D], ALU.add).then_inc(agg_added, 1)

            def agg_steps(i, before, c, sorting, last):
                for j in range(U):
                    if j % HALF == 0:
                        blk = blocks_of(c, 2 * i + j // HALF)
                        if sorting and not (last and j):
                            dve.wait_ge(pay_ready, C0 // HALF + 2 * i + j // HALF + 2)
                        if not (last and j):
                            dve.wait_ge(rec_ready, before // HALF + 2 * i + j // HALF + 2)
                    if sorting and not (last and j >= HALF):
                        ahead = (j + HALF) % U
                        sort_build(C0 + U * i + j + HALF, ahead // HALF, ahead % HALF, ahead, S1, False)
                    agg_add(before + U * i + j, blk[j % HALF], j)
                    if not (last and j >= HALF):
                        sw_build(before + U * i + j + HALF, (j + HALF) % U)

            def first_built(before):
                dve.wait_ge(rec_ready, before // HALF + 1)
                for j in range(HALF):
                    sw_build(before + j, j)

            first_built(0)
            with dve.Fori(0, C1 // U - 1) as i:
                agg_steps(i, 0, 0, True, False)
            agg_steps(C1 // U - 1, 0, 0, True, True)
            records(1)

            def w1_low(m):
                dve.wait_ge(w_hi, m + 1)
                at = (m // 2) * WE + (m % 2) * H
                dve.scalar_tensor_tensor(out=Wall[:, bass.ds(at + KC * H, H)],
                                         in0=stage[:, bass.ds((m % 2) * H, H)], scalar=biasT[:, bass.ds(64 + m, 1)],
                                         in1=Wall[:, bass.ds(at, H)], op0=ALU.mult, op1=ALU.subtract).then_inc(w_done, 1)
                dve.wait_ge(b1_mm, 2 + m + 1)
                dve.tensor_tensor(b1T[:, bass.ds(m * (HC // 2), HC // 2)], biasT[:, bass.ds(m * (HC // 2), HC // 2)],
                                  bank[7][:, 0:HC // 2], ALU.add).then_inc(b1_free, 1)

            def w2_low(m):
                dve.wait_ge(w_hi, 2 * NE + m + 1)
                at = W2BASE + (m // 2) * WE + (m % 2) * H
                dve.scalar_tensor_tensor(out=Wall[:, bass.ds(at + 2 * H, H)], in0=stage[:, bass.ds((m % 2) * H, H)],
                                         scalar=WSCALE, in1=Wall[:, bass.ds(at, H)],
                                         op0=ALU.mult, op1=ALU.subtract).then_inc(w_done, 1)

            dve.wait_ge(bias_mm, 2)
            link(dve.tensor_scalar(biasT[:, 64:80], biasT[:, 64:80], WSCALE, None, ALU.mult))
            dve.nop().then_inc(g_scaled, 1)

            def agg_loop(it0, n, work, shift):
                with dve.Fori(it0, it0 + n) as i:
                    agg_steps(i, S0, 1, False, False)
                    if work:
                        work(i - shift)

            first_built(S0)
            agg_loop(0, 2 * NE, w1_low, 0)
            agg_loop(2 * NE, 2 * PREP2, w2_low, 2 * NE)
            if S1 // U - 1 > 2 * (NE + PREP2):
                agg_loop(2 * (NE + PREP2), S1 // U - 1 - 2 * (NE + PREP2), None, 0)
            agg_steps(S1 // U - 1, S0, 1, False, True)

            dve.wait_ge(mlp_in, 80)
            nstat = NT

            def row_stats(rows, t):
                dve.bn_stats(stats[:, t, :], rows[:, t, :]).then_inc(stats_done, 1)

            for n in range(NT + G + 1):
                u = n - G
                if n > 0 and n % G == 0:
                    g = n // G - 1
                    coefficients(2 + g, G * max(g - 1, 0), min(G * (g + 1), NT))
                    if g:
                        dve.nop().then_inc(xn_coef, 1)
                if 0 <= u < NT:
                    dve.scalar_tensor_tensor(out=h2[:, u, :], in0=h2[:, u, :], scalar=mean1[:, u:u + 1], in1=gsc_bc,
                                             op0=ALU.subtract, op1=ALU.mult).then_inc(centred, 1)
                if 0 <= u < NT:
                    dve.wait_ge(centred, u + 1)
                    dve.wait_ge(x_shift, u // G + 1)
                    dve.scalar_tensor_tensor(out=x1[:, u, :], in0=h2[:, u, :], scalar=rstd[:, u:u + 1], in1=x1[:, u, :],
                                             op0=ALU.mult, op1=ALU.add).then_inc(x1_done, 1)
                    dve.wait_ge(x1_done, u + 1)
                    row_stats(x1, u)
                    nstat += 1
                if n < NT:
                    dve.wait_ge(h2_relu, n + 1)
                    row_stats(h2, n)
                    nstat += 1
                if n % G == G - 1:
                    g = n // G
                    dve.wait_ge(stats_done, nstat)
                    moments(G * max(g - 1, 0), min(G * (g + 1), NT))
                    if g < NT // G:
                        w = slice(G * g, G * (g + 1))
                        link(dve.tensor_scalar(mean1[:, w], lnt[:, 0, w], 0.5, None, ALU.mult))
                        link(dve.tensor_scalar(lnt[:, 2, w], lnt[:, 2, w], GNN_EPS, None, ALU.add))
                    if g:
                        w = slice(G * (g - 1), G * g)
                        v_, u_ = lnt[:, 2, w], lnt[:, 3, w]
                        link(dve.tensor_scalar(u_, v_, LN_EPS, None, ALU.add))
                        link(dve.scalar_tensor_tensor(out=v_, in0=u_, scalar=LN_EPS, in1=v_, op0=ALU.mult, op1=ALU.add))
                        link(dve.reciprocal(u_, u_))
                        link(dve.tensor_tensor(u_, u_, v_, ALU.mult))
                    dve.nop().then_inc(var_ready, 1)
            dve.nop().then_inc(var_ready, 1)
            dve.wait_ge(root_done, 3 + NT // G)
            refine(lnt[:, 1, :], lnt[:, 3, :], lnt[:, 2, :])
            link(dve.tensor_tensor(lnt[:, 1, :], lnt[:, 1, :], lnt[:, 3, :], ALU.mult))

            dve.wait_ge(lg_mm, NT)
            bc_e = lambda a: a.rearrange("p (t a) -> p t a", a=1).to_broadcast([P, NT, NE])
            e_row = iota_f[:, 0:NE].rearrange("p (a e) -> p a e", a=1).to_broadcast([P, NT, NE])
            oh = r_oh.rearrange("p (b t) -> p b t", b=NE)
            link(dve.tensor_tensor(lg, bank[7][:, 0:NT * NE].rearrange("p (t e) -> p t e", e=NE), bc_e(lnt[:, 1, :]), ALU.mult))
            link(dve.tensor_tensor(lg, lg, br_bc[:, :].rearrange("p (a e) -> p a e", a=1).to_broadcast([P, NT, NE]), ALU.add))
            link(dve.tensor_scalar(r_ok, tile_at[:, 0:NT], part_i[:, 0:1], float(N), ALU.add, ALU.is_lt))
            for k in range(KTOP):
                link(dve.tensor_reduce(topv[:, k, :], lg, AX_X, ALU.max))
                link(dve.tensor_tensor(eq, lg, bc_e(topv[:, k, :]), ALU.is_lt))
                link(dve.scalar_tensor_tensor(out=cand, in0=eq, scalar=float(NE), in1=e_row, op0=ALU.mult, op1=ALU.add))
                link(dve.tensor_reduce(topi[:, k, :], cand, AX_X, ALU.min))
                link(dve.tensor_tensor(eq, e_row, bc_e(topi[:, k, :]), ALU.is_equal))
                if k == 0:
                    link(dve.scalar_tensor_tensor(out=lg, in0=eq, scalar=-3.0e38, in1=lg, op0=ALU.mult, op1=ALU.add))
                link(dve.tensor_tensor(oh[:, :, k * NT:(k + 1) * NT].rearrange("p b t -> p t b"), eq, bc_e(r_ok), ALU.mult))
            link(dve.tensor_tensor(r_e, topv[:, 1, :], topv[:, 0, :], ALU.subtract))
            dve.nop().then_inc(top_ready, 1)
            place(3, NE, RC, oh, r_cum.rearrange("p (b t) -> p b t", b=NE), r_pos.rearrange("p (b t) -> p b t", b=NE),
                  FT, pos_f, exp_tab[:, :])
            link(dve.tensor_copy(pos_n, pos_f))
            link(dve.tensor_scalar(pos_n, pos_n, P - 1, None, ALU.bitwise_and))
            link(dve.tensor_copy(pos_lo, pos_n))
            dve.nop().then_inc(pos_ready, 1)
            link(dve.tensor_tensor(pos_hi, pos_f, pos_lo, ALU.subtract))
            link(dve.tensor_scalar(pos_hi, pos_hi, 1.0 / P, None, ALU.mult))
            dve.wait_ge(exp_done, 1)
            link(dve.tensor_scalar(gate[:, 0, :], gate[:, 1, :], 1.0, None, ALU.add))
            link(dve.reciprocal(gate[:, 0, :], gate[:, 0, :]))
            link(dve.tensor_tensor(gate[:, 1, :], gate[:, 1, :], gate[:, 0, :], ALU.mult))
            link(dve.tensor_scalar(r_e, tile_at[:, 0:NT], part_i[:, 0:1], 1.0, ALU.add, ALU.add))
            for k in range(KTOP):
                link(dve.tensor_tensor(node_no[:, k * NT:(k + 1) * NT], r_e, r_ok, ALU.mult))
                link(dve.tensor_tensor(gate[:, k, :], gate[:, k, :], r_ok, ALU.mult))
            dve.wait_ge(rows_stored, STORES)
            gates = gate[:, :, :].rearrange("p k t -> p (k t)")
            for c in range(RC // SCH):
                col = slice(c * SCH, (c + 1) * SCH)
                per = lambda a: a[:, col].rearrange("p (c a) -> p c a", a=1).to_broadcast([P, SCH, FT])
                node_hot, gate_hot = slot_hi[:, col, 0, :], slot_hi[:, col, 1, :]
                link(dve.tensor_tensor(node_hot, iota_f[:, 0:FT].rearrange("p (a n) -> p a n", a=1).to_broadcast([P, SCH, FT]),
                                       per(pos_hi), ALU.is_equal))
                link(dve.tensor_tensor(gate_hot, node_hot, per(gates), ALU.mult))
                link(dve.tensor_tensor(node_hot, node_hot, per(node_no), ALU.mult))
                dve.nop().then_inc(slot_hi_built, 1)
            with dve.Fori(2 * PREP2, 2 * NE) as m:
                w2_low(m)
            dve.wait_ge(slots_mm, 1)
            link(dve.tensor_scalar(slot_gate[:, :], bank[0][:, 0:FT], 0.5, spare[:, 0:1], ALU.is_lt, ALU.mult))
            link(dve.scalar_tensor_tensor(out=slot_tok[:, :], in0=bank[0][:, 0:FT], scalar=-1.0, in1=slot_gate[:, :],
                                          op0=ALU.add, op1=ALU.add))
            link(dve.tensor_scalar(slot_gate[:, :], bank[0][:, FT:2 * FT], 1.0 / WSCALE, None, ALU.mult))
            dve.nop().then_inc(slots_ready, 1)

            def x_low(t, q):
                dve.wait_ge(fx_hi, t + 1)
                dve.wait_ge(up_mm, 2 * t + 2)
                dve.tensor_tensor(xlo[q], bank[6 + q][:, 0:D], xhi[q], ALU.subtract).then_inc(fx_split, 1)

            def h_parts(t, q):
                dve.wait_ge(gelu_done, 4 + 2 * t + 2)
                dve.wait_ge(down_mm, t + 1)
                dve.tensor_copy(hhi[q], h32[q]).then_inc(hhi_done, 1)
                dve.wait_ge(hhi_done, t + 1)
                dve.tensor_tensor(hlo[q], h32[q], hhi[q], ALU.subtract).then_inc(h_split, 1)

            def y_rows(t, q):
                dve.wait_ge(down_mm, 2 + t + 1)
                dve.wait_ge(y_free, t + 1)
                dve.tensor_scalar(ysb[q], bank[4 + q][:, 0:D], slot_gate[:, bass.ds(t, 1)], None, ALU.mult).then_inc(y_out, 1)

            x_low(0, 0)
            x_low(1, 1)
            h_parts(0, 0)
            with dve.Fori(0, FT // 2 - 1) as i:
                for q in range(2):
                    x_low(2 * i + q + 2, q)
                    h_parts(2 * i + q + 1, 1 - q)
                    y_rows(2 * i + q, q)
            h_parts(FT - 1, 1)
            y_rows(FT - 2, 0)
            y_rows(FT - 1, 1)


_OUT = ((3125, 256), "float32")


def kernel(**inputs):
    import concourse.bacc as _bacc
    from concourse.bass_utils import run_bass_kernel_spmd as _run

    nc = _bacc.Bacc("TRN2", target_bir_lowering=False, num_devices=1,
                    dynamic_dma_scratch_size=20480)
    arrays, args = {}, []
    for name, a in inputs.items():
        a = np.ascontiguousarray(a)
        arrays[f"in_{name}"] = a
        args.append(nc.dram_tensor(f"in_{name}", a.shape, mybir.dt.from_np(a.dtype), kind="ExternalInput").ap())
    out = nc.dram_tensor("out_dram", _OUT[0], F32, kind="ExternalOutput").ap()
    moe_gnn_program(nc, *args, out)
    r = _run(nc, [arrays], core_ids=[0])
    return r.results[0]["out_dram"]
```

```python
from contextlib import ExitStack

import numpy as np

import concourse.bass as bass
from concourse import mybir

ALU = mybir.AluOpType
ACT = mybir.ActivationFunctionType
AX_X = mybir.AxisListType.X
F32 = mybir.dt.float32
F16 = mybir.dt.float16
BF16 = mybir.dt.bfloat16
I32 = mybir.dt.int32
U32 = mybir.dt.uint32

P = 128


def moe_gnn_program(nc, x, src, dst, edge_weight, gW1, gb1, gW2, gb2, geps, goffset, gscale,
                    Wr, br, ln_g, ln_b, W1, b1, W2, b2, out):
    N, D = x.shape
    E = src.shape[0]
    NE, _, H = W1.shape
    KC, HC = D // P, H // P
    NT = (N + P - 1) // P
    LAST = N - (NT - 1) * P
    NB = NT
    U = 8
    HALF = U // 2

    EC_FULL = (E + P - 1) // P
    EC = (EC_FULL + U - 1) // U * U
    extra = NB - 1
    C0 = (EC - extra) // 2 // U * U
    S0 = (C0 + extra + U - 1) // U * U
    C1 = EC - C0
    S1 = (C1 + extra + U - 1) // U * U
    assert C1 == S0 and S1 <= 256
    COLS, SLOTS, CSTART = (C0, C1), (S0, S1), (0, C0)
    CMAX, SMAX = max(COLS), max(SLOTS)

    KTOP = 2
    LN_EPS, GNN_EPS = 1e-5, 1e-10
    RC = KTOP * NT
    FT = (N * KTOP + NE * (P - 1)) // P
    XR = 4
    FT += -FT % XR
    WSCALE = 32.0
    WE = 2 * KC * H
    assert WE == 2 * HC * D
    PREP2 = (S1 // U - 1 - 2 * NE) // 2
    G = 5
    assert NT % G == 0 and 0 < PREP2 < NE

    xl_d = nc.dram_tensor("xl_d", (N, D), F32, kind="Internal").ap()
    xn_d = nc.dram_tensor("xn_d", (N + P, D), F32, kind="Internal").ap()
    sum_d = nc.dram_tensor("sum_d", (N + P, D), F32, kind="Internal").ap()
    biasrow_d = nc.dram_tensor("biasrow_d", (3, (NE + 1) * D), BF16, kind="Internal").ap()

    with ExitStack() as ctx:
        def sb(name, shape, dt):
            return ctx.enter_context(nc.sbuf_tensor(name, shape, dt))

        def sem(name):
            return ctx.enter_context(nc.semaphore(name))

        bank = [ctx.enter_context(nc.psum_tensor(f"bank{i}", [P, 512], F32)) for i in range(8)]

        Wall = sb("Wall", [P, 2 * NE * WE], F16)
        RA = sb("RA", [P, NT * D], F32)
        RB = sb("RB", [P, NT * D], F32)
        gbuf = sb("gbuf", [P, U, D], F32)
        stage = sb("stage", [P, KC * H], F32)
        W2BASE = NE * WE

        def f32view(t, at, n):
            return t[:, 2 * at:2 * (at + n)].bitcast(F32)

        w2f = W2BASE // 2
        x_in = f32view(Wall, w2f, NT * D).rearrange("p (t d) -> p t d", d=D)
        xl = f32view(Wall, w2f + NT * D, NT * D).rearrange("p (t d) -> p t d", d=D)
        acc = RA[:, :].rearrange("p (t d) -> p t d", d=D)
        h2, xn = acc, acc
        x1 = RB[:, :].rearrange("p (t d) -> p t d", d=D)
        NBC = NB * CMAX
        e_oh = Wall[:, 0:NBC]
        e_cum = Wall[:, NBC:2 * NBC]
        e_pos = Wall[:, 2 * NBC:4 * NBC].bitcast(F32)
        e_oh1 = Wall[:, 4 * NBC:5 * NBC]
        PAY = 5
        epay = RB[:, 0:EC * PAY].rearrange("p (c k) -> p c k", k=PAY)
        e16 = RB[:, 0:EC * PAY].bitcast(F16).rearrange("p (c k two) -> p c k two", k=PAY, two=2)
        eb16 = RB[:, 0:EC * PAY].bitcast(BF16).rearrange("p (c k two) -> p c k two", k=PAY, two=2)
        nwords, wwords = e16[:, :, 2, :], eb16[:, :, 3, :]
        at = EC * PAY
        SR = U
        WT_ON_DVE = (3, 7)
        HI_ON_POOL = (0, 2, 4, 6)
        lo_hot = RB[:, at:at + SR * P // 2].bitcast(F16).rearrange("p (s n) -> p s n", s=SR)
        at += SR * P // 2
        lo_node = RB[:, at:at + SR * P].rearrange("p (s n) -> p s n", s=SR)
        at += SR * P
        lo_wt = RB[:, at:at + SR * P].rearrange("p (s n) -> p s n", s=SR)
        at += SR * P
        lo_rest = RB[:, at:at + SR * P // 2].bitcast(BF16).rearrange("p (s n) -> p s n", s=SR)
        at += SR * P // 2
        hi16 = RB[:, at:at + SR * SMAX // 2].bitcast(F16).rearrange("p (s n) -> p s n", s=SR)
        at += SR * SMAX // 2
        assert at <= NT * D
        rec_i, rec_f = [], []
        at = w2f + 2 * NT * D
        for c in range(2):
            rec_i.append(f32view(Wall, at, SLOTS[c]).bitcast(I32))
            at += SLOTS[c]
            rec_f.append(f32view(Wall, at, 2 * SLOTS[c]).rearrange("p (c k) -> p c k", k=2))
            at += 2 * SLOTS[c]
        assert w2f + PREP2 * WE // 2 <= w2f + 2 * NT * D
        gw1 = f32view(Wall, at, KC * D).rearrange("p (c n) -> p c n", c=KC)
        gw2 = f32view(Wall, at + KC * D, KC * D).rearrange("p (c n) -> p c n", c=KC)
        at += 2 * KC * D
        gb2_rows = f32view(Wall, at, D // 2).bitcast(BF16)[0:3, :]
        gsc_bc, gof_bc = (f32view(Wall, at + k * D, D) for k in range(1, 3))
        assert at + 3 * D <= NE * WE
        xs = [RA[:, q * D:(q + 1) * D] for q in range(XR)]
        at = XR * D
        xhi, xlo, hhi, hlo, h32, ysb = [], [], [], [], [], []
        for q in range(2):
            for lst, n in ((xhi, D // 2), (xlo, D // 2), (hhi, H // 2), (hlo, H // 2)):
                lst.append(RA[:, at:at + n].bitcast(F16))
                at += n
            h32.append(RA[:, at:at + H])
            at += H
            ysb.append(RA[:, at:at + D])
            at += D
        assert at <= NT * D
        aggT, h1T, xT = ([stage[:, (2 * k + q) * D:(2 * k + q + 1) * D] for q in range(2)] for k in range(3))

        ident = sb("ident", [P, P], F32)
        ones = sb("ones", [P, P], F32)
        above = sb("above", [P, P], F32)
        upto = sb("upto", [32, 32], F32)
        iota_i = RA[:, 0:256].bitcast(I32)
        iota_f = sb("iota_f", [P, P], F32)
        iota_h = sb("iota_h", [P, 256], F16)
        tile_at = sb("tile_at", [P, NT], F32)
        part_i = sb("part_i", [P, 1], F32)
        zero_h = sb("zero_h", [P, 256], F16)
        one_h = sb("one_h", [P, 1], F16)
        one_b = sb("one_b", [3, P], BF16)
        Sw = sb("Sw", [P, 4, P], F32)
        pay_slot = sb("pay_slot", [P, 2, HALF, PAY], F32)
        idx_slot = sb("idx_slot", [P, U], I32)
        rec_slot = sb("rec_slot", [P, 2, HALF, 2], F32)
        blk_tab = [sb(f"blk_tab{c}", [1, SLOTS[c] // HALF], I32) for c in range(2)]
        exp_tab = sb("exp_tab", [1, FT // XR], I32)
        exp_row = sb("exp_row", [1, FT + XR + FT // XR], F32)
        biasT = sb("biasT", [P, P], F32)
        b1T = sb("b1T", [P, NE * HC], F32)
        BC = (NE + 1) * D // P
        b2raw = sb("b2raw", [P, BC], F32)
        b2parts = sb("b2parts", [P, 3, BC], BF16)
        b2rows = gbuf[0:3, U // 2:, :].rearrange("p a d -> p (a d)").bitcast(BF16)
        spare = sb("spare", [P, 1], F32)
        slot_tok = sb("slot_tok", [P, FT], I32)
        slot_gate = sb("slot_gate", [P, FT], F32)
        eps1 = sb("eps1", [P, 1], F32)
        Wr_sb = sb("Wr_sb", [P, KC, NE], F32)
        br_bc = sb("br_bc", [P, NE], F32)
        lnt = sb("lnt", [P, 4, NT], F32)
        rstd = sb("rstd", [P, NT], F32)
        nmr = sb("nmr", [P, NT], F32)
        mean1 = sb("mean1", [P, NT], F32)
        warm = sb("warm", [P, 1], F32)
        ends = sb("ends", [P, 1], F32)
        small = Sw[:, :, :].rearrange("p s n -> p (s n)")
        stats = small[:, 0:NT * 6].rearrange("p (t s) -> p t s", s=6)
        at = NT * 6
        cnt, cprev, first = (small[:, at + 32 * k:at + 32 * (k + 1)] for k in range(3))
        at += 96
        room_i, room_f = small[:, at:at + 33].bitcast(I32), small[:, at + 34:at + 67]
        at += 68
        past = small[0:32, at:at + P].bitcast(F16)
        blk_row = stage[0:1, 1600:1600 + SMAX]
        assert at + P <= 4 * P
        gate = sb("gate", [P, 2, NT], F32)
        rows_in = stage[:, 0:P]

        ei = [stage[:, (k + 1) * 400:(k + 1) * 400 + EC].bitcast(I32) for k in range(3)]
        e_src, e_dst, e_tmp = ei
        ew = gbuf[:, 0:2, :].rearrange("p a d -> p (a d)")[:, 0:EC]
        blk_h = gbuf[:, 2:4, :].rearrange("p a d -> p (a d)")[:, 0:EC // 2].bitcast(F16)
        pos_i = gbuf[:, 6:8, :].rearrange("p a d -> p (a d)")[:, 0:CMAX].bitcast(I32)
        pos_j = gbuf[:, 6:8, :].rearrange("p a d -> p (a d)")[:, CMAX:2 * CMAX].bitcast(I32)
        rt = gbuf[:, :, :].rearrange("p a d -> p (a d)")
        def rslice(k, n):
            return rt[:, 200 * k:200 * k + n]
        lg = rslice(0, NT * NE).rearrange("p (t e) -> p t e", e=NE)
        eq = rslice(1, NT * NE).rearrange("p (t e) -> p t e", e=NE)
        cand = rslice(2, NT * NE).rearrange("p (t e) -> p t e", e=NE)
        topv = rslice(3, 2 * NT).rearrange("p (k t) -> p k t", k=2)
        topi = rslice(4, 2 * NT).rearrange("p (k t) -> p k t", k=2)
        r_ok = rslice(5, NT)
        r_e = rslice(6, NT)
        r_oh = rt[:, 1400:1400 + NE * RC // 2].bitcast(F16)
        r_cum = rt[:, 1600:1600 + NE * RC // 2].bitcast(F16)
        r_pos = rt[:, 0:NE * RC]
        pos_f = rslice(2, RC)
        pos_hi, pos_lo, node_no = (rt[:, 450 + 50 * k:450 + 50 * k + RC] for k in range(3))
        pos_n = rslice(3, RC).bitcast(I32)
        slot_lo = RB[:, :].rearrange("p (c n) -> p c n", n=P)
        slot_hi = RA[:, 0:RC * 2 * FT].rearrange("p (c k n) -> p c k n", k=2, n=FT)
        SCH = RC // 5

        edges_in = sem("edges_in")
        x_loaded = sem("x_loaded")
        sums_done = sem("sums_done")
        stats_done = sem("stats_done")
        var_ready = sem("var_ready")
        root_done = sem("root_done")
        x1_done = sem("x1_done")
        hhi_done = sem("hhi_done")
        g_scaled = sem("g_scaled")
        small_in = sem("small_in")
        const_done = sem("const_done")
        dve_step = sem("dve_step")
        act_step = sem("act_step")
        pool_step = sem("pool_step")
        xl_scaled = sem("xl_scaled")
        xl_done = sem("xl_done")
        eps_ready = sem("eps_ready")
        acc_set = sem("acc_set")
        xl_stored = sem("xl_stored")
        spare_zeroed = sem("spare_zeroed")
        counts_ready = sem("counts_ready")
        counts_mm = sem("counts_mm")
        ends_mm = sem("ends_mm")
        room_ready = sem("room_ready")
        past_ready = sem("past_ready")
        table_mm = sem("table_mm")
        bias_mm = sem("bias_mm")
        payload_set = sem("payload_set")
        blocks_ready = sem("blocks_ready")
        blocks_hot = sem("blocks_hot")
        pay_ready = sem("pay_ready")
        hot_built = sem("hot_built")
        words_built = sem("words_built")
        sort_built = sem("sort_built")
        hi_built = sem("hi_built")
        sort_mm = sem("sort_mm")
        recs_taken = sem("recs_taken")
        idx_ready = sem("idx_ready")
        rec_ready = sem("rec_ready")
        gathered = [sem(f"gathered{j}") for j in range(U)]
        slot_claimed = sem("slot_claimed")
        sw_built = sem("sw_built")
        agg_mm = sem("agg_mm")
        agg_added = sem("agg_added")
        staged = sem("staged")
        w_hi = sem("w_hi")
        w_done = sem("w_done")
        b1_mm = sem("b1_mm")
        mlp_in = sem("mlp_in")
        t_mm = sem("t_mm")
        t_out = sem("t_out")
        h1_mm = sem("h1_mm")
        h1_out = sem("h1_out")
        h2_mm = sem("h2_mm")
        h2_relu = sem("h2_relu")
        x_again = sem("x_again")
        x_shift = sem("x_shift")
        centred = sem("centred")
        xn_coef = sem("xn_coef")
        norm_out = sem("norm_out")
        r_mm = sem("r_mm")
        r_out = sem("r_out")
        lg_mm = sem("lg_mm")
        top_ready = sem("top_ready")
        exp_done = sem("exp_done")
        pos_ready = sem("pos_ready")
        rows_stored = sem("rows_stored")
        slot_lo_built = sem("slot_lo_built")
        slot_hi_built = sem("slot_hi_built")
        slot_gate_built = sem("slot_gate_built")
        slots_mm = sem("slots_mm")
        slots_ready = sem("slots_ready")
        b2_in = sem("b2_in")
        b2_ready = sem("b2_ready")
        xs_in = [sem(f"xs_in{q}") for q in range(XR)]
        ft_mm = sem("ft_mm")
        fx_hi = sem("fx_hi")
        fx_split = sem("fx_split")
        up_mm = sem("up_mm")
        gelu_done = sem("gelu_done")
        h_split = sem("h_split")
        down_mm = sem("down_mm")
        y_out = sem("y_out")
        y_free = sem("y_free")
        y_added = [sem(f"y_added{q}") for q in range(2)]
        out_done = sem("out_done")

        block = ctx.enter_context(nc.Block())
        FULL = (NT - 1) * P
        STORES = 16 * 2 * (NT // G + 1)

        @block.sync
        def _(sp):
            pcols = EC_FULL
            rows = E // pcols
            rest = E - rows * pcols
            sp.wait_ge(const_done, 1)
            for a, t in ((src, e_src), (dst, e_dst), (edge_weight, ew)):
                sp.dma_start(t[0:rows, 0:pcols], a[0:rows * pcols].rearrange("(p c) -> p c", c=pcols)
                             ).then_inc(edges_in, 16)
                sp.dma_start(t[rows:rows + 1, 0:rest], a[rows * pcols:E].rearrange("(p c) -> p c", p=1)
                             ).then_inc(edges_in, 16)
            sp.wait_ge(const_done, 2)
            sp.dma_start(x_in[:, 0:NT - 1, :], x[0:FULL, :].rearrange("(t p) d -> p t d", p=P)).then_inc(x_loaded, 16)
            sp.dma_start(x_in[0:LAST, NT - 1, :], x[FULL:N, :]).then_inc(x_loaded, 16)
            sp.wait_ge(const_done, 3)
            sp.dma_start(rows_in[0:64, :], b1.rearrange("e (c p) -> (e c) p", p=P)).then_inc(small_in, 16)
            sp.dma_start(rows_in[64:80, :], ln_g.rearrange("e (c p) -> (e c) p", p=P)).then_inc(small_in, 16)
            sp.dma_start(rows_in[80:96, :], ln_b.rearrange("e (c p) -> (e c) p", p=P)).then_inc(small_in, 16)
            sp.dma_start(rows_in[96:98, :], gb1.rearrange("(c p) -> c p", p=P)).then_inc(small_in, 16)
            sp.dma_start(eps1[:, :], geps.partition_broadcast(P)).then_inc(small_in, 16)
            sp.dma_start(Wr_sb[:, :, :], Wr.rearrange("(c p) e -> p c e", p=P)).then_inc(small_in, 16)
            sp.dma_start(br_bc[:, :], br.partition_broadcast(P)).then_inc(small_in, 16)
            sp.dma_start(gw1, gW1.rearrange("(c p) n -> p c n", p=P)).then_inc(mlp_in, 16)
            sp.dma_start(gw2, gW2.rearrange("(c p) n -> p c n", p=P)).then_inc(mlp_in, 16)
            sp.dma_start(b2raw[:, 0:BC - KC], b2.rearrange("e d -> (e d)").rearrange("(p c) -> p c", p=P)).then_inc(b2_in, 16)
            sp.dma_start(b2raw[:, BC - KC:BC], gb2.rearrange("(p c) -> p c", p=P)).then_inc(b2_in, 16)
            sp.dma_start(gsc_bc, gscale.partition_broadcast(P)).then_inc(mlp_in, 16)
            sp.dma_start(gof_bc, goffset.partition_broadcast(P)).then_inc(mlp_in, 16)
            sp.wait_ge(xl_done, NT)
            sp.dma_start(xl_d[0:FULL, :].rearrange("(t p) d -> p t d", p=P), xl[:, 0:NT - 1, :]).then_inc(xl_stored, 16)
            sp.dma_start(xl_d[FULL:N, :], xl[0:LAST, NT - 1, :]).then_inc(xl_stored, 16)
            zrow = zero_h[:, :].bitcast(F32)
            for rows in (xn_d, sum_d):
                for h in range(KC):
                    sp.dma_start(rows[N:N + P, h * P:(h + 1) * P], zrow).then_inc(spare_zeroed, 16)
            sp.wait_ge(b2_ready, 1)
            sp.dma_start(biasrow_d[:, 0:NE * D].rearrange("k (p c) -> p k c", p=P), b2parts[:, :, 0:BC - KC]).then_inc(b2_in, 16)
            sp.dma_start(biasrow_d[:, NE * D:].rearrange("k (p c) -> p k c", p=P), b2parts[:, :, BC - KC:BC]).then_inc(b2_in, 16)
            sp.wait_ge(b2_in, 64)
            sp.dma_start(gb2_rows, biasrow_d[:, NE * D:]).then_inc(mlp_in, 16)
            sp.wait_ge(recs_taken, 1)
            sp.wait_ge(bias_mm, 2)
            w1_v = W1.rearrange("e (c p) h -> p e c h", p=P)
            w2_v = W2.rearrange("e (c p) d -> p e c d", p=P)
            with sp.Fori(0, PREP2) as e:
                sp.wait_ge(w_done, 4 * e + 2)
                sp.dma_start(stage[:, :].rearrange("p (a c h) -> p a c h", a=1, c=KC),
                             w1_v[:, bass.ds(e, 1), :, :]).then_inc(staged, 16)
                sp.wait_ge(w_done, 4 * e + 4)
                sp.dma_start(stage[:, :].rearrange("p (a c d) -> p a c d", a=1, c=HC),
                             w2_v[:, bass.ds(e, 1), :, :]).then_inc(staged, 16)
            with sp.Fori(PREP2, NE) as e:
                sp.wait_ge(w_done, 2 * e + 2 * PREP2 + 2)
                sp.dma_start(stage[:, :].rearrange("p (a c h) -> p a c h", a=1, c=KC),
                             w1_v[:, bass.ds(e, 1), :, :]).then_inc(staged, 16)
            sp.wait_ge(recs_taken, 2)
            sp.dma_start(x1[:, 0:NT - 1, :], x[0:FULL, :].rearrange("(t p) d -> p t d", p=P)).then_inc(x_again, 16)
            sp.dma_start(x1[0:LAST, NT - 1, :], x[FULL:N, :]).then_inc(x_again, 16)
            for g in range(NT // G):
                for rows, dst_d, ready in ((x1, sum_d, x1_done), (xn, xn_d, norm_out)):
                    sp.wait_ge(ready, G * (g + 1))
                    last = g == NT // G - 1
                    full = G - 1 if last else G
                    at = g * G * P
                    sp.dma_start(dst_d[at:at + full * P, :].rearrange("(t p) d -> p t d", p=P),
                                 rows[:, G * g:G * g + full, :]).then_inc(rows_stored, 16)
                    if last:
                        sp.dma_start(dst_d[FULL:N, :], rows[0:LAST, NT - 1, :]).then_inc(rows_stored, 16)
            sp.wait_ge(lg_mm, NT)
            with sp.Fori(0, NE - PREP2) as e:
                sp.wait_ge(w_done, 2 + 2 * NE + 2 * PREP2 + 2 * e)
                sp.dma_start(stage[:, :].rearrange("p (a c d) -> p a c d", a=1, c=HC),
                             w2_v[:, bass.ds(e + PREP2, 1), :, :]).then_inc(staged, 16)
            sp.wait_ge(slot_hi_built, RC // SCH)
            sp.dma_start(b2rows, biasrow_d[:, 0:NE * D]).then_inc(b2_in, 16)
            for q in range(2):
                sp.wait_ge(y_added[q], 16 * (FT // 2))
            sp.dma_start(out, sum_d[0:N, :]).then_inc(out_done, 16)
            sp.wait_ge(out_done, 16)

        @block.gpsimd
        def _(pool):
            steps = [0]

            def link(ins):
                steps[0] += 1
                ins.then_inc(pool_step, 1)
                pool.wait_ge(pool_step, steps[0])

            pool.memset(e_src, NB * P)
            pool.memset(e_dst, -2)
            link(pool.memset(ew, 0.0))
            pool.nop().then_inc(const_done, 1)
            link(pool.memset(x_in[:, NT - 1, :], 0.0))
            pool.nop().then_inc(const_done, 1)
            link(pool.iota(iota_i[:, 0:1], [[1, 1]], base=0, channel_multiplier=1))
            link(pool.tensor_copy(part_i[:, :], iota_i[:, 0:1]))
            link(pool.iota(iota_i[:, :], [[1, 256]], base=0, channel_multiplier=0))
            pool.tensor_copy(iota_f[:, :], iota_i[:, 0:P])
            pool.tensor_copy(iota_h[:, :], iota_i[:, :])
            pool.tensor_scalar(tile_at[:, :], iota_i[:, 0:NT], float(P), None, ALU.mult)
            pool.tensor_scalar(spare[:, :], part_i[:, :], float(N + 1), None, ALU.add)
            pool.memset(zero_h[:, :], 0.0)
            pool.memset(one_h[:, :], 1.0)
            pool.memset(one_b[:, :], 1.0)
            pool.memset(ones[:, :], 1.0)
            pool.memset(above[:, :], 1.0)
            pool.memset(upto[:, :], 1.0)
            pool.memset(rows_in, 0.0)
            link(pool.memset(ident[:, :], 0.0))
            pool.affine_select(out=ident[:, :], in_=ident[:, :], compare_op=ALU.not_equal, fill=1.0, base=0,
                               pattern=[[-1, P]], channel_multiplier=1)
            pool.affine_select(out=above[:, :], in_=above[:, :], compare_op=ALU.is_ge, fill=0.0, base=-1,
                               pattern=[[1, P]], channel_multiplier=-1)
            link(pool.affine_select(out=upto[:, :], in_=upto[:, :], compare_op=ALU.is_ge, fill=0.0, base=0,
                                    pattern=[[1, 32]], channel_multiplier=-1))
            pool.nop().then_inc(const_done, 1)

            pool.wait_ge(blocks_ready, 1)
            for b in range(NB):
                m = pool.tensor_scalar(e_oh1[:, b * C1:(b + 1) * C1], blk_h[:, C0:EC], float(b), None, ALU.is_equal)
            m.then_inc(blocks_hot, 1)

            pool.wait_ge(eps_ready, 1)
            for g in range(NT // G):
                pool.wait_ge(xl_done, G * (g + 1))
                rows = slice(G * g, G * (g + 1))
                pool.tensor_scalar(acc[:, rows, :], xl[:, rows, :], eps1[:, 0:1], None, ALU.mult).then_inc(acc_set, 1)

            with pool.Fori(0, C0 // U) as i:
                for j in HI_ON_POOL:
                    if j % HALF == 0:
                        pool.wait_ge(pay_ready, 2 * i + j // HALF + 1)
                    pool.wait_ge(sort_mm, U * i + j + 1)
                    pool.sem_inc(slot_claimed, 1)
                    pool.tensor_scalar(hi16[:, j, 0:S0], iota_h[:, 0:S0], pay_slot[:, j // HALF, j % HALF, 1:2], None,
                                       ALU.is_equal).then_inc(hi_built, 1)

            pool.wait_ge(xl_stored, 32)

            def gathers(tiles, before):
                with pool.Fori(0, tiles // U) as i:
                    for j in range(U):
                        if j % 2 == 0:
                            pool.wait_ge(idx_ready, before // 2 + 4 * i + j // 2 + 1)
                        pool.wait_ge(agg_mm, before + U * i + j + 1)
                        pool.sem_inc(slot_claimed, 1)
                        pool.indirect_dma_start(
                            out=gbuf[:, j, :], out_offset=None, in_=xl_d,
                            in_offset=bass.IndirectOffsetOnAxis(ap=idx_slot[:, j:j + 1].bitcast(U32), axis=0),
                        ).then_inc(gathered[j], 16)

            gathers(S0, 0)
            gathers(S1, S0)

            pool.wait_ge(x_again, 32)
            pool.wait_ge(mlp_in, 80)
            for g in range(NT // G):
                rows = x1[:, G * g:G * (g + 1), :]
                pool.tensor_tensor(rows, rows, gof_bc.rearrange("p (a d) -> p a d", a=1).to_broadcast([P, G, D]),
                                   ALU.add).then_inc(x_shift, 1)
            for t in range(NT):
                pool.wait_ge(xn_coef, t // G + 1)
                pool.tensor_scalar(xn[:, t, :], x1[:, t, :], rstd[:, t:t + 1], nmr[:, t:t + 1],
                                   ALU.mult, ALU.add).then_inc(norm_out, 1)
            pool.wait_ge(pos_ready, 1)
            pool.wait_ge(rows_stored, STORES)
            for c in range(0, RC, 2):
                pool.tensor_scalar(slot_lo[:, c, :], iota_f[:, :], pos_lo[:, c:c + 1], None, ALU.is_equal
                                   ).then_inc(slot_lo_built, 1)
            pool.wait_ge(slots_ready, 1)
            pool.wait_ge(spare_zeroed, 64)

            def node_rows(t):
                return bass.IndirectOffsetOnAxis(ap=slot_tok[:, t:t + 1].bitcast(U32), axis=0)

            def gather(t):
                pool.indirect_dma_start(out=xs[t % XR], out_offset=None, in_=xn_d, in_offset=node_rows(t)
                                        ).then_inc(xs_in[t % XR], 16)

            for t in range(XR):
                gather(t)
            for t in range(FT):
                if t + XR < FT:
                    pool.wait_ge(ft_mm, 2 + t + 1)
                    gather(t + XR)
                pool.wait_ge(y_out, 2 + t + 1)
                if t:
                    pool.wait_ge(y_added[(t - 1) % 2], 16 * ((t - 1) // 2 + 1))
                    pool.sem_inc(y_free, 1)
                pool.indirect_dma_start(out=sum_d, out_offset=node_rows(t), in_=ysb[t % 2], in_offset=None,
                                        compute_op=ALU.add).then_inc(y_added[t % 2], 16)

        @block.tensor
        def _(pe):
            mm = nc.tensor.matmul
            pe.nop().then_inc(sort_mm, SR)
            pe.nop().then_inc(agg_mm, U)
            pe.nop().then_inc(ft_mm, 2)
            pe.nop().then_inc(up_mm, 4)
            pe.nop().then_inc(down_mm, 2)
            pe.wait_ge(const_done, 3)
            misc = bank[7]

            def prefixes(nth, B, S):
                pe.wait_ge(counts_ready, nth)
                mm(misc[:, 0:B], above[:, :], cnt[:, 0:B], start=True, stop=True)
                mm(misc[:, 32:32 + B], ones[:, :], cnt[:, 0:B], start=True, stop=True)
                mm(misc[0:B, 64:65], cnt[:, 0:B], ones[:, 0:1], start=True, stop=True).then_inc(counts_mm, 1)
                pe.wait_ge(room_ready, nth)
                mm(misc[0:B, 96:97], upto[0:B, 0:B], room_f[0:B, 32:33], start=True, stop=True).then_inc(ends_mm, 1)
                pe.wait_ge(past_ready, nth)
                mm(misc[0:1, 128:128 + S], one_h32[0:B, :], past[0:B, 0:S], start=True, stop=True).then_inc(table_mm, 1)

            one_h32 = one_h[0:32, :]

            prefixes(1, NB, S0)
            prefixes(2, NB, S1)
            pe.wait_ge(payload_set, 2)
            pe.wait_ge(small_in, 112)
            nc.tensor.transpose(misc[:, 0:P], rows_in, ident[:, :]).then_inc(bias_mm, 1)

            def clear(S):
                for k in range(5):
                    mm(bank[k][:, 0:S], zero_h[:, 0:P], zero_h[:, 0:S], start=True, stop=False, skip_group_check=True)

            def sort_step(c, S, s, hi=0):
                pe.wait_ge(sort_built, c + 1)
                pe.wait_ge(words_built, c + 1)
                if S == S0 and s in HI_ON_POOL:
                    pe.wait_ge(hi_built, hi + 1)
                node = lo_node[:, s, :].bitcast(F16).rearrange("p (n two) -> p n two", two=2)
                wt = lo_wt[:, s, :].bitcast(BF16).rearrange("p (n two) -> p n two", two=2)
                for k, left in enumerate((node[:, :, 1], node[:, :, 0], wt[:, :, 1], wt[:, :, 0], lo_rest[:, s, :])):
                    m = mm(bank[k][:, 0:S], left, hi16[:, s, 0:S], start=False, stop=False, skip_group_check=True)
                m.then_inc(sort_mm, 1)

            def agg_step(g, gi, j):
                pe.wait_ge(sw_built, g + 1)
                pe.wait_ge(agg_added, g + 1)
                pe.wait_ge(gathered[j], gi)
                mm(bank[5 + j % 2][:, 0:D], Sw[:, j % 4, :], gbuf[:, j, :], start=True, stop=True).then_inc(agg_mm, 1)

            clear(S0)
            with pe.Fori(0, C0 // U) as i:
                for j in range(U):
                    sort_step(U * i + j, S0, j % SR, HALF * i + j // 2)
            pe.wait_ge(recs_taken, 1)
            clear(S1)
            with pe.Fori(0, C1 // U) as i:
                for j in range(U):
                    agg_step(U * i + j, 16 * (i + 1), j)
                    sort_step(C0 + U * i + j, S1, j % SR)

            def eight(i):
                for j in range(U):
                    agg_step(S0 + U * i + j, 16 * (S0 // U + i + 1), j)

            def ln_b_product(e, a, load):
                pe.wait_ge(staged, 16 * (load + 1))
                pe.wait_ge(w_done, 2 * load + a + 2)
                for hc in range(HC // 2):
                    for kc in range(KC):
                        w = kc * H + (HC // 2 * a + hc) * P
                        m = mm(misc[:, hc:hc + 1], stage[:, w:w + P],
                               biasT[:, bass.ds(80 + KC * e + kc, 1)], start=kc == 0, stop=kc == KC - 1)
                m.then_inc(b1_mm, 1)

            with pe.Fori(0, PREP2) as e:
                for a in range(4):
                    eight(4 * e + a)
                    if a < 2:
                        ln_b_product(e, a, 2 * e)
            with pe.Fori(PREP2, NE) as e:
                for a in range(2):
                    eight(2 * e + 2 * PREP2 + a)
                    ln_b_product(e, a, e + PREP2)
            with pe.Fori(2 * (NE + PREP2), S1 // U) as i:
                eight(i)

            pe.wait_ge(agg_added, 2 + S0 + S1)
            pe.wait_ge(mlp_in, 80)
            for n in range(-2, NT + 2 * G + 3):
                t = n + 2
                if 0 <= t < NT:
                    if t >= 2:
                        pe.wait_ge(t_out, t - 1)
                    for kc in range(KC):
                        m = nc.tensor.transpose(bank[t % 2][:, kc * P:kc * P + P], acc[:, t, kc * P:kc * P + P], ident[:, :])
                    m.then_inc(t_mm, 1)
                t = n - 2 * G - 2
                if 0 <= t < NT:
                    pe.wait_ge(norm_out, t + 1)
                    if t >= 2:
                        pe.wait_ge(r_out, t - 1)
                    for kc in range(KC):
                        m = nc.tensor.transpose(bank[5 + t % 2][:, kc * P:kc * P + P], xn[:, t, kc * P:kc * P + P], ident[:, :])
                    m.then_inc(r_mm, 1)
                t = n + 1
                if 0 <= t < NT:
                    pe.wait_ge(t_out, t + 1)
                    if t >= 2:
                        pe.wait_ge(h1_out, KC * (t - 1))
                    for oc in range(KC):
                        for kc in range(KC):
                            m = mm(bank[2 + t % 2][:, oc * P:oc * P + P], gw1[:, kc, oc * P:oc * P + P],
                                   aggT[t % 2][:, kc * P:kc * P + P], start=kc == 0, stop=kc == KC - 1)
                    m.then_inc(h1_mm, 1)
                t = n
                if 0 <= t < NT:
                    pe.wait_ge(h1_out, KC * (t + 1))
                    if t >= 1:
                        pe.wait_ge(h2_relu, t)
                    mm(bank[4][:, 0:D], one_b[:, :], gb2_rows, start=True, stop=False)
                    for kc in range(KC):
                        m = mm(bank[4][:, 0:D], h1T[t % 2][:, kc * P:kc * P + P], gw2[:, kc, :],
                               start=False, stop=kc == KC - 1)
                    m.then_inc(h2_mm, 1)
                t = n - 2 * G - 3
                if 0 <= t < NT:
                    pe.wait_ge(r_out, t + 1)
                    for kc in range(KC):
                        m = mm(misc[:, t * NE:(t + 1) * NE], xT[t % 2][:, kc * P:kc * P + P], Wr_sb[:, kc, :],
                               start=kc == 0, stop=kc == KC - 1)
                    m.then_inc(lg_mm, 1)
            prefixes(3, NE, FT)
            for c in range(RC):
                if c % 2 == 0:
                    pe.wait_ge(slot_lo_built, c // 2 + 1)
                if c % SCH == 0:
                    pe.wait_ge(slot_hi_built, c // SCH + 1)
                    pe.wait_ge(slot_gate_built, c // SCH + 1)
                m = mm(bank[0][:, 0:2 * FT], slot_lo[:, c, :], slot_hi[:, c, :, :].rearrange("p k n -> p (k n)"),
                       start=c == 0, stop=c == RC - 1)
            m.then_inc(slots_mm, 1)

            def turn(t, q, n):
                pe.wait_ge(xs_in[q], 16 * n)
                pe.wait_ge(fx_split, t + 1)
                for kc in range(KC):
                    m = nc.tensor.transpose(bank[6 + q % 2][:, kc * P:kc * P + P], xs[q][:, kc * P:kc * P + P], ident[:, :])
                m.then_inc(ft_mm, 1)

            def experts(group):
                word = pe.value_load(exp_tab[0:1, bass.ds(group, 1)], min_val=0, max_val=NE ** (XR + 1) - 1)
                return [(word // NE ** k) % NE for k in range(XR + 1)]

            def up(t, q, ex):
                e = pe.snap(ex * WE)
                pe.wait_ge(fx_split, 2 + t + 1)
                for hb in range(2):
                    pe.wait_ge(gelu_done, 2 * t + hb + 1)
                    for hc in range(HC // 2 * hb, HC // 2 * (hb + 1)):
                        o = bank[2 * q + hb][:, (hc % 4) * P:(hc % 4) * P + P]
                        for kc in range(KC):
                            w = [Wall[:, bass.ds(e + (part * KC + kc) * H + hc * P, P)] for part in range(2)]
                            xh, xo = xhi[q][:, kc * P:kc * P + P], xlo[q][:, kc * P:kc * P + P]
                            mm(o, w[0], xh, start=kc == 0, stop=False)
                            mm(o, w[0], xo, start=False, stop=False)
                            m = mm(o, w[1], xh, start=False, stop=kc == KC - 1)
                    m.then_inc(up_mm, 1)

            def down(t, q, ex):
                ew2 = pe.snap(ex * WE + W2BASE)
                eb = pe.snap(ex * D)
                pe.wait_ge(y_out, t + 1)
                mm(bank[4 + q][:, 0:D], one_b[:, :], b2rows[:, bass.ds(eb, D)], start=True, stop=False)
                pe.wait_ge(h_split, 2 + t + 1)
                for hc in range(HC):
                    w = [Wall[:, bass.ds(ew2 + part * HC * D + hc * D, D)] for part in range(2)]
                    hh, hl = hhi[q][:, hc * P:hc * P + P], hlo[q][:, hc * P:hc * P + P]
                    mm(bank[4 + q][:, 0:D], hh, w[0], start=False, stop=False)
                    mm(bank[4 + q][:, 0:D], hh, w[1], start=False, stop=False)
                    m = mm(bank[4 + q][:, 0:D], hl, w[0], start=False, stop=hc == HC - 1)
                m.then_inc(down_mm, 1)

            turn(0, 0, 1)
            turn(1, 1, 1)
            up(0, 0, experts(0)[0])
            pe.wait_ge(w_done, 2 + 4 * NE)
            pe.wait_ge(b2_in, 80)
            with pe.Fori(0, FT // XR - 1) as i:
                ex = experts(i)
                for q in range(XR):
                    turn(XR * i + q + 2, (q + 2) % XR, i + 1 + (q + 2) // XR)
                    up(XR * i + q + 1, (q + 1) % 2, ex[q + 1])
                    down(XR * i + q, q % 2, ex[q])
            ex = experts(FT // XR - 1)
            for q in range(XR):
                t = FT - XR + q
                if t + 2 < FT:
                    turn(t + 2, (t + 2) % XR, (t + 2) // XR + 1)
                if t + 1 < FT:
                    up(t + 1, (t + 1) % 2, ex[q + 1])
                down(t, q % 2, ex[q])

        @block.scalar
        def _(act):
            steps = [0]

            def link(ins):
                steps[0] += 1
                ins.then_inc(act_step, 1)
                act.wait_ge(act_step, steps[0])

            act.nop().then_inc(gelu_done, 4)
            def root(nth, lo, hi):
                act.wait_ge(var_ready, nth)
                act.activation(rstd[:, lo:hi], lnt[:, 2, lo:hi], ACT.Sqrt).then_inc(root_done, 1)

            act.wait_ge(x_loaded, 32)
            for t in range(NT):
                act.activation(xl[:, t, :], x_in[:, t, :], ACT.Copy, accum_out=mean1[:, t:t + 1]).then_inc(sums_done, 1)
            act.wait_ge(sums_done, NT)
            link(act.activation(nmr[:, :], mean1[:, :], ACT.Copy, scale=-1.0 / D))
            for t in range(NT):
                act.activation(xl[:, t, :], x_in[:, t, :], ACT.Square, bias=nmr[:, t:t + 1],
                               accum_out=rstd[:, t:t + 1]).then_inc(sums_done, 1)
            root(1, 0, NT)
            act.wait_ge(xl_scaled, 1)
            act.wait_ge(small_in, 112)
            act.activation(eps1[:, :], eps1[:, :], ACT.Copy, bias=1.0).then_inc(eps_ready, 1)
            with act.Fori(0, NT // G) as g:
                for k in range(G):
                    t = G * g + k
                    act.activation(xl[:, bass.ds(t, 1), :], x_in[:, bass.ds(t, 1), :], ACT.Identity,
                                   bias=nmr[:, bass.ds(t, 1)], scale=rstd[:, bass.ds(t, 1)]).then_inc(xl_done, 1)
            act.wait_ge(bias_mm, 1)
            act.activation(biasT[:, :], bank[7][:, 0:P], ACT.Copy).then_inc(bias_mm, 1)

            def pay(col, h):
                act.activation(pay_slot[:, h, :, :].rearrange("p c k -> p (c k)"),
                               epay.rearrange("p c k -> p (c k)")[:, bass.ds(col * PAY, HALF * PAY)], ACT.Copy).then_inc(pay_ready, 1)

            def idx(c, col, j):
                act.activation(idx_slot[:, j:j + 2], rec_i[c][:, bass.ds(col, 2)], ACT.Copy).then_inc(idx_ready, 1)

            def rec(c, col, h):
                act.activation(rec_slot[:, h, :, :].rearrange("p c k -> p (c k)"),
                               rec_f[c].rearrange("p c k -> p (c k)")[:, bass.ds(col * 2, HALF * 2)], ACT.Copy).then_inc(rec_ready, 1)

            def pay_next(col, h, hi=None):
                act.wait_ge(sort_built, col + HALF)
                act.wait_ge(words_built, col + HALF)
                if hi is not None:
                    act.wait_ge(hi_built, hi)
                pay(col + U, h)

            def idx_next(c, col, gi, j):
                act.wait_ge(gathered[j], gi)
                act.wait_ge(gathered[j + 1], gi)
                idx(c, col + j + U, j)

            def rec_next(c, tile, col, h):
                act.wait_ge(sw_built, tile + HALF)
                rec(c, col + U, h)

            def words(col, s, chunk):
                h, jj = s // HALF, s % HALF
                act.wait_ge(hot_built, col + 1)
                last = act.activation(lo_node[:, s, :], lo_hot[:, s, :], ACT.Copy, scale=pay_slot[:, h, jj, 2:3])
                if chunk:
                    last = act.activation(lo_rest[:, s, :], lo_hot[:, s, :], ACT.Copy, scale=pay_slot[:, h, jj, 4:5])
                if chunk or s not in WT_ON_DVE:
                    last = act.activation(lo_wt[:, s, :], lo_hot[:, s, :], ACT.Copy, scale=pay_slot[:, h, jj, 3:4])
                last.then_inc(words_built, 1)

            act.wait_ge(payload_set, 1)
            pay(0, 0)
            pay(HALF, 1)
            act.wait_ge(pay_ready, 1)
            for j in range(HALF):
                words(j, j, 0)
            with act.Fori(0, C0 // U - 1) as i:
                for h in range(2):
                    act.wait_ge(pay_ready, 2 * i + h + 2)
                    for jj in range(HALF):
                        words(U * i + HALF * (h + 1) + jj, HALF * (1 - h) + jj, 0)
                        if jj == 0:
                            pay_next(U * i + HALF * h, h, HALF * i + 2 * (h + 1))
            act.wait_ge(payload_set, 2)
            act.wait_ge(sort_built, C0 - HALF)
            act.wait_ge(words_built, C0 - HALF)
            act.wait_ge(hi_built, (C0 - HALF) // 2)
            pay(C0, 0)
            for j in range(HALF, U):
                words(C0 - U + j, j, 0)
            act.wait_ge(sort_built, C0)
            act.wait_ge(words_built, C0)
            act.wait_ge(hi_built, C0 // 2)
            pay(C0 + HALF, 1)
            act.wait_ge(recs_taken, 1)
            for j in range(0, U, 2):
                idx(0, j, j)
            rec(0, 0, 0)
            rec(0, HALF, 1)
            with act.Fori(0, C1 // U - 1) as i:
                for h in range(2):
                    act.wait_ge(pay_ready, C0 // HALF + 2 * i + h + 1)
                    for j in range(HALF * h, HALF * (h + 1), 2):
                        words(C0 + U * i + j, j, 1)
                        words(C0 + U * i + j + 1, j + 1, 1)
                        idx_next(0, U * i, 16 * (i + 1), j)
                    rec_next(0, U * i + HALF * h, U * i + HALF * h, h)
                    pay_next(C0 + U * i + HALF * h, h)
            for h in range(2):
                act.wait_ge(pay_ready, EC // HALF - 2 + h + 1)
                for j in range(HALF * h, HALF * (h + 1)):
                    words(EC - U + j, j, 1)
            act.wait_ge(recs_taken, 2)
            for j in range(0, U, 2):
                act.wait_ge(gathered[j], 16 * (S0 // U))
                act.wait_ge(gathered[j + 1], 16 * (S0 // U))
                idx(1, j, j)
            for h in range(2):
                act.wait_ge(sw_built, S0 - U + HALF * (h + 1))
                rec(1, HALF * h, h)

            def w1_high(e, a, load):
                act.wait_ge(staged, 16 * (load + 1))
                act.activation(Wall[:, bass.ds(e * WE + a * H, H)], stage[:, a * H:(a + 1) * H], ACT.Copy,
                               scale=biasT[:, bass.ds(64 + KC * e + a, 1)]).then_inc(w_hi, 1)

            def w2_high(e, a, load):
                act.wait_ge(staged, 16 * (load + 1))
                act.activation(Wall[:, bass.ds(W2BASE + e * WE + a * H, H)], stage[:, a * H:(a + 1) * H],
                               ACT.Copy, scale=WSCALE).then_inc(w_hi, 1)

            def rec_step(i):
                for h in range(2):
                    for j in range(HALF * h, HALF * (h + 1), 2):
                        idx_next(1, U * i, 16 * (S0 // U + i + 1), j)
                    rec_next(1, S0 + U * i + HALF * h, U * i + HALF * h, h)

            act.wait_ge(g_scaled, 1)
            with act.Fori(0, PREP2) as e:
                for a in range(4):
                    rec_step(4 * e + a)
                    if a < 2:
                        w1_high(e, a, 2 * e)
                    else:
                        w2_high(e, a - 2, 2 * e + 1)
            with act.Fori(PREP2, NE) as e:
                for a in range(2):
                    rec_step(2 * e + 2 * PREP2 + a)
                    w1_high(e, a, e + PREP2)
            if S1 // U - 1 > 2 * (NE + PREP2):
                with act.Fori(2 * (NE + PREP2), S1 // U - 1) as i:
                    rec_step(i)

            act.wait_ge(w_done, 2 + 2 * (NE + PREP2))
            for n in range(-2, NT + 2 * G + 3):
                t = n + 2
                if 0 <= t < NT:
                    act.wait_ge(t_mm, t + 1)
                    if t >= 2:
                        act.wait_ge(h1_mm, t - 1)
                    act.activation(aggT[t % 2], bank[t % 2][:, 0:D], ACT.Copy).then_inc(t_out, 1)
                t = n - 2 * G - 3
                if 0 <= t < NT:
                    act.wait_ge(r_mm, t + 1)
                    if t >= 2:
                        act.wait_ge(lg_mm, t - 1)
                    act.activation(xT[t % 2], bank[5 + t % 2][:, 0:D], ACT.Copy).then_inc(r_out, 1)
                t = n + 1
                if 0 <= t < NT:
                    act.wait_ge(h1_mm, t + 1)
                    if t >= 2:
                        act.wait_ge(h2_mm, t - 1)
                    for oc in range(KC):
                        act.activation(h1T[t % 2][:, oc * P:oc * P + P], bank[2 + t % 2][:, oc * P:oc * P + P], ACT.Relu,
                                       bias=biasT[:, 96 + oc:97 + oc]).then_inc(h1_out, 1)
                t = n
                if t > 0 and t % G == 0 and t <= NT + G:
                    g = t // G - 1
                    root(2 + g, G * max(g - 1, 0), min(G * (g + 1), NT))
                if 0 <= t < NT:
                    act.wait_ge(h2_mm, t + 1)
                    act.activation(h2[:, t, :], bank[4][:, 0:D], ACT.Relu).then_inc(h2_relu, 1)
            act.wait_ge(var_ready, 3 + NT // G)
            act.activation(lnt[:, 1, :], lnt[:, 3, :], ACT.Sqrt).then_inc(root_done, 1)
            act.wait_ge(top_ready, 1)
            act.activation(gate[:, 1, :], r_e, ACT.Exp).then_inc(exp_done, 1)
            act.wait_ge(x1_done, NT)
            for e in range(PREP2, NE - 1):
                for a in range(2):
                    w2_high(e, a, NE + e)
            for c in range(RC // SCH):
                act.wait_ge(slot_hi_built, c + 1)
                for col in range(c * SCH, (c + 1) * SCH):
                    k, t = divmod(col, NT)
                    m = act.activation(slot_hi[:, col, 1, :], slot_hi[:, col, 1, :], ACT.Copy, scale=gate[:, k, t:t + 1])
                m.then_inc(slot_gate_built, 1)
            for a in range(2):
                w2_high(NE - 1, a, 2 * NE - 1)
            act.activation(warm[:, :], eps1[:, :], ACT.Gelu)

            def x_high(t, q):
                act.wait_ge(ft_mm, 2 + t + 1)
                act.wait_ge(up_mm, 2 * t + 2)
                act.activation(xhi[q], bank[6 + q][:, 0:D], ACT.Copy).then_inc(fx_hi, 1)

            def expert_word(group):
                return act.value_load(exp_tab[0:1, bass.ds(group, 1)], min_val=0, max_val=NE ** (XR + 1) - 1)

            def gelu(t, q, word, k):
                e = act.snap((word // NE ** k) % NE * HC)
                act.wait_ge(h_split, t + 1)
                for hb in range(2):
                    act.wait_ge(up_mm, 4 + 2 * t + hb + 1)
                    for hc in range(HC // 2 * hb, HC // 2 * (hb + 1)):
                        m = act.activation(h32[q][:, hc * P:hc * P + P], bank[2 * q + hb][:, (hc % 4) * P:(hc % 4) * P + P],
                                           ACT.Gelu, bias=b1T[:, bass.ds(e + hc, 1)], scale=1.0 / WSCALE)
                    m.then_inc(gelu_done, 1)

            x_high(0, 0)
            x_high(1, 1)
            gelu(0, 0, expert_word(0), 0)
            with act.Fori(0, FT // XR - 1) as i:
                word = expert_word(i)
                for q in range(XR):
                    x_high(XR * i + q + 2, q % 2)
                    gelu(XR * i + q + 1, (q + 1) % 2, word, q + 1)
            word = expert_word(FT // XR - 1)
            for q in range(1, XR):
                if q + 1 < XR:
                    x_high(FT - XR + q + 1, (q + 1) % 2)
                gelu(FT - XR + q, q % 2, word, q)

        @block.vector
        def _(dve):
            steps = [0]

            def link(ins):
                steps[0] += 1
                ins.then_inc(dve_step, 1)
                dve.wait_ge(dve_step, steps[0])

            dve.nop().then_inc(agg_added, 2)
            dve.nop().then_inc(fx_split, 2)
            dve.nop().then_inc(h_split, 2)
            dve.nop().then_inc(y_out, 2)
            dve.nop().then_inc(y_free, 2)
            dve.nop().then_inc(w_done, 2)
            dve.wait_ge(const_done, 3)

            dve.wait_ge(edges_in, 96)

            link(dve.tensor_scalar(e_tmp, e_src, 7, None, ALU.arith_shift_right))
            link(dve.tensor_copy(blk_h, e_tmp))
            dve.nop().then_inc(blocks_ready, 1)
            link(dve.tensor_scalar(e_src, e_src, P - 1, None, ALU.bitwise_and))
            link(dve.tensor_scalar(e_tmp, e_dst, 1, None, ALU.arith_shift_right))
            link(dve.tensor_scalar(nwords[:, :, 1], e_tmp, 1.0, None, ALU.add))
            link(dve.tensor_scalar(e_dst, e_dst, 1, 7, ALU.bitwise_and, ALU.arith_shift_left))
            link(dve.tensor_tensor(e_dst, e_dst, e_src, ALU.bitwise_or))
            link(dve.tensor_copy(nwords[:, :, 0], e_dst))
            link(dve.tensor_copy(wwords[:, :, 1], ew))
            link(dve.tensor_tensor(ew, ew, wwords[:, :, 1], ALU.subtract))
            link(dve.tensor_copy(wwords[:, :, 0], ew))
            link(dve.tensor_tensor(epay[:, :, 4], ew, wwords[:, :, 0], ALU.subtract))

            def place(nth, B, T, oh, cum, work, S, pos, table, misc=bank[7]):
                flat = oh.rearrange("p b t -> p (b t)")
                cflat = cum.rearrange("p b t -> p (b t)")
                link(dve.tensor_tensor_scan(cflat, one_h[:, 0:1].to_broadcast([P, B * T]), flat, 0.0, ALU.mult, ALU.add))
                link(dve.tensor_copy(cprev[:, 1:B], cum[:, 0:B - 1, T - 1]))
                link(dve.memset(cprev[:, 0:1], 0.0))
                link(dve.tensor_tensor(cnt[:, 0:B], cum[:, :, T - 1], cprev[:, 0:B], ALU.subtract))
                dve.nop().then_inc(counts_ready, 1)
                dve.wait_ge(counts_mm, nth)
                link(dve.tensor_scalar(room_i[:, 0:B], misc[:, 32:32 + B], float(P - 1), None, ALU.add))
                link(dve.tensor_scalar(room_i[0:B, 32:33], misc[0:B, 64:65], float(P - 1), None, ALU.add))
                link(dve.tensor_scalar(room_i[:, 0:B], room_i[:, 0:B], -P, None, ALU.bitwise_and))
                link(dve.tensor_scalar(room_i[0:B, 32:33], room_i[0:B, 32:33], -P, None, ALU.bitwise_and))
                link(dve.tensor_copy(room_f[:, 0:B], room_i[:, 0:B]))
                link(dve.tensor_copy(room_f[0:B, 32:33], room_i[0:B, 32:33]))
                link(dve.tensor_tensor_scan(first[:, 0:B], ones[:, 0:B], room_f[:, 0:B], 0.0, ALU.mult, ALU.add))
                link(dve.tensor_tensor(first[:, 0:B], first[:, 0:B], room_f[:, 0:B], ALU.subtract))
                link(dve.tensor_tensor(first[:, 0:B], first[:, 0:B], misc[:, 0:B], ALU.add))
                dve.nop().then_inc(room_ready, 1)
                link(dve.scalar_tensor_tensor(out=first[:, 0:B], in0=first[:, 0:B], scalar=-1.0, in1=cprev[:, 0:B],
                                              op0=ALU.add, op1=ALU.subtract))
                for b in range(B):
                    m = dve.scalar_tensor_tensor(out=work[:, b, :], in0=cum[:, b, :], scalar=first[:, b:b + 1], in1=oh[:, b, :],
                                                 op0=ALU.add, op1=ALU.mult)
                link(m)
                link(dve.tensor_reduce(pos, work.rearrange("p b t -> p t b"), AX_X, ALU.add))
                dve.wait_ge(ends_mm, nth)
                link(dve.tensor_scalar(ends[0:B, :], misc[0:B, 96:97], 1.0 / P, None, ALU.mult))
                link(dve.tensor_scalar(past[0:B, 0:S], iota_h[0:B, 0:S], ends[0:B, 0:1], None, ALU.is_ge))
                dve.nop().then_inc(past_ready, 1)
                dve.wait_ge(table_mm, nth)
                link(dve.tensor_scalar(table, misc[0:1, 128:128 + S], float(B - 1), None, ALU.min))
                return table

            def edge_places(c):
                T, c0 = COLS[c], CSTART[c]
                oh = (e_oh, e_oh1)[c][:, 0:NB * T].rearrange("p (b t) -> p b t", b=NB)
                cum = e_cum[:, 0:NB * T].rearrange("p (b t) -> p b t", b=NB)
                work = e_pos[:, 0:NB * T].rearrange("p (b t) -> p b t", b=NB)
                if c:
                    dve.wait_ge(blocks_hot, 1)
                else:
                    link(dve.tensor_tensor(oh, blk_h[:, c0:c0 + T].rearrange("p (a t) -> p a t", a=1).to_broadcast([P, NB, T]),
                                           iota_h[:, 0:NB].rearrange("p (b a) -> p b a", a=1).to_broadcast([P, NB, T]), ALU.is_equal))
                place(c + 1, NB, T, oh, cum, work, SLOTS[c], pos_j[:, 0:T].bitcast(F32), blk_row[:, 0:SLOTS[c]])
                four = blk_row[:, 0:SLOTS[c]].rearrange("p (g k) -> p g k", k=HALF)
                for k in range(HALF - 2, 0, -1):
                    link(dve.scalar_tensor_tensor(out=four[:, :, k], in0=four[:, :, k + 1], scalar=float(NB),
                                                  in1=four[:, :, k], op0=ALU.mult, op1=ALU.add))
                link(dve.scalar_tensor_tensor(out=blk_tab[c][:, :], in0=four[:, :, 1], scalar=float(NB),
                                              in1=four[:, :, 0], op0=ALU.mult, op1=ALU.add))
                link(dve.tensor_copy(pos_i[:, 0:T], pos_j[:, 0:T].bitcast(F32)))
                link(dve.tensor_scalar(pos_j[:, 0:T], pos_i[:, 0:T], P - 1, None, ALU.bitwise_and))
                link(dve.tensor_copy(epay[:, c0:c0 + T, 0], pos_j[:, 0:T]))
                link(dve.tensor_scalar(pos_j[:, 0:T], pos_i[:, 0:T], 7, None, ALU.arith_shift_right))
                link(dve.tensor_copy(epay[:, c0:c0 + T, 1], pos_j[:, 0:T]))
                dve.nop().then_inc(payload_set, 1)

            def moments(lo, hi):
                m0, v0, m1, v1 = (stats[:, lo:hi, k] for k in (1, 2, 4, 5))
                mean, dev, var = (lnt[:, k, lo:hi] for k in range(3))
                link(dve.tensor_tensor(mean, m0, m1, ALU.add))
                link(dve.tensor_tensor(dev, m0, m1, ALU.subtract))
                link(dve.tensor_tensor(var, v0, v1, ALU.add))
                link(dve.scalar_tensor_tensor(out=dev, in0=dev, scalar=0.25, in1=dev, op0=ALU.mult, op1=ALU.mult))
                link(dve.scalar_tensor_tensor(out=var, in0=var, scalar=1.0 / D, in1=dev, op0=ALU.mult, op1=ALU.add))

            def refine(r_, v_, tmp):
                link(dve.reciprocal(r_, r_))
                link(dve.tensor_tensor(tmp, r_, r_, ALU.mult))
                link(dve.scalar_tensor_tensor(out=tmp, in0=tmp, scalar=-0.5, in1=v_, op0=ALU.mult, op1=ALU.mult))
                link(dve.scalar_tensor_tensor(out=r_, in0=tmp, scalar=1.5, in1=r_, op0=ALU.add, op1=ALU.mult))

            def coefficients(nth, lo, hi):
                dve.wait_ge(root_done, nth)
                refine(rstd[:, lo:hi], lnt[:, 2, lo:hi], lnt[:, 1, lo:hi])
                link(dve.scalar_tensor_tensor(out=nmr[:, lo:hi], in0=lnt[:, 0, lo:hi], scalar=-0.5, in1=rstd[:, lo:hi],
                                              op0=ALU.mult, op1=ALU.mult))

            edge_places(0)
            dve.wait_ge(sums_done, 2 * NT)
            link(dve.tensor_scalar(lnt[:, 0, :], nmr[:, :], -2.0, None, ALU.mult))
            link(dve.tensor_scalar(lnt[:, 2, :], rstd[:, :], 1.0 / D, LN_EPS, ALU.mult, ALU.add))
            dve.nop().then_inc(var_ready, 1)
            coefficients(1, 0, NT)
            dve.nop().then_inc(xl_scaled, 1)
            edge_places(1)
            dve.wait_ge(b2_in, 32)
            link(dve.tensor_scalar(b2raw[:, 0:BC - KC], b2raw[:, 0:BC - KC], WSCALE, None, ALU.mult))
            for k in range(3):
                link(dve.tensor_copy(b2parts[:, k, :], b2raw[:, :]))
                if k < 2:
                    link(dve.tensor_tensor(b2raw[:, :], b2raw[:, :], b2parts[:, k, :], ALU.subtract))
            dve.nop().then_inc(b2_ready, 1)

            def sort_build(c, h, jj, s, chunk):
                dve.wait_ge(sort_mm, c + 1)
                p_ = [pay_slot[:, h, jj, k:k + 1] for k in range(PAY)]
                S = SLOTS[chunk]
                last = dve.tensor_scalar(lo_hot[:, s, :], iota_h[:, 0:P], p_[0], None, ALU.is_equal)
                last.then_inc(hot_built, 1)
                if chunk == 0:
                    last = dve.tensor_scalar(lo_rest[:, s, :], iota_h[:, 0:P], p_[0], p_[4], ALU.is_equal, ALU.mult)
                    if s in WT_ON_DVE:
                        last = dve.tensor_scalar(lo_wt[:, s, :], iota_h[:, 0:P], p_[0], p_[3], ALU.is_equal, ALU.mult)
                if chunk or s not in HI_ON_POOL:
                    last = dve.tensor_scalar(hi16[:, s, 0:S], iota_h[:, 0:S], p_[1], None, ALU.is_equal)
                last.then_inc(sort_built, 1)

            def records(c):
                S = SLOTS[c]
                dve.wait_ge(sort_mm, SR + sum(COLS[:c + 1]))
                odd = e_pos[:, 0:S]
                twice = e_pos[:, 256:256 + S]
                link(dve.tensor_scalar(odd, bank[1][:, 0:S], float(P), None, ALU.is_ge))
                link(dve.scalar_tensor_tensor(out=twice, in0=bank[0][:, 0:S], scalar=2.0, in1=odd, op0=ALU.mult, op1=ALU.add))
                link(dve.tensor_scalar(rec_i[c], twice, -2.0, 0.0, ALU.add, ALU.max))
                link(dve.scalar_tensor_tensor(out=rec_f[c][:, :, 0], in0=odd, scalar=-float(P), in1=bank[1][:, 0:S],
                                              op0=ALU.mult, op1=ALU.add))
                link(dve.tensor_copy(odd, bank[4][:, 0:S]))
                link(dve.tensor_tensor(odd, odd, bank[3][:, 0:S], ALU.add))
                link(dve.tensor_tensor(rec_f[c][:, :, 1], odd, bank[2][:, 0:S], ALU.add))
                if c:
                    link(dve.memset(x1[:, NT - 1, :], 0.0))
                dve.nop().then_inc(recs_taken, 1)

            with dve.Fori(0, C0 // U) as i:
                for j in range(U):
                    if j % HALF == 0:
                        dve.wait_ge(pay_ready, 2 * i + j // HALF + 1)
                    sort_build(U * i + j, j // HALF, j % HALF, j % SR, 0)
            dve.wait_ge(pay_ready, C0 // HALF + 1)
            for j in range(HALF):
                sort_build(C0 + j, 0, j, j, 1)
            records(0)
            dve.wait_ge(acc_set, NT // G)

            def sw_build(g, j):
                dve.wait_ge(agg_mm, g + 5)
                r = rec_slot[:, j // HALF, j % HALF, :]
                dve.tensor_scalar(Sw[:, j % 4, :], iota_f[:, 0:P], r[:, 0:1], r[:, 1:2], ALU.is_equal, ALU.mult).then_inc(sw_built, 1)

            def blocks_of(c, group):
                word = dve.value_load(blk_tab[c][0:1, bass.ds(group, 1)], min_val=0, max_val=NB ** HALF - 1)
                return [(word // NB ** k) % NB for k in range(HALF)]

            def agg_add(g, b, j):
                dve.wait_ge(agg_mm, U + g + 1)
                dve.wait_ge(agg_added, 2 + g)
                a = RA[:, bass.ds(b * D, D)]
                dve.tensor_tensor(a, a, bank[5 + j % 2][:, 0:D], ALU.add).then_inc(agg_added, 1)

            def agg_steps(i, before, c, sorting, last):
                for j in range(U):
                    if j % HALF == 0:
                        blk = blocks_of(c, 2 * i + j // HALF)
                        if sorting and not (last and j):
                            dve.wait_ge(pay_ready, C0 // HALF + 2 * i + j // HALF + 2)
                        if not (last and j):
                            dve.wait_ge(rec_ready, before // HALF + 2 * i + j // HALF + 2)
                    if sorting and not (last and j >= HALF):
                        ahead = (j + HALF) % U
                        sort_build(C0 + U * i + j + HALF, ahead // HALF, ahead % HALF, ahead, 1)
                    agg_add(before + U * i + j, blk[j % HALF], j)
                    if not (last and j >= HALF):
                        sw_build(before + U * i + j + HALF, (j + HALF) % U)

            def first_built(before):
                dve.wait_ge(rec_ready, before // HALF + 1)
                for j in range(HALF):
                    sw_build(before + j, j)

            first_built(0)
            with dve.Fori(0, C1 // U - 1) as i:
                agg_steps(i, 0, 0, True, False)
            agg_steps(C1 // U - 1, 0, 0, True, True)
            records(1)

            def w1_low(e, a, n):
                dve.wait_ge(w_hi, n + 1)
                dve.scalar_tensor_tensor(out=Wall[:, bass.ds(e * WE + (KC + a) * H, H)],
                                         in0=stage[:, a * H:(a + 1) * H], scalar=biasT[:, bass.ds(64 + KC * e + a, 1)],
                                         in1=Wall[:, bass.ds(e * WE + a * H, H)],
                                         op0=ALU.mult, op1=ALU.subtract)
                dve.wait_ge(b1_mm, 2 * e + a + 1)
                at = e * HC + a * (HC // 2)
                dve.tensor_tensor(b1T[:, bass.ds(at, HC // 2)], biasT[:, bass.ds(at, HC // 2)],
                                  bank[7][:, 0:HC // 2], ALU.add).then_inc(w_done, 1)

            def w2_low(e, a, n):
                dve.wait_ge(w_hi, n + 1)
                dve.scalar_tensor_tensor(out=Wall[:, bass.ds(W2BASE + e * WE + (2 + a) * H, H)],
                                         in0=stage[:, a * H:(a + 1) * H], scalar=WSCALE,
                                         in1=Wall[:, bass.ds(W2BASE + e * WE + a * H, H)],
                                         op0=ALU.mult, op1=ALU.subtract).then_inc(w_done, 1)

            dve.wait_ge(bias_mm, 2)
            link(dve.tensor_scalar(biasT[:, 64:80], biasT[:, 64:80], WSCALE, None, ALU.mult))
            dve.nop().then_inc(g_scaled, 1)

            first_built(S0)
            with dve.Fori(0, PREP2) as e:
                for a in range(4):
                    agg_steps(4 * e + a, S0, 1, False, False)
                    if a < 2:
                        w1_low(e, a, 4 * e + a)
                    else:
                        w2_low(e, a - 2, 4 * e + a)
            with dve.Fori(PREP2, NE) as e:
                for a in range(2):
                    agg_steps(2 * e + 2 * PREP2 + a, S0, 1, False, False)
                    w1_low(e, a, 2 * e + 2 * PREP2 + a)
            if S1 // U - 1 > 2 * (NE + PREP2):
                with dve.Fori(2 * (NE + PREP2), S1 // U - 1) as i:
                    agg_steps(i, S0, 1, False, False)
            agg_steps(S1 // U - 1, S0, 1, False, True)

            dve.wait_ge(mlp_in, 80)
            nstat = 0

            def row_stats(rows, t):
                dve.bn_stats(stats[:, t, :], rows[:, t, :]).then_inc(stats_done, 1)

            for n in range(NT + G + 1):
                u = n - G
                if n > 0 and n % G == 0:
                    g = n // G - 1
                    coefficients(2 + g, G * max(g - 1, 0), min(G * (g + 1), NT))
                    if g:
                        dve.nop().then_inc(xn_coef, 1)
                if 0 <= u < NT:
                    dve.scalar_tensor_tensor(out=h2[:, u, :], in0=h2[:, u, :], scalar=mean1[:, u:u + 1], in1=gsc_bc,
                                             op0=ALU.subtract, op1=ALU.mult).then_inc(centred, 1)
                if 0 <= u < NT:
                    dve.wait_ge(centred, u + 1)
                    dve.wait_ge(x_shift, u // G + 1)
                    dve.scalar_tensor_tensor(out=x1[:, u, :], in0=h2[:, u, :], scalar=rstd[:, u:u + 1], in1=x1[:, u, :],
                                             op0=ALU.mult, op1=ALU.add).then_inc(x1_done, 1)
                    dve.wait_ge(x1_done, u + 1)
                    row_stats(x1, u)
                    nstat += 1
                if n < NT:
                    dve.wait_ge(h2_relu, n + 1)
                    row_stats(h2, n)
                    nstat += 1
                if n % G == G - 1:
                    g = n // G
                    dve.wait_ge(stats_done, nstat)
                    moments(G * max(g - 1, 0), min(G * (g + 1), NT))
                    if g < NT // G:
                        w = slice(G * g, G * (g + 1))
                        link(dve.tensor_scalar(mean1[:, w], lnt[:, 0, w], 0.5, None, ALU.mult))
                        link(dve.tensor_scalar(lnt[:, 2, w], lnt[:, 2, w], GNN_EPS, None, ALU.add))
                    if g:
                        w = slice(G * (g - 1), G * g)
                        v_, u_ = lnt[:, 2, w], lnt[:, 3, w]
                        link(dve.tensor_scalar(u_, v_, LN_EPS, None, ALU.add))
                        link(dve.scalar_tensor_tensor(out=v_, in0=u_, scalar=LN_EPS, in1=v_, op0=ALU.mult, op1=ALU.add))
                        link(dve.reciprocal(u_, u_))
                        link(dve.tensor_tensor(u_, u_, v_, ALU.mult))
                    dve.nop().then_inc(var_ready, 1)
            dve.nop().then_inc(var_ready, 1)
            dve.wait_ge(root_done, 3 + NT // G)
            refine(lnt[:, 1, :], lnt[:, 3, :], lnt[:, 2, :])
            link(dve.tensor_tensor(lnt[:, 1, :], lnt[:, 1, :], lnt[:, 3, :], ALU.mult))

            dve.wait_ge(lg_mm, NT)
            bc_e = lambda a: a.rearrange("p (t a) -> p t a", a=1).to_broadcast([P, NT, NE])
            e_row = iota_f[:, 0:NE].rearrange("p (a e) -> p a e", a=1).to_broadcast([P, NT, NE])
            oh = r_oh.rearrange("p (b t) -> p b t", b=NE)
            link(dve.tensor_tensor(lg, bank[7][:, 0:NT * NE].rearrange("p (t e) -> p t e", e=NE), bc_e(lnt[:, 1, :]), ALU.mult))
            link(dve.tensor_tensor(lg, lg, br_bc[:, :].rearrange("p (a e) -> p a e", a=1).to_broadcast([P, NT, NE]), ALU.add))
            link(dve.tensor_scalar(r_ok, tile_at[:, 0:NT], part_i[:, 0:1], float(N), ALU.add, ALU.is_lt))
            for k in range(KTOP):
                link(dve.tensor_reduce(topv[:, k, :], lg, AX_X, ALU.max))
                link(dve.tensor_tensor(eq, lg, bc_e(topv[:, k, :]), ALU.is_lt))
                link(dve.scalar_tensor_tensor(out=cand, in0=eq, scalar=float(NE), in1=e_row, op0=ALU.mult, op1=ALU.add))
                link(dve.tensor_reduce(topi[:, k, :], cand, AX_X, ALU.min))
                link(dve.tensor_tensor(eq, e_row, bc_e(topi[:, k, :]), ALU.is_equal))
                if k == 0:
                    link(dve.scalar_tensor_tensor(out=lg, in0=eq, scalar=-3.0e38, in1=lg, op0=ALU.mult, op1=ALU.add))
                link(dve.tensor_tensor(oh[:, :, k * NT:(k + 1) * NT].rearrange("p b t -> p t b"), eq, bc_e(r_ok), ALU.mult))
            link(dve.tensor_tensor(r_e, topv[:, 1, :], topv[:, 0, :], ALU.subtract))
            dve.nop().then_inc(top_ready, 1)
            place(3, NE, RC, oh, r_cum.rearrange("p (b t) -> p b t", b=NE), r_pos.rearrange("p (b t) -> p b t", b=NE),
                  FT, pos_f, exp_row[:, 0:FT])
            link(dve.tensor_copy(pos_n, pos_f))
            link(dve.tensor_scalar(pos_n, pos_n, P - 1, None, ALU.bitwise_and))
            link(dve.tensor_copy(pos_lo, pos_n))
            dve.nop().then_inc(pos_ready, 1)
            link(dve.tensor_tensor(pos_hi, pos_f, pos_lo, ALU.subtract))
            link(dve.tensor_scalar(pos_hi, pos_hi, 1.0 / P, None, ALU.mult))
            dve.wait_ge(exp_done, 1)
            link(dve.tensor_scalar(gate[:, 0, :], gate[:, 1, :], 1.0, None, ALU.add))
            link(dve.reciprocal(gate[:, 0, :], gate[:, 0, :]))
            link(dve.tensor_tensor(gate[:, 1, :], gate[:, 1, :], gate[:, 0, :], ALU.mult))
            link(dve.memset(exp_row[:, FT:FT + XR], 0.0))
            digit = [exp_row[:, k:k + FT].rearrange("p (g k) -> p g k", k=XR)[:, :, 0] for k in range(XR + 1)]
            words = exp_row[:, FT + XR:]
            for k in range(XR, 0, -1):
                link(dve.scalar_tensor_tensor(out=exp_tab[:, :] if k == 1 else words, in0=digit[XR] if k == XR else words,
                                              scalar=float(NE), in1=digit[k - 1], op0=ALU.mult, op1=ALU.add))
            link(dve.tensor_scalar(r_e, tile_at[:, 0:NT], part_i[:, 0:1], 1.0, ALU.add, ALU.add))
            for k in range(KTOP):
                link(dve.tensor_tensor(node_no[:, k * NT:(k + 1) * NT], r_e, r_ok, ALU.mult))
                link(dve.tensor_tensor(gate[:, k, :], gate[:, k, :], r_ok, ALU.mult))
            dve.wait_ge(rows_stored, STORES)
            for c in range(RC // SCH):
                col = slice(c * SCH, (c + 1) * SCH)
                per = lambda a: a[:, col].rearrange("p (c a) -> p c a", a=1).to_broadcast([P, SCH, FT])
                link(dve.tensor_tensor(slot_hi[:, col, 1, :],
                                       iota_f[:, 0:FT].rearrange("p (a n) -> p a n", a=1).to_broadcast([P, SCH, FT]),
                                       per(pos_hi), ALU.is_equal))
                link(dve.tensor_tensor(slot_hi[:, col, 0, :], slot_hi[:, col, 1, :], per(node_no), ALU.mult))
                for odd in range(c * SCH + 1, (c + 1) * SCH, 2):
                    m = dve.tensor_scalar(slot_lo[:, odd, :], iota_f[:, :], pos_lo[:, odd:odd + 1], None, ALU.is_equal)
                m.then_inc(slot_hi_built, 1)
                if c == 2:
                    for e in range(PREP2, NE - 1):
                        for a in range(2):
                            w2_low(e, a, 2 * (NE + e) + a)
            dve.wait_ge(slots_mm, 1)
            link(dve.tensor_scalar(slot_gate[:, :], bank[0][:, 0:FT], 0.5, spare[:, 0:1], ALU.is_lt, ALU.mult))
            link(dve.scalar_tensor_tensor(out=slot_tok[:, :], in0=bank[0][:, 0:FT], scalar=-1.0, in1=slot_gate[:, :],
                                          op0=ALU.add, op1=ALU.add))
            link(dve.tensor_scalar(slot_gate[:, :], bank[0][:, FT:2 * FT], 1.0 / WSCALE, None, ALU.mult))
            dve.nop().then_inc(slots_ready, 1)
            for a in range(2):
                w2_low(NE - 1, a, 2 * (2 * NE - 1) + a)

            def x_low(t, q):
                dve.wait_ge(fx_hi, t + 1)
                dve.wait_ge(up_mm, 2 * t + 2)
                dve.tensor_tensor(xlo[q], bank[6 + q][:, 0:D], xhi[q], ALU.subtract).then_inc(fx_split, 1)

            def h_parts(t, q):
                dve.wait_ge(gelu_done, 4 + 2 * t + 2)
                dve.wait_ge(down_mm, t + 1)
                dve.tensor_copy(hhi[q], h32[q]).then_inc(hhi_done, 1)
                dve.wait_ge(hhi_done, t + 1)
                dve.tensor_tensor(hlo[q], h32[q], hhi[q], ALU.subtract).then_inc(h_split, 1)

            def y_rows(t, q):
                dve.wait_ge(down_mm, 2 + t + 1)
                dve.wait_ge(y_free, t + 1)
                dve.tensor_scalar(ysb[q], bank[4 + q][:, 0:D], slot_gate[:, bass.ds(t, 1)], None, ALU.mult).then_inc(y_out, 1)

            x_low(0, 0)
            x_low(1, 1)
            h_parts(0, 0)
            with dve.Fori(0, FT // 2 - 1) as i:
                for q in range(2):
                    x_low(2 * i + q + 2, q)
                    h_parts(2 * i + q + 1, 1 - q)
                    y_rows(2 * i + q, q)
            h_parts(FT - 1, 1)
            y_rows(FT - 2, 0)
            y_rows(FT - 1, 1)


_OUT = ((3125, 256), "float32")


def kernel(**inputs):
    import concourse.bacc as _bacc
    from concourse.bass_utils import run_bass_kernel_spmd as _run

    nc = _bacc.Bacc("TRN2", target_bir_lowering=False, num_devices=1,
                    dynamic_dma_scratch_size=20480)
    arrays, args = {}, []
    for name, a in inputs.items():
        a = np.ascontiguousarray(a)
        arrays[f"in_{name}"] = a
        args.append(nc.dram_tensor(f"in_{name}", a.shape, mybir.dt.from_np(a.dtype), kind="ExternalInput").ap())
    out = nc.dram_tensor("out_dram", _OUT[0], F32, kind="ExternalOutput").ap()
    moe_gnn_program(nc, *args, out)
    r = _run(nc, [arrays], core_ids=[0])
    return r.results[0]["out_dram"]
```
